# Optimizing a Trainium2 kernel written in Bass

```python
import numpy as np
import jax
import jax.numpy as jnp

def _softmax(x, axis=-1):
    return jax.nn.softmax(x, axis=axis)

def _gelu(x):
    return jax.nn.gelu(x, approximate=True)

def _silu(x):
    return jax.nn.silu(x)

def _sigmoid(x):
    return jax.nn.sigmoid(x)

def _layernorm(x, axis=-1, eps=1e-05):
    m = jnp.mean(x, axis=axis, keepdims=True)
    v = jnp.var(x, axis=axis, keepdims=True)
    return (x - m) / jnp.sqrt(v + eps)

def _scatter_add(tgt, idx, src, axis=0):
    return tgt.at[idx].add(src)

def _segment_sum(src, seg, n):
    return jax.ops.segment_sum(src, seg, n)
kernel_name = 'mk_recurrent_d2_jaxref_r8_5d3515'

def setup_inputs(seed: int=0):
    np.random.seed(seed)
    _w = jnp.asarray

    def _L0_attn_setup():
        import jax, jax.numpy as jnp
        import numpy as np
        D_MODEL = 128
        H = 4
        DK = 128
        DV = 32
        EPS = 1e-05
        SCALE = DK ** (-0.5)

        def _delta_rule(q, k, v, beta):
            b = q.shape[0]
            qt = jnp.moveaxis(q, 1, 0)
            kt = jnp.moveaxis(k, 1, 0)
            vt = jnp.moveaxis(v, 1, 0)
            bt = jnp.moveaxis(beta, 1, 0)
            S0 = jnp.zeros((b, H, DK, DV), q.dtype)

            def step(S, inp):
                q_t, k_t, v_t, b_t = inp
                pred = jnp.einsum('bhk,bhkv->bhv', k_t, S)
                delta = (v_t - pred) * b_t[..., None]
                S = S + k_t[..., :, None] * delta[..., None, :]
                o_t = jnp.einsum('bhk,bhkv->bhv', q_t, S)
                return (S, o_t)
            _, o = jax.lax.scan(step, S0, (qt, kt, vt, bt))
            return jnp.moveaxis(o, 0, 1)
        key = jax.random.key(seed)
        ks = jax.random.split(key, 8)
        w = lambda k, i, o: jax.random.normal(k, (i, o), jnp.float32) * 2.0 ** (-2.5) * (6.0 / (i + o)) ** 0.5 * 2
        return {'x': jax.random.normal(ks[0], (2, 512, D_MODEL), jnp.float32), 'Wq': w(ks[1], D_MODEL, H * DK), 'Wk': w(ks[2], D_MODEL, H * DK), 'Wv': w(ks[3], D_MODEL, H * DV), 'Wb': w(ks[4], D_MODEL, H), 'Wg': w(ks[5], D_MODEL, H * DV), 'Wo': w(ks[6], H * DV, D_MODEL), 'norm_w': jnp.ones((DV,), jnp.float32)}
    _L0_attn_in = _L0_attn_setup()

    def _L0_ffn_setup():
        import jax, jax.numpy as jnp
        import numpy as np
        B, S, D = (2, 128, 128)
        H, HD = (16, 64)
        E_R = 31
        K_ACT = 3
        INTER = 128
        EPS = 1e-05
        BASE = 10000.0

        def _rmsnorm(x, gamma):
            rms = jnp.sqrt(jnp.mean(x * x, axis=-1, keepdims=True) + EPS)
            return x / rms * gamma

        def _rope(x, theta):
            seq = x.shape[2]
            angles = jnp.arange(seq, dtype=theta.dtype)[:, None] * theta
            cos = jnp.cos(angles)[None, None]
            sin = jnp.sin(angles)[None, None]
            x1, x2 = (x[..., 0::2], x[..., 1::2])
            return jnp.concatenate([x1 * cos - x2 * sin, x1 * sin + x2 * cos], axis=-1)

        def _forward(x, theta, gamma1, gamma2, q_w, q_b, k_w, k_b, v_w, v_b, o_w, o_b, router_w, router_b, sh_w1, sh_b1, sh_w2, sh_b2, re_w1, re_b1, re_w2, re_b2):
            b, s, d = x.shape
            xn = _rmsnorm(x, gamma1)
            q = (xn @ q_w + q_b).reshape(b, s, H, HD).transpose(0, 2, 1, 3)
            k = (xn @ k_w + k_b).reshape(b, s, H, HD).transpose(0, 2, 1, 3)
            v = (xn @ v_w + v_b).reshape(b, s, H, HD).transpose(0, 2, 1, 3)
            q = _rope(q, theta)
            k = _rope(k, theta)
            scale = 1.0 / np.sqrt(HD)
            scores = jnp.einsum('bhqd,bhkd->bhqk', q, k) * scale
            causal = jnp.tril(jnp.ones((s, s), dtype=bool))
            scores = jnp.where(causal, scores, -jnp.inf)
            attn = jax.nn.softmax(scores, axis=-1)
            ctx = jnp.einsum('bhqk,bhkd->bhqd', attn, v)
            ctx = ctx.transpose(0, 2, 1, 3).reshape(b, s, H * HD)
            attn_out = ctx @ o_w + o_b + xn
            an = _rmsnorm(attn_out, gamma2)
            shared = jax.nn.gelu(an @ sh_w1 + sh_b1, approximate=False) @ sh_w2 + sh_b2
            logits = an @ router_w + router_b
            aff = jax.nn.softmax(logits, axis=-1)
            topv, topi = jax.lax.top_k(aff, K_ACT)
            gates = jnp.sum(jax.nn.one_hot(topi, E_R, dtype=aff.dtype) * topv[..., None], axis=-2)
            h = jax.nn.gelu(jnp.einsum('bsd,edh->besh', an, re_w1) + re_b1[None, :, None, :], approximate=False)
            routed = jnp.einsum('bse,besh,ehd->bsd', gates, h, re_w2) + jnp.einsum('bse,ed->bsd', gates, re_b2)
            return shared + routed + an + attn_out
        key = jax.random.key(seed)
        ks = jax.random.split(key, 24)
        s = 0.02
        theta = BASE ** (-jnp.arange(HD // 2, dtype=jnp.float32) * 2.0 / HD)
        inp = {'x': jax.random.normal(ks[0], (B, S, D), jnp.float32), 'positions': jnp.arange(S, dtype=jnp.int32), 'theta': theta, 'gamma1': jnp.ones((D,), jnp.float32), 'gamma2': jnp.ones((D,), jnp.float32), 'q_w': jax.random.normal(ks[1], (D, H * HD), jnp.float32) * s, 'q_b': jnp.zeros((H * HD,), jnp.float32), 'k_w': jax.random.normal(ks[2], (D, H * HD), jnp.float32) * s, 'k_b': jnp.zeros((H * HD,), jnp.float32), 'v_w': jax.random.normal(ks[3], (D, H * HD), jnp.float32) * s, 'v_b': jnp.zeros((H * HD,), jnp.float32), 'o_w': jax.random.normal(ks[4], (H * HD, D), jnp.float32) * s, 'o_b': jnp.zeros((D,), jnp.float32), 'router_w': jax.random.normal(ks[5], (D, E_R), jnp.float32) * s, 'router_b': jnp.zeros((E_R,), jnp.float32), 'sh_w1': jax.random.normal(ks[6], (D, INTER), jnp.float32) * s, 'sh_b1': jnp.zeros((INTER,), jnp.float32), 'sh_w2': jax.random.normal(ks[7], (INTER, D), jnp.float32) * s, 'sh_b2': jnp.zeros((D,), jnp.float32), 're_w1': jax.random.normal(ks[8], (E_R, D, INTER), jnp.float32) * s, 're_b1': jnp.zeros((E_R, INTER), jnp.float32), 're_w2': jax.random.normal(ks[9], (E_R, INTER, D), jnp.float32) * s, 're_b2': jnp.zeros((E_R, D), jnp.float32)}
        return inp
    _L0_ffn_in = _L0_ffn_setup()

    def _L1_attn_setup():
        import jax, jax.numpy as jnp
        import numpy as np
        NUM_HEADS = 16
        EPS = 1e-06

        def _split_heads(t, h):
            b, s, d = t.shape
            return t.reshape(b, s, h, d // h).transpose(0, 2, 1, 3)
        key = jax.random.key(seed)
        ks = jax.random.split(key, 6)
        b, s, d = (4, 512, 128)
        scale = 1.0 / np.sqrt(d)
        return {'x': jax.random.normal(ks[0], (b, s, d), dtype=jnp.float32), 'wq': jax.random.normal(ks[1], (d, d), dtype=jnp.float32) * scale, 'wk': jax.random.normal(ks[2], (d, d), dtype=jnp.float32) * scale, 'wv': jax.random.normal(ks[3], (d, d), dtype=jnp.float32) * scale, 'wo': jax.random.normal(ks[4], (d, d), dtype=jnp.float32) * scale, 'bo': jnp.zeros((d,), dtype=jnp.float32)}
    _L1_attn_in = _L1_attn_setup()

    def _L1_ffn_setup():
        import jax, jax.numpy as jnp
        import numpy as np
        B, S = (4, 64)
        H = 128
        I = 352
        E = 8
        K = 2
        IS = 176
        key = jax.random.key(seed)
        ks = jax.random.split(key, 8)

        def init(k, shape, fan_in):
            return (jax.random.normal(k, shape, jnp.float32) / np.sqrt(fan_in)).astype(jnp.float32)
        return {'hidden_states': jax.random.normal(ks[0], (B, S, H), jnp.float32), 'gate_w': init(ks[1], (H, E), H), 'Wg': init(ks[2], (E, H, I), H), 'Wu': init(ks[3], (E, H, I), H), 'Wd': init(ks[4], (E, I, H), I), 'Sg': init(ks[5], (H, IS), H), 'Su': init(ks[6], (H, IS), H), 'Sd': init(ks[7], (IS, H), IS)}
    _L1_ffn_in = _L1_ffn_setup()
    _d = {'L0_attn_x': _L0_attn_in['x'], 'L0_attn_Wq': _L0_attn_in['Wq'], 'L0_attn_Wk': _L0_attn_in['Wk'], 'L0_attn_Wv': _L0_attn_in['Wv'], 'L0_attn_Wb': _L0_attn_in['Wb'], 'L0_attn_Wg': _L0_attn_in['Wg'], 'L0_attn_Wo': _L0_attn_in['Wo'], 'L0_attn_norm_w': _L0_attn_in['norm_w'], 'L0_ffn_positions': _L0_ffn_in['positions'], 'L0_ffn_theta': _L0_ffn_in['theta'], 'L0_ffn_gamma1': _L0_ffn_in['gamma1'], 'L0_ffn_gamma2': _L0_ffn_in['gamma2'], 'L0_ffn_q_w': _L0_ffn_in['q_w'], 'L0_ffn_q_b': _L0_ffn_in['q_b'], 'L0_ffn_k_w': _L0_ffn_in['k_w'], 'L0_ffn_k_b': _L0_ffn_in['k_b'], 'L0_ffn_v_w': _L0_ffn_in['v_w'], 'L0_ffn_v_b': _L0_ffn_in['v_b'], 'L0_ffn_o_w': _L0_ffn_in['o_w'], 'L0_ffn_o_b': _L0_ffn_in['o_b'], 'L0_ffn_router_w': _L0_ffn_in['router_w'], 'L0_ffn_router_b': _L0_ffn_in['router_b'], 'L0_ffn_sh_w1': _L0_ffn_in['sh_w1'], 'L0_ffn_sh_b1': _L0_ffn_in['sh_b1'], 'L0_ffn_sh_w2': _L0_ffn_in['sh_w2'], 'L0_ffn_sh_b2': _L0_ffn_in['sh_b2'], 'L0_ffn_re_w1': _L0_ffn_in['re_w1'], 'L0_ffn_re_b1': _L0_ffn_in['re_b1'], 'L0_ffn_re_w2': _L0_ffn_in['re_w2'], 'L0_ffn_re_b2': _L0_ffn_in['re_b2'], 'L1_attn_wq': _L1_attn_in['wq'], 'L1_attn_wk': _L1_attn_in['wk'], 'L1_attn_wv': _L1_attn_in['wv'], 'L1_attn_wo': _L1_attn_in['wo'], 'L1_attn_bo': _L1_attn_in['bo'], 'L1_ffn_gate_w': _L1_ffn_in['gate_w'], 'L1_ffn_Wg': _L1_ffn_in['Wg'], 'L1_ffn_Wu': _L1_ffn_in['Wu'], 'L1_ffn_Wd': _L1_ffn_in['Wd'], 'L1_ffn_Sg': _L1_ffn_in['Sg'], 'L1_ffn_Su': _L1_ffn_in['Su'], 'L1_ffn_Sd': _L1_ffn_in['Sd']}
    _x0 = _d['L0_attn_x']
    _d['L0_attn_x'] = jax.random.normal(jax.random.fold_in(jax.random.key(seed), 1), (32, 256, 128), dtype=_x0.dtype)
    del _x0
    return _d

def reference(L0_attn_x, L0_attn_Wq, L0_attn_Wk, L0_attn_Wv, L0_attn_Wb, L0_attn_Wg, L0_attn_Wo, L0_attn_norm_w, L0_ffn_positions, L0_ffn_theta, L0_ffn_gamma1, L0_ffn_gamma2, L0_ffn_q_w, L0_ffn_q_b, L0_ffn_k_w, L0_ffn_k_b, L0_ffn_v_w, L0_ffn_v_b, L0_ffn_o_w, L0_ffn_o_b, L0_ffn_router_w, L0_ffn_router_b, L0_ffn_sh_w1, L0_ffn_sh_b1, L0_ffn_sh_w2, L0_ffn_sh_b2, L0_ffn_re_w1, L0_ffn_re_b1, L0_ffn_re_w2, L0_ffn_re_b2, L1_attn_wq, L1_attn_wk, L1_attn_wv, L1_attn_wo, L1_attn_bo, L1_ffn_gate_w, L1_ffn_Wg, L1_ffn_Wu, L1_ffn_Wd, L1_ffn_Sg, L1_ffn_Su, L1_ffn_Sd):

    def _L0_attn_ref(x, Wq, Wk, Wv, Wb, Wg, Wo, norm_w):
        import jax, jax.numpy as jnp
        import numpy as np
        D_MODEL = 128
        H = 4
        DK = 128
        DV = 32
        EPS = 1e-05
        SCALE = DK ** (-0.5)

        def _delta_rule(q, k, v, beta):
            b = q.shape[0]
            qt = jnp.moveaxis(q, 1, 0)
            kt = jnp.moveaxis(k, 1, 0)
            vt = jnp.moveaxis(v, 1, 0)
            bt = jnp.moveaxis(beta, 1, 0)
            S0 = jnp.zeros((b, H, DK, DV), q.dtype)

            def step(S, inp):
                q_t, k_t, v_t, b_t = inp
                pred = jnp.einsum('bhk,bhkv->bhv', k_t, S)
                delta = (v_t - pred) * b_t[..., None]
                S = S + k_t[..., :, None] * delta[..., None, :]
                o_t = jnp.einsum('bhk,bhkv->bhv', q_t, S)
                return (S, o_t)
            _, o = jax.lax.scan(step, S0, (qt, kt, vt, bt))
            return jnp.moveaxis(o, 0, 1)
        b, n, _ = x.shape
        q = (x @ Wq).reshape(b, n, H, DK)
        k = (x @ Wk).reshape(b, n, H, DK)
        v = (x @ Wv).reshape(b, n, H, DV)
        beta = jax.nn.sigmoid(x @ Wb)
        k = k * jax.lax.rsqrt(jnp.sum(k * k, axis=-1, keepdims=True) + 1e-12)
        q = q * SCALE
        o = _delta_rule(q, k, v, beta)
        g = (x @ Wg).reshape(b, n, H, DV)
        o = o * jax.lax.rsqrt(jnp.mean(o * o, axis=-1, keepdims=True) + EPS) * norm_w
        o = o * (g * jax.nn.sigmoid(g))
        return o.reshape(b, n, H * DV) @ Wo

    def _L0_ffn_ref(x, positions, theta, gamma1, gamma2, q_w, q_b, k_w, k_b, v_w, v_b, o_w, o_b, router_w, router_b, sh_w1, sh_b1, sh_w2, sh_b2, re_w1, re_b1, re_w2, re_b2):
        import jax, jax.numpy as jnp
        import numpy as np
        B, S, D = (2, 128, 128)
        H, HD = (16, 64)
        E_R = 31
        K_ACT = 3
        INTER = 128
        EPS = 1e-05
        BASE = 10000.0

        def _rmsnorm(x, gamma):
            rms = jnp.sqrt(jnp.mean(x * x, axis=-1, keepdims=True) + EPS)
            return x / rms * gamma

        def _rope(x, theta):
            seq = x.shape[2]
            angles = jnp.arange(seq, dtype=theta.dtype)[:, None] * theta
            cos = jnp.cos(angles)[None, None]
            sin = jnp.sin(angles)[None, None]
            x1, x2 = (x[..., 0::2], x[..., 1::2])
            return jnp.concatenate([x1 * cos - x2 * sin, x1 * sin + x2 * cos], axis=-1)

        def _forward(x, theta, gamma1, gamma2, q_w, q_b, k_w, k_b, v_w, v_b, o_w, o_b, router_w, router_b, sh_w1, sh_b1, sh_w2, sh_b2, re_w1, re_b1, re_w2, re_b2):
            b, s, d = x.shape
            xn = _rmsnorm(x, gamma1)
            q = (xn @ q_w + q_b).reshape(b, s, H, HD).transpose(0, 2, 1, 3)
            k = (xn @ k_w + k_b).reshape(b, s, H, HD).transpose(0, 2, 1, 3)
            v = (xn @ v_w + v_b).reshape(b, s, H, HD).transpose(0, 2, 1, 3)
            q = _rope(q, theta)
            k = _rope(k, theta)
            scale = 1.0 / np.sqrt(HD)
            scores = jnp.einsum('bhqd,bhkd->bhqk', q, k) * scale
            causal = jnp.tril(jnp.ones((s, s), dtype=bool))
            scores = jnp.where(causal, scores, -jnp.inf)
            attn = jax.nn.softmax(scores, axis=-1)
            ctx = jnp.einsum('bhqk,bhkd->bhqd', attn, v)
            ctx = ctx.transpose(0, 2, 1, 3).reshape(b, s, H * HD)
            attn_out = ctx @ o_w + o_b + xn
            an = _rmsnorm(attn_out, gamma2)
            shared = jax.nn.gelu(an @ sh_w1 + sh_b1, approximate=False) @ sh_w2 + sh_b2
            logits = an @ router_w + router_b
            aff = jax.nn.softmax(logits, axis=-1)
            topv, topi = jax.lax.top_k(aff, K_ACT)
            gates = jnp.sum(jax.nn.one_hot(topi, E_R, dtype=aff.dtype) * topv[..., None], axis=-2)
            h = jax.nn.gelu(jnp.einsum('bsd,edh->besh', an, re_w1) + re_b1[None, :, None, :], approximate=False)
            routed = jnp.einsum('bse,besh,ehd->bsd', gates, h, re_w2) + jnp.einsum('bse,ed->bsd', gates, re_b2)
            return shared + routed + an + attn_out
        del positions
        return _forward(x, theta, gamma1, gamma2, q_w, q_b, k_w, k_b, v_w, v_b, o_w, o_b, router_w, router_b, sh_w1, sh_b1, sh_w2, sh_b2, re_w1, re_b1, re_w2, re_b2)

    def _L1_attn_ref(x, wq, wk, wv, wo, bo):
        import jax, jax.numpy as jnp
        import numpy as np
        NUM_HEADS = 16
        EPS = 1e-06

        def _split_heads(t, h):
            b, s, d = t.shape
            return t.reshape(b, s, h, d // h).transpose(0, 2, 1, 3)
        h = NUM_HEADS
        q = _split_heads(x @ wq.T, h)
        k = _split_heads(x @ wk.T, h)
        v = _split_heads(x @ wv.T, h)
        qf = jax.nn.elu(q) + 1.0
        kf = jax.nn.elu(k) + 1.0
        k_sum = jnp.sum(kf, axis=-2)
        denom = jnp.sum(qf * k_sum[:, :, None, :], axis=-1, keepdims=True) + EPS
        kv = jnp.einsum('bhsd,bhse->bhde', kf, v)
        q_kv = jnp.einsum('bhsd,bhde->bhse', qf, kv)
        out = q_kv / denom
        b, _, s, dh = out.shape
        out = out.transpose(0, 2, 1, 3).reshape(b, s, h * dh)
        return out @ wo.T + bo

    def _L1_ffn_ref(hidden_states, gate_w, Wg, Wu, Wd, Sg, Su, Sd):
        import jax, jax.numpy as jnp
        import numpy as np
        B, S = (4, 64)
        H = 128
        I = 352
        E = 8
        K = 2
        IS = 176
        b, s, h = hidden_states.shape
        x = hidden_states.reshape(-1, h)
        T = x.shape[0]
        logits = x @ gate_w
        top_v, top_i = jax.lax.top_k(logits, K)
        top_p = jax.nn.softmax(top_v, axis=-1)
        combine = jnp.zeros((T, E), x.dtype).at[jnp.arange(T)[:, None], top_i].add(top_p)
        g = jnp.einsum('th,ehi->tei', x, Wg)
        u = jnp.einsum('th,ehi->tei', x, Wu)
        d = jnp.einsum('tei,eih->teh', jax.nn.silu(g) * u, Wd)
        expert_out = jnp.einsum('te,teh->th', combine, d)
        shared = jax.nn.silu(x @ Sg) * (x @ Su) @ Sd
        return (expert_out + shared).reshape(b, s, h)
    x = L0_attn_x
    xn = _layernorm(x, axis=-1)
    s = _L0_attn_ref(xn, L0_attn_Wq, L0_attn_Wk, L0_attn_Wv, L0_attn_Wb, L0_attn_Wg, L0_attn_Wo, L0_attn_norm_w)
    g = _silu(_L0_ffn_ref(xn, L0_ffn_positions, L0_ffn_theta, L0_ffn_gamma1, L0_ffn_gamma2, L0_ffn_q_w, L0_ffn_q_b, L0_ffn_k_w, L0_ffn_k_b, L0_ffn_v_w, L0_ffn_v_b, L0_ffn_o_w, L0_ffn_o_b, L0_ffn_router_w, L0_ffn_router_b, L0_ffn_sh_w1, L0_ffn_sh_b1, L0_ffn_sh_w2, L0_ffn_sh_b2, L0_ffn_re_w1, L0_ffn_re_b1, L0_ffn_re_w2, L0_ffn_re_b2))
    x = x + s * g
    xn = _layernorm(x, axis=-1)
    s = _L1_attn_ref(xn, L1_attn_wq, L1_attn_wk, L1_attn_wv, L1_attn_wo, L1_attn_bo)
    g = _silu(_L1_ffn_ref(xn, L1_ffn_gate_w, L1_ffn_Wg, L1_ffn_Wu, L1_ffn_Wd, L1_ffn_Sg, L1_ffn_Su, L1_ffn_Sd))
    x = x + s * g
    return x

_drawn_inputs = setup_inputs


def setup_inputs(seed=0):
    import zlib

    import numpy as np

    out = dict(_drawn_inputs(seed))
    spreads = {'L0_attn_norm_w': (1.0, 0.2),
     'L0_ffn_gamma1': (1.0, 0.2),
     'L0_ffn_gamma2': (1.0, 0.2),
     'L0_ffn_q_b': (0.0, 0.8),
     'L0_ffn_k_b': (0.0, 0.8),
     'L0_ffn_v_b': (0.0, 0.467),
     'L0_ffn_o_b': (0.0, 0.29),
     'L0_ffn_router_b': (0.0, 0.8),
     'L0_ffn_sh_b1': (0.0, 0.8),
     'L0_ffn_sh_b2': (0.0, 0.524),
     'L0_ffn_re_b1': (0.0, 0.8),
     'L0_ffn_re_b2': (0.0, 0.8),
     'L1_attn_bo': (0.0, 0.1)}
    factors = {'L0_ffn_theta': 8.0,
     'L0_ffn_q_w': 8.0,
     'L0_ffn_k_w': 8.0,
     'L0_ffn_v_w': 8.0,
     'L0_ffn_o_w': 3.102,
     'L0_ffn_router_w': 8.0,
     'L0_ffn_sh_w1': 8.0,
     'L0_ffn_sh_w2': 8.0,
     'L0_ffn_re_w1': 8.0,
     'L0_ffn_re_w2': 8.0,
     'L1_attn_wq': 22.189,
     'L1_attn_wk': 4.411}
    for name, (base, spread) in spreads.items():
        noise = np.random.default_rng([zlib.crc32(name.encode()), seed]).standard_normal(out[name].shape)
        drawn = base * np.exp(spread * noise) if base else spread * noise
        out[name] = jnp.asarray(drawn.astype(out[name].dtype))
    for name, factor in factors.items():
        out[name] = (out[name] * factor).astype(out[name].dtype)
    return out
```

```python
from contextlib import ExitStack

import concourse.bass as bass
import numpy as np
from concourse import mybir

ALU = mybir.AluOpType
ACT = mybir.ActivationFunctionType
F32 = mybir.dt.float32
F16 = mybir.dt.float16
BF16 = mybir.dt.bfloat16
AX = mybir.AxisListType.X

P = 128
SEQ = 256
TILE = 512
TB = TILE // P
SEQS = TILE // SEQ
EPS = 1e-5


class Signal:

    def __init__(self, handle, per, first=0):
        self.handle, self.per, self.first = handle, per, first

    def at(self, turn, n):
        return turn * self.per + (self.first + n)

    def before(self, turn, n=None):
        return turn * self.per + (self.first + (self.per if n is None else n) - self.per)


class Memory:

    def __init__(self, nc, ctx, name):
        self.nc, self.ctx, self.name, self.handles = nc, ctx, name, []
        ctx.callback(self.clear_semaphores)

    def sbuf(self, name, shape, dtype=F32):
        return self.ctx.enter_context(self.nc.sbuf_tensor(f"{self.name}_{name}", shape, dtype))

    def banks(self, name, n):
        return [self.ctx.enter_context(self.nc.psum_tensor(f"{self.name}_{name}_bank{k}", [P, 512], F32)) for k in range(n)]

    def count(self, name, per=1, first=0):
        self.handles.append(self.nc.alloc_semaphore(f"{self.name}_{name}"))
        return Signal(self.handles[-1], per, first)

    def clear_semaphores(self):
        self.nc.clear_and_free_semaphores(self.handles)
        self.nc.all_engine_barrier()


def split_product(pe, out, left, right, start=True, stop=True):
    (lh, ll), (rh, rl) = left, right
    pe.matmul(out, ll, rh, start=start, stop=False, skip_group_check=True)
    pe.matmul(out, lh, rl, start=False, stop=False, skip_group_check=True)
    return pe.matmul(out, lh, rh, start=False, stop=stop, skip_group_check=True)


def over(ap, n, axis=1):
    ap = ap.unsqueeze(axis)
    shape = list(ap.shape)
    shape[axis] = n
    return ap.to_broadcast(shape)


def delta_phase(nc, x, wq, wk, wvgb, wo, norm_w, eye, below, upto, xn_out, s_out):
    H, DK, DV = 4, 128, 32
    turns = x.shape[0] // TILE
    LEVELS = 7
    SCALE = DK ** -0.5
    x_v = x.rearrange("(n t p) d -> n p t d", t=TB, p=P)
    xn_v = xn_out.rearrange("(n t p) d -> n p t d", t=TB, p=P)
    nv = wvgb.shape[1]

    with ExitStack() as ctx:
        m = Memory(nc, ctx, "delta")
        eye32, eye16 = m.sbuf("eye32", [P, P]), m.sbuf("eye16", [P, P], F16)
        below_m, upto_m = m.sbuf("below", [P, P]), m.sbuf("upto", [P, P])
        eps = m.sbuf("eps", [P, 2])
        norm_row = m.sbuf("norm_row", [P, DV])
        stage = m.sbuf("w_stage", [P, 512 + 512 + nv + 128])
        w_pair = m.sbuf("w_pair", [P, 2, 512 + 512 + nv + 128], F16)
        cut = {"q": (0, 512), "k": (512, 1024), "vgb": (1024, 1024 + nv), "o": (1024 + nv, 1152 + nv)}

        def weight(name, a=0, b=None):
            lo, hi = cut[name]
            b = hi - lo if b is None else b
            return w_pair[:, 0, lo + a:lo + b], w_pair[:, 1, lo + a:lo + b]

        x_in = m.sbuf("x_in", [P, TB, P])
        stats = m.sbuf("stats", [P, TB, 6])
        mean_var = m.sbuf("mean_var", [P, TB, 2])
        std = m.sbuf("std", [P, TB])
        rstd = m.sbuf("rstd", [P, TB])
        xn = m.sbuf("xn", [P, TB, P])
        xT = m.sbuf("xT", [P, 2, TILE], F16)
        ksq = m.sbuf("ksq", [P, TB, H * DK])
        kss = m.sbuf("kss", [P, TB * H])
        knorm = m.sbuf("knorm", [P, TB * H])
        krn = m.sbuf("krn", [P, TB * H])
        khat = m.sbuf("khat", [P, TB, H * DK])
        kT = m.sbuf("kT", [P, 2, TB, H * P], F16)
        qT = m.sbuf("qT", [P, 2, H, TILE], F16)
        v = m.sbuf("v", [P, TB, H * DV])
        g = m.sbuf("g", [P, TB, H * DV])
        gate = m.sbuf("gate", [P, TB, H * DV])
        beta = m.sbuf("beta", [P, TB, H])
        neg_beta = m.sbuf("neg_beta", [P, TB, H])
        b32 = [m.sbuf(f"b32_{s}", [P, H * P]) for s in range(SEQS)]
        power = [[m.sbuf(f"power{s}_{k}", [P, 2, H * P], F16) for k in range(2)] for s in range(SEQS)]
        powerT = [[m.sbuf(f"powerT{s}_{k}", [P, 2, H * P], F16) for k in range(2)] for s in range(SEQS)]
        rhs32 = [m.sbuf(f"rhs32_{s}", [P, H * DV]) for s in range(SEQS)]
        rhs = [m.sbuf(f"rhs{s}", [P, 2, H * DV], F16) for s in range(SEQS)]
        qk = [m.sbuf(f"qk{s}", [P, H * P]) for s in range(SEQS)]
        upd = [m.sbuf(f"upd{s}", [P, H * DV]) for s in range(SEQS)]
        state = [m.sbuf(f"state{s}", [P, 2, H * DV], F16) for s in range(SEQS)]
        o = m.sbuf("o", [P, TB, H * DV])
        osq = m.sbuf("osq", [P, TB * H * DV])
        oss = m.sbuf("oss", [P, TB * H])
        ostd = m.sbuf("ostd", [P, TB * H])
        orn = m.sbuf("orn", [P, TB * H])
        og = m.sbuf("og", [P, TB * H * DV])
        oT = m.sbuf("oT", [P, 2, TILE], F16)
        sT = m.sbuf("sT", [P, TILE])

        pow_ps, powT_ps = m.banks("pow", 2), m.banks("powT", 2)
        rhs_ps, misc_ps = m.banks("rhs", 2), m.banks("misc", 2)
        prep = pow_ps + powT_ps

        S = m.count
        const_in = S("const_in")
        w_ready = S("w_ready")
        x_loaded = S("x_loaded", 16)
        stats_done, aggr_done = S("stats_done"), S("aggr_done")
        std_done, rstd_done = S("std_done"), S("rstd_done")
        xn_done, xn_stored = S("xn_done", 1, 1), S("xn_stored", 16, 16)
        xT_ps_done, xT_hi, xT_lo = S("xT_ps_done"), S("xT_hi"), S("xT_lo")
        k_ps, ksq_done, kss_done = S("k_ps", TB), S("ksq_done", TB), S("kss_done", 1)
        knorm_done, krn_done, khat_done = S("knorm_done"), S("krn_done"), S("khat_done", TB)
        kT_ps, kT_hi, kT_lo = S("kT_ps", TB), S("kT_hi", TB), S("kT_lo", TB)
        q_ps, q_hi, q_lo = S("q_ps", H), S("q_hi", H), S("q_lo", H)
        v_ps, g_sig, gate_half, gate_done = S("v_ps", TB), S("g_sig", TB), S("gate_half"), S("gate_done")
        negb_done = S("negb_done", 1)
        gram_ps, b32_done, b_hi, b_lo = S("gram_ps", TB), S("b32_done", TB), S("b_hi", TB), S("b_lo", TB)
        qk_ps, qk_done = S("qk_ps", TB), S("qk_done", TB)
        bT_ps, bT_done = S("bT_ps", TB), S("bT_done", TB)
        ks_ps, rhs_sub, rhs32_done = S("ks_ps", SEQS), S("rhs_sub", SEQS), S("rhs32_done", TB)
        NR = TB * LEVELS
        rhs_hi, rhs_lo = S("rhs_hi", NR), S("rhs_lo", NR)
        rhs_step = S("rhs_step", TB * LEVELS)
        NP = TB * (LEVELS - 2)
        NT = TB * (LEVELS - 1)
        pow_step, pow_hi, pow_lo = S("pow_step", NP), S("pow_hi", NP), S("pow_lo", NP)
        powT_step, powT_hi, powT_lo = S("powT_step", NT), S("powT_hi", NT), S("powT_lo", NT)
        upd_done = S("upd_done", TB)
        state_ps, state_hi, state_lo = S("state_ps", SEQS), S("state_hi", SEQS), S("state_lo", SEQS)
        o_ps, o_out = S("o_ps", TB), S("o_out", TB)
        osq_done, oss_done, ostd_done, orn_done = S("osq_done"), S("oss_done"), S("ostd_done"), S("orn_done")
        on_done, og_done = S("on_done"), S("og_done", 1)
        oT_ps, oT_hi, oT_lo = S("oT_ps"), S("oT_hi"), S("oT_lo")
        s_ps, s_copied, s_stored = S("s_ps"), S("s_copied"), S("s_stored", 16, 16)
        order = S("order")

        block = ctx.enter_context(nc.Block())

        @block.sync
        def _(sp):
            for dst, src in ((stage[:, 0:512], wq), (stage[:, 512:1024], wk), (stage[:, 1024:1024 + nv], wvgb),
                             (stage[:, 1024 + nv:], wo), (eye32[:], eye), (below_m[:], below), (upto_m[:], upto),
                             (norm_row[:], norm_w.rearrange("(a d) -> a d", a=1).to_broadcast([P, DV]))):
                sp.dma_start(dst, src).then_inc(const_in.handle, 16)
            sp.sem_inc(xn_stored.handle, 16)
            sp.sem_inc(s_stored.handle, 16)
            sp.sem_inc(xn_done.handle, 1)
            with sp.Fori(0, turns) as i:
                sp.wait_ge(xn_done.handle, xn_done.before(i))
                sp.dma_start(x_in[:], x_v[i]).then_inc(x_loaded.handle, 16)
                sp.wait_ge(xn_done.handle, xn_done.at(i, 1))
                sp.dma_start(xn_v[i], xn[:]).then_inc(xn_stored.handle, 16)
            sp.wait_ge(xn_stored.handle, 16 * (turns + 1))
            sp.wait_ge(s_stored.handle, 16 * (turns + 1))

        @block.tensor
        def _(te):
            pe = nc.tensor
            te.wait_ge(const_in.handle, 16 * 8)
            te.wait_ge(w_ready.handle, 3)
            with te.Fori(0, turns) as i:
                te.wait_ge(xn_done.handle, xn_done.at(i, 1))
                for t in range(TB):
                    last = pe.transpose(misc_ps[0][:, t * P:(t + 1) * P], xn[:, t, :], eye32[:])
                last.then_inc(xT_ps_done.handle, 1)
                te.wait_ge(xT_lo.handle, xT_lo.at(i, 1))
                for t in range(TB):
                    split_product(pe, prep[t][:], (xT[:, 0, t * P:(t + 1) * P], xT[:, 1, t * P:(t + 1) * P]),
                                  weight("k")).then_inc(k_ps.handle, 1)
                for t in range(TB):
                    bank = misc_ps[t % 2]
                    if t >= 2:
                        te.wait_ge(g_sig.handle, g_sig.at(i, t - 1))
                    split_product(pe, bank[:, 0:nv], (xT[:, 0, t * P:(t + 1) * P], xT[:, 1, t * P:(t + 1) * P]),
                                  weight("vgb")).then_inc(v_ps.handle, 1)
                for t in range(TB):
                    te.wait_ge(khat_done.handle, khat_done.at(i, t + 1))
                    for h in range(H):
                        last = pe.transpose(prep[t][:, h * P:(h + 1) * P], khat[:, t, h * DK:(h + 1) * DK], eye32[:])
                    last.then_inc(kT_ps.handle, 1)
                for h in range(H):
                    bank = rhs_ps[h % 2]
                    if h >= 2:
                        te.wait_ge(q_lo.handle, q_lo.at(i, h - 1))
                    split_product(pe, bank[:], weight("q", h * DK, (h + 1) * DK),
                                  (xT[:, 0, :], xT[:, 1, :])).then_inc(q_ps.handle, 1)
                for c in range(2):
                    for s in range(SEQS):
                        t, n = 2 * s + c, 2 * c + s
                        kt = [(kT[:, 0, t, h * P:(h + 1) * P], kT[:, 1, t, h * P:(h + 1) * P]) for h in range(H)]
                        if c == 0:
                            te.wait_ge(kT_lo.handle, kT_lo.at(i, TB))
                        for h in range(H):
                            last = split_product(pe, pow_ps[s][:, h * P:(h + 1) * P], kt[h], kt[h])
                        last.then_inc(gram_ps.handle, 1)
                        te.wait_ge(q_lo.handle, q_lo.at(i, H))
                        for h in range(H):
                            q = (qT[:, 0, h, t * P:(t + 1) * P], qT[:, 1, h, t * P:(t + 1) * P])
                            last = split_product(pe, powT_ps[s][:, h * P:(h + 1) * P], kt[h], q)
                        last.then_inc(qk_ps.handle, 1)
                        if c == 1:
                            te.wait_ge(state_lo.handle, state_lo.at(i, s + 1))
                            for h in range(H):
                                st = (state[s][:, 0, h * DV:(h + 1) * DV], state[s][:, 1, h * DV:(h + 1) * DV])
                                last = split_product(pe, rhs_ps[s][:, h * DV:(h + 1) * DV], kt[h], st)
                            last.then_inc(ks_ps.handle, 1)
                    for s in range(SEQS):
                        n = 2 * c + s
                        te.wait_ge(b_lo.handle, b_lo.at(i, n + 1))
                        if c == 0 and s == 0:
                            te.wait_ge(g_sig.handle, g_sig.at(i, TB))
                        if c == 1:
                            te.wait_ge(o_out.handle, o_out.at(i, s + 1))
                        tr = misc_ps[s][:].bitcast(F16)
                        for half in range(2):
                            for h in range(H):
                                at = (half * H + h) * P
                                last = pe.transpose(tr[:, at:at + P], power[s][0][:, half, h * P:(h + 1) * P], eye16[:])
                        last.then_inc(bT_ps.handle, 1)
                        te.wait_ge(rhs_lo.handle, rhs_lo.at(i, c * SEQS * LEVELS + s + 1))
                        pe.matmul(rhs_ps[s][:, 0:H * DV], eye16[:], rhs[s][:, 1, :], start=True, stop=False,
                                  skip_group_check=True)
                        pe.matmul(rhs_ps[s][:, 0:H * DV], eye16[:], rhs[s][:, 0, :], start=False, stop=False,
                                  skip_group_check=True)
                    for level in range(LEVELS):
                        cur = level % 2
                        for s in range(SEQS):
                            n = 2 * c + s
                            pw, pT = power[s][cur], powerT[s][cur]
                            done = c * SEQS * LEVELS + level * SEQS + s + 1
                            if level == 0:
                                te.wait_ge(bT_done.handle, bT_done.at(i, n + 1))
                            else:
                                te.wait_ge(powT_lo.handle, powT_lo.at(i, c * SEQS * (LEVELS - 1) + (level - 1) * SEQS + s + 1))
                                te.wait_ge(rhs_lo.handle, rhs_lo.at(i, done))
                            for h in range(H):
                                last = split_product(pe, rhs_ps[s][:, h * DV:(h + 1) * DV],
                                                     (pT[:, 0, h * P:(h + 1) * P], pT[:, 1, h * P:(h + 1) * P]),
                                                     (rhs[s][:, 0, h * DV:(h + 1) * DV], rhs[s][:, 1, h * DV:(h + 1) * DV]),
                                                     start=False, stop=(level == LEVELS - 1))
                            last.then_inc(rhs_step.handle, 1)
                            if level == LEVELS - 1:
                                continue
                            if level == 0:
                                te.wait_ge(b_lo.handle, b_lo.at(i, n + 1))
                                te.wait_ge(qk_done.handle, qk_done.at(i, n + 1))
                            else:
                                te.wait_ge(pow_lo.handle, pow_lo.at(i, c * SEQS * (LEVELS - 2) + (level - 1) * SEQS + s + 1))
                            ph = [(pw[:, 0, h * P:(h + 1) * P], pw[:, 1, h * P:(h + 1) * P]) for h in range(H)]
                            pt = [(pT[:, 0, h * P:(h + 1) * P], pT[:, 1, h * P:(h + 1) * P]) for h in range(H)]
                            for h in range(H):
                                last = split_product(pe, powT_ps[s][:, h * P:(h + 1) * P], ph[h], pt[h])
                            last.then_inc(powT_step.handle, 1)
                            if level < LEVELS - 2:
                                for h in range(H):
                                    last = split_product(pe, pow_ps[s][:, h * P:(h + 1) * P], pt[h], ph[h])
                                last.then_inc(pow_step.handle, 1)
                    for s in range(SEQS):
                        t, n = 2 * s + c, 2 * c + s
                        te.wait_ge(upd_done.handle, upd_done.at(i, n + 1))
                        for h in range(H):
                            out = misc_ps[s][:, h * DV:(h + 1) * DV]
                            if c == 1:
                                q = (qT[:, 0, h, t * P:(t + 1) * P], qT[:, 1, h, t * P:(t + 1) * P])
                                st = (state[s][:, 0, h * DV:(h + 1) * DV], state[s][:, 1, h * DV:(h + 1) * DV])
                                split_product(pe, out, q, st, stop=False)
                            last = pe.matmul(out, qk[s][:, h * P:(h + 1) * P], upd[s][:, h * DV:(h + 1) * DV],
                                             start=(c == 0), stop=True, skip_group_check=True)
                        last.then_inc(o_ps.handle, 1)
                        if c == 0:
                            for h in range(H):
                                last = pe.matmul(rhs_ps[s][:, h * DV:(h + 1) * DV], khat[:, t, h * DK:(h + 1) * DK],
                                                 upd[s][:, h * DV:(h + 1) * DV], start=True, stop=True)
                            last.then_inc(state_ps.handle, 1)
                te.wait_ge(og_done.handle, og_done.at(i, 1))
                for t in range(TB):
                    last = pe.transpose(misc_ps[0][:, t * P:(t + 1) * P], og[:, t * P:(t + 1) * P], eye32[:])
                last.then_inc(oT_ps.handle, 1)
                te.wait_ge(oT_lo.handle, oT_lo.at(i, 1))
                split_product(pe, misc_ps[1][:], weight("o"), (oT[:, 0, :], oT[:, 1, :])).then_inc(s_ps.handle, 1)
                te.wait_ge(s_copied.handle, s_copied.at(i, 1))

        @block.scalar
        def _(ac):
            act = nc.scalar.activation
            ac.wait_ge(const_in.handle, 16 * 8)
            act(w_pair[:, 0, :], stage[:], ACT.Copy).then_inc(w_ready.handle, 1)
            act(eye16[:], eye32[:], ACT.Copy).then_inc(w_ready.handle, 1)
            ac.wait_ge(order.handle, 2)
            with ac.Fori(0, turns) as i:
                ac.wait_ge(aggr_done.handle, aggr_done.at(i, 1))
                act(std[:], mean_var[:, :, 1], ACT.Sqrt, bias=eps[:, 0:1]).then_inc(std_done.handle, 1)
                ac.wait_ge(xT_ps_done.handle, xT_ps_done.at(i, 1))
                act(xT[:, 0, :], misc_ps[0][:], ACT.Copy).then_inc(xT_hi.handle, 1)
                for t in range(TB):
                    ac.wait_ge(k_ps.handle, k_ps.at(i, t + 1))
                    act(ksq[:, t, :], prep[t][:], ACT.Square).then_inc(ksq_done.handle, 1)
                ac.wait_ge(kss_done.handle, kss_done.at(i, 1))
                act(knorm[:], kss[:], ACT.Sqrt, bias=eps[:, 1:2]).then_inc(knorm_done.handle, 1)
                for t in range(TB):
                    bank = misc_ps[t % 2]
                    ac.wait_ge(v_ps.handle, v_ps.at(i, t + 1))
                    act(v[:, t, :], bank[:, 0:128], ACT.Copy)
                    act(g[:, t, :], bank[:, 128:256], ACT.Copy)
                    act(gate[:, t, :], bank[:, 128:256], ACT.Sigmoid)
                    act(beta[:, t, :], bank[:, 256:260], ACT.Sigmoid).then_inc(g_sig.handle, 1)
                for t in range(TB):
                    ac.wait_ge(kT_ps.handle, kT_ps.at(i, t + 1))
                    act(kT[:, 0, t, :], prep[t][:], ACT.Copy).then_inc(kT_hi.handle, 1)
                for h in range(H):
                    ac.wait_ge(q_ps.handle, q_ps.at(i, h + 1))
                    act(qT[:, 0, h, :], rhs_ps[h % 2][:], ACT.Copy, scale=SCALE).then_inc(q_hi.handle, 1)
                for c in range(2):
                    for s in range(SEQS):
                        n = 2 * c + s
                        ac.wait_ge(b32_done.handle, b32_done.at(i, n + 1))
                        act(power[s][0][:, 0, :], b32[s][:], ACT.Copy).then_inc(b_hi.handle, 1)
                        ac.wait_ge(rhs32_done.handle, rhs32_done.at(i, n + 1))
                        act(rhs[s][:, 0, :], rhs32[s][:], ACT.Copy).then_inc(rhs_hi.handle, 1)
                    for s in range(SEQS):
                        n = 2 * c + s
                        ac.wait_ge(bT_ps.handle, bT_ps.at(i, n + 1))
                        act(powerT[s][0][:].rearrange("p a n -> p (a n)"), misc_ps[s][:].bitcast(F16), ACT.Copy).then_inc(bT_done.handle, 1)
                    for level in range(LEVELS):
                        new = (level + 1) % 2
                        for s in range(SEQS):
                            ac.wait_ge(rhs_step.handle, rhs_step.at(i, c * SEQS * LEVELS + level * SEQS + s + 1))
                            if level == LEVELS - 1:
                                act(upd[s][:], rhs_ps[s][:, 0:H * DV], ACT.Copy).then_inc(upd_done.handle, 1)
                                continue
                            act(rhs[s][:, 0, :], rhs_ps[s][:, 0:H * DV], ACT.Copy).then_inc(rhs_hi.handle, 1)
                            ac.wait_ge(powT_step.handle, powT_step.at(i, c * SEQS * (LEVELS - 1) + level * SEQS + s + 1))
                            act(powerT[s][new][:, 0, :], powT_ps[s][:], ACT.Copy).then_inc(powT_hi.handle, 1)
                            if level < LEVELS - 2:
                                ac.wait_ge(pow_step.handle, pow_step.at(i, c * SEQS * (LEVELS - 2) + level * SEQS + s + 1))
                                act(power[s][new][:, 0, :], pow_ps[s][:], ACT.Copy).then_inc(pow_hi.handle, 1)
                    for s in range(SEQS):
                        t, n = 2 * s + c, 2 * c + s
                        if c == 0:
                            ac.wait_ge(state_ps.handle, state_ps.at(i, s + 1))
                            act(state[s][:, 0, :], rhs_ps[s][:, 0:H * DV], ACT.Copy).then_inc(state_hi.handle, 1)
                        ac.wait_ge(o_ps.handle, o_ps.at(i, n + 1))
                        act(o[:, t, :], misc_ps[s][:, 0:H * DV], ACT.Copy).then_inc(o_out.handle, 1)
                ac.wait_ge(o_out.handle, o_out.at(i, TB))
                act(osq[:], o[:].rearrange("p t n -> p (t n)"), ACT.Square).then_inc(osq_done.handle, 1)
                ac.wait_ge(oss_done.handle, oss_done.at(i, 1))
                act(ostd[:], oss[:], ACT.Sqrt, bias=eps[:, 0:1], scale=1.0 / DV).then_inc(ostd_done.handle, 1)
                ac.wait_ge(oT_ps.handle, oT_ps.at(i, 1))
                act(oT[:, 0, :], misc_ps[0][:], ACT.Copy).then_inc(oT_hi.handle, 1)
                ac.wait_ge(s_ps.handle, s_ps.at(i, 1))
                ac.wait_ge(s_stored.handle, s_stored.before(i))
                act(sT[:], misc_ps[1][:], ACT.Copy).then_inc(s_copied.handle, 1)
                ac.wait_ge(s_copied.handle, s_copied.at(i, 1))
                ac.dma_start(s_out[:, bass.ts(i, TILE)], sT[:]).then_inc(s_stored.handle, 16)

        @block.vector
        def _(ve):
            vec = nc.vector
            vec.memset(eps[:, 0:1], EPS).then_inc(order.handle, 1)
            vec.memset(eps[:, 1:2], 1e-12).then_inc(order.handle, 1)
            ve.wait_ge(w_ready.handle, 2)
            ve.wait_ge(const_in.handle, 16 * 8)
            vec.tensor_tensor(w_pair[:, 1, :], stage[:], w_pair[:, 0, :], ALU.subtract).then_inc(w_ready.handle, 1)

            def low(out, exact, high):
                return vec.tensor_tensor(out, exact, high, ALU.subtract)

            with ve.Fori(0, turns) as i:
                ve.wait_ge(x_loaded.handle, x_loaded.at(i, 16))
                for t in range(TB):
                    last = vec.bn_stats(stats[:, t, :], x_in[:, t, :])
                last.then_inc(stats_done.handle, 1)
                ve.wait_ge(stats_done.handle, stats_done.at(i, 1))
                ve.sem_inc(order.handle, 1)
                for t in range(TB):
                    last = vec.bn_aggr(mean_var[:, t, :], stats[:, t, :])
                last.then_inc(aggr_done.handle, 1)
                ve.wait_ge(std_done.handle, std_done.at(i, 1))
                vec.reciprocal(rstd[:], std[:]).then_inc(rstd_done.handle, 1)
                ve.wait_ge(rstd_done.handle, rstd_done.at(i, 1))
                ve.wait_ge(xn_stored.handle, xn_stored.before(i))
                for t in range(TB):
                    last = vec.tensor_scalar(xn[:, t, :], x_in[:, t, :], mean_var[:, t, 0:1], rstd[:, t:t + 1],
                                             ALU.subtract, ALU.mult)
                last.then_inc(xn_done.handle, 1)
                ve.wait_ge(xT_hi.handle, xT_hi.at(i, 1))
                low(xT[:, 1, :], misc_ps[0][:], xT[:, 0, :]).then_inc(xT_lo.handle, 1)
                for t in range(TB):
                    ve.wait_ge(ksq_done.handle, ksq_done.at(i, t + 1))
                    last = vec.tensor_reduce(kss[:, t * H:(t + 1) * H], ksq[:, t, :].rearrange("p (h d) -> p h d", h=H),
                                             AX, ALU.add)
                last.then_inc(kss_done.handle, 1)
                ve.wait_ge(knorm_done.handle, knorm_done.at(i, 1))
                vec.reciprocal(krn[:], knorm[:]).then_inc(krn_done.handle, 1)
                ve.wait_ge(krn_done.handle, krn_done.at(i, 1))
                for t in range(TB):
                    vec.tensor_tensor(khat[:, t, :].rearrange("p (h d) -> p h d", h=H),
                                      prep[t][:].rearrange("p (h d) -> p h d", h=H),
                                      over(krn[:, t * H:(t + 1) * H], DK, 2), ALU.mult).then_inc(khat_done.handle, 1)
                ve.wait_ge(g_sig.handle, g_sig.at(i, TB))
                vec.tensor_scalar(neg_beta[:], beta[:], -1.0, None, ALU.mult).then_inc(negb_done.handle, 1)
                for t in range(TB):
                    ve.wait_ge(kT_hi.handle, kT_hi.at(i, t + 1))
                    low(kT[:, 1, t, :], prep[t][:], kT[:, 0, t, :]).then_inc(kT_lo.handle, 1)
                for h in range(H):
                    ve.wait_ge(q_hi.handle, q_hi.at(i, h + 1))
                    vec.scalar_tensor_tensor(out=qT[:, 1, h, :], in0=rhs_ps[h % 2][:], scalar=SCALE, in1=qT[:, 0, h, :],
                                             op0=ALU.mult, op1=ALU.subtract).then_inc(q_lo.handle, 1)
                for c in range(2):
                    for s in range(SEQS):
                        t, n = 2 * s + c, 2 * c + s
                        bt = over(beta[:, t, :], DV, 2)
                        r3 = rhs32[s][:].rearrange("p (h d) -> p h d", h=H)
                        v3 = v[:, t, :].rearrange("p (h d) -> p h d", h=H)
                        ve.wait_ge(gram_ps.handle, gram_ps.at(i, n + 1))
                        if c == 0 and s == 0:
                            ve.wait_ge(negb_done.handle, negb_done.at(i, 1))
                        for h in range(H):
                            last = vec.scalar_tensor_tensor(out=b32[s][:, h * P:(h + 1) * P],
                                                            in0=pow_ps[s][:, h * P:(h + 1) * P],
                                                            scalar=neg_beta[:, t, h:h + 1], in1=below_m[:],
                                                            op0=ALU.mult, op1=ALU.mult)
                        last.then_inc(b32_done.handle, 1)
                        if c == 0:
                            vec.tensor_tensor(r3, v3, bt, ALU.mult).then_inc(rhs32_done.handle, 1)
                        else:
                            ve.wait_ge(ks_ps.handle, ks_ps.at(i, s + 1))
                            vec.tensor_tensor(rhs32[s][:], v[:, t, :], rhs_ps[s][:, 0:H * DV], ALU.subtract)\
                               .then_inc(rhs_sub.handle, 1)
                            ve.wait_ge(rhs_sub.handle, rhs_sub.at(i, s + 1))
                            vec.tensor_tensor(r3, r3, bt, ALU.mult).then_inc(rhs32_done.handle, 1)
                        ve.wait_ge(qk_ps.handle, qk_ps.at(i, n + 1))
                        vec.tensor_tensor(qk[s][:].rearrange("p (h n) -> p h n", h=H),
                                          powT_ps[s][:].rearrange("p (h n) -> p h n", h=H),
                                          over(upto_m[:], H), ALU.mult).then_inc(qk_done.handle, 1)
                        ve.wait_ge(b_hi.handle, b_hi.at(i, n + 1))
                        low(power[s][0][:, 1, :], b32[s][:], power[s][0][:, 0, :]).then_inc(b_lo.handle, 1)
                        ve.wait_ge(rhs_hi.handle, rhs_hi.at(i, c * SEQS * LEVELS + s + 1))
                        low(rhs[s][:, 1, :], rhs32[s][:], rhs[s][:, 0, :]).then_inc(rhs_lo.handle, 1)
                    for level in range(LEVELS - 1):
                        new = (level + 1) % 2
                        for s in range(SEQS):
                            ve.wait_ge(rhs_hi.handle, rhs_hi.at(i, c * SEQS * LEVELS + (level + 1) * SEQS + s + 1))
                            low(rhs[s][:, 1, :], rhs_ps[s][:, 0:H * DV], rhs[s][:, 0, :]).then_inc(rhs_lo.handle, 1)
                            ve.wait_ge(powT_hi.handle, powT_hi.at(i, c * SEQS * (LEVELS - 1) + level * SEQS + s + 1))
                            low(powerT[s][new][:, 1, :], powT_ps[s][:], powerT[s][new][:, 0, :])\
                                .then_inc(powT_lo.handle, 1)
                            if level < LEVELS - 2:
                                ve.wait_ge(pow_hi.handle, pow_hi.at(i, c * SEQS * (LEVELS - 2) + level * SEQS + s + 1))
                                low(power[s][new][:, 1, :], pow_ps[s][:], power[s][new][:, 0, :])\
                                    .then_inc(pow_lo.handle, 1)
                    if c == 0:
                        for s in range(SEQS):
                            ve.wait_ge(state_hi.handle, state_hi.at(i, s + 1))
                            low(state[s][:, 1, :], rhs_ps[s][:, 0:H * DV], state[s][:, 0, :])\
                                .then_inc(state_lo.handle, 1)
                ve.wait_ge(osq_done.handle, osq_done.at(i, 1))
                vec.tensor_reduce(oss[:], osq[:].rearrange("p (n d) -> p n d", d=DV), AX, ALU.add)\
                   .then_inc(oss_done.handle, 1)
                ve.wait_ge(ostd_done.handle, ostd_done.at(i, 1))
                vec.reciprocal(orn[:], ostd[:]).then_inc(orn_done.handle, 1)
                ve.wait_ge(orn_done.handle, orn_done.at(i, 1))
                ve.wait_ge(gate_done.handle, gate_done.at(i, 1))
                vec.tensor_tensor(og[:].rearrange("p (n d) -> p n d", d=DV),
                                  o[:].rearrange("p t (h d) -> p (t h) d", d=DV), over(orn[:], DV, 2), ALU.mult)\
                   .then_inc(on_done.handle, 1)
                ve.wait_ge(on_done.handle, on_done.at(i, 1))
                vec.tensor_tensor(og[:], og[:], gate[:].rearrange("p t n -> p (t n)"), ALU.mult)\
                   .then_inc(og_done.handle, 1)
                ve.wait_ge(oT_hi.handle, oT_hi.at(i, 1))
                low(oT[:, 1, :], misc_ps[0][:], oT[:, 0, :]).then_inc(oT_lo.handle, 1)

        @block.gpsimd
        def _(po):
            with po.Fori(0, turns) as i:
                po.wait_ge(g_sig.handle, g_sig.at(i, TB))
                nc.gpsimd.tensor_tensor(gate[:], gate[:], g[:], ALU.mult).then_inc(gate_half.handle, 1)
                po.wait_ge(gate_half.handle, gate_half.at(i, 1))
                nc.gpsimd.tensor_tensor(gate[:].rearrange("p t (h d) -> p (t h) d", d=DV),
                                        gate[:].rearrange("p t (h d) -> p (t h) d", d=DV),
                                        over(norm_row[:], TB * H), ALU.mult).then_inc(gate_done.handle, 1)


def attention_phase(nc, xn_in, qk_w, qk_b, v_w, v_b, o_w, o_b, gamma1, gamma2, theta, position, half_sign,
                    eye, future, an_out, rest_out, turns):
    HEADS, HD, PAIRS = 16, 64, 8
    xn_v = xn_in.rearrange("(n t p) d -> n p t d", t=TB, p=P)
    TWO_PI = 6.283185307179586
    C1 = 6.28125
    C2 = float(np.float32(np.round((TWO_PI - C1) * 2 ** 21) / 2 ** 21))
    C3 = TWO_PI - C1 - C2
    ROUND = 1.5 * 2.0 ** 23
    UNITS = PAIRS * SEQS * 2

    with ExitStack() as ctx:
        m = Memory(nc, ctx, "attn")
        eye32, future_m = m.sbuf("eye32", [P, P]), m.sbuf("future32", [P, P])
        eyeb, futureb = m.sbuf("eyeb", [P, P], BF16), m.sbuf("futureb", [P, P], BF16)
        ones = m.sbuf("ones", [P, P])
        eps = m.sbuf("eps", [P, 1])
        gam1, gam2, ob = m.sbuf("gam1", [P, 1]), m.sbuf("gam2", [P, 1]), m.sbuf("ob", [P, 1])
        vb = m.sbuf("vb", [P, PAIRS])
        qkb = m.sbuf("qkb", [P, 4, PAIRS])
        th, sign = m.sbuf("th", [P, 1]), m.sbuf("sign", [P, 1])
        pos = m.sbuf("pos", [P, SEQ])
        ang = [m.sbuf(f"ang{k}", [P, SEQ]) for k in range(4)]
        table = m.sbuf("table", [P, 2, 2, SEQ])
        stage = m.sbuf("w_stage", [P, 2048])
        qkw = m.sbuf("qkw", [P, 2, 4 * 1024], F16)
        vw = m.sbuf("vw", [P, 2, 1024], F16)
        ow = m.sbuf("ow", [P, 2, 1024], F16)

        xn = m.sbuf("xn", [P, TB, P])
        sq = m.sbuf("sq", [P, TB * P])
        ss, std, rr = m.sbuf("ss", [P, TB]), m.sbuf("std", [P, TB]), m.sbuf("rr", [P, TB])
        x2 = m.sbuf("x2", [P, TB, P])
        x2T = m.sbuf("x2T", [P, TILE])
        xT = m.sbuf("xT", [P, 2, TILE], F16)
        V = m.sbuf("V", [P, TB, HEADS, HD + 1])
        rope1 = [m.sbuf(f"rope1{w}", [P, TILE]) for w in range(2)]
        rope2 = [m.sbuf(f"rope2{w}", [P, TILE]) for w in range(2)]
        rot = [m.sbuf(f"rot{w}", [P, TILE]) for w in range(2)]
        qk = [[m.sbuf(f"qk{w}_{k}", [P, 2, TILE], F16) for k in range(2)] for w in range(2)]
        nmax = [m.sbuf(f"nmax{k}", [P, 3]) for k in range(2)]
        prob = [m.sbuf(f"prob{k}", [P, 384]) for k in range(2)]
        probT = [m.sbuf(f"probT{k}", [P, 384]) for k in range(2)]
        rden = m.sbuf("rden", [P, SEQS, 4])
        ctxn = [m.sbuf(f"ctxn{k}", [P, SEQS, 2, P]) for k in range(2)]
        ctxT = m.sbuf("ctxT", [P, 2, PAIRS, TILE], F16)
        attn = m.sbuf("attn", [P, TILE])
        asq = m.sbuf("asq", [P, TILE])
        astd, arr = m.sbuf("astd", [P, TB]), m.sbuf("arr", [P, TB])
        diag = m.sbuf("diag", [P, TILE])
        an = m.sbuf("an", [P, TILE])
        rest = m.sbuf("rest", [P, TILE])

        (pa, pb), sc, pt, cx = m.banks("proj", 2), m.banks("score", 2), m.banks("probT", 2), m.banks("ctx", 2)

        S = m.count
        const_in, stage_in, stage_hi, w_ready = S("const_in"), S("stage_in"), S("stage_hi"), S("w_ready")
        ready, table_done = S("ready"), S("table_done")
        tab, act_tab = S("tab"), S("act_tab")
        x_loaded = S("x_loaded", 16)
        sq_done, ss_done, std_done, rr_done, x2_done = S("sq_done"), S("ss_done"), S("std_done"), S("rr_done"), S("x2_done", 1, 1)
        x2_ps, x2T_done, xT_hi, xT_lo = S("x2_ps"), S("x2T_done"), S("xT_hi"), S("xT_lo")
        v_ps, v_out = S("v_ps", 2 * TB), S("v_out", 2 * TB)
        a_ps, a_rope = S("a_ps", 2 * PAIRS), S("a_rope", 2 * PAIRS)
        b_ps, b_rope = S("b_ps", 2 * PAIRS), S("b_rope", 2 * PAIRS)
        rot_done, qk_hi, qk_lo = S("rot_done", 2 * PAIRS, 2), S("qk_hi", 2 * PAIRS, 2), S("qk_lo", 2 * PAIRS)
        sc_ps, max_done, nmax_done, exp_done = S("sc_ps", UNITS), S("max_done", UNITS), S("nmax_done", UNITS), S("exp_done", UNITS)
        pt_ps = S("pt_ps", UNITS)
        pt_even, pt_odd = S("pt_even", UNITS // 2), S("pt_odd", UNITS // 2)
        pv_done, rden_done, norm_done = S("pv_done", UNITS), S("rden_done", UNITS // 2), S("norm_done", UNITS // 2)
        ct_ps, ct_hi, ct_lo = S("ct_ps", PAIRS), S("ct_hi", PAIRS), S("ct_lo", PAIRS)
        o_ps, attn_half, attn_done, asq_done = S("o_ps"), S("attn_half"), S("attn_done"), S("asq_done")
        asum_ps, astd_done, arr_done, diag_done = S("asum_ps"), S("astd_done"), S("arr_done"), S("diag_done")
        bc_ps, an_done, rest_done, stored = S("bc_ps"), S("an_done"), S("rest_done"), S("stored", 32, 32)
        order = S("order")

        block = ctx.enter_context(nc.Block())
        consts = [(eye32, eye), (future_m, future), (gam1, gamma1.rearrange("(p a) -> p a", a=1)),
                  (gam2, gamma2.rearrange("(p a) -> p a", a=1)), (ob, o_b.rearrange("(p a) -> p a", a=1)),
                  (vb, v_b), (qkb, qk_b), (th, theta), (sign, half_sign),
                  (pos, position.to_broadcast([P, SEQ]))]
        loads = [(qk_w[:, 0:2048], qkw[:, :, 0:2048]), (qk_w[:, 2048:4096], qkw[:, :, 2048:4096]),
                 (v_w, vw[:]), (o_w.rearrange("(j p) n -> p j n", p=P), ow[:])]

        @block.sync
        def _(sp):
            for dst, src in consts:
                sp.dma_start(dst[:], src).then_inc(const_in.handle, 16)
            for n, (src, dst) in enumerate(loads):
                if n:
                    sp.wait_ge(w_ready.handle, n)
                width = dst.shape[2]
                to = stage[:, 0:width]
                if len(src.shape) == 3:
                    to = to.rearrange("p (j n) -> p j n", j=PAIRS)
                sp.dma_start(to, src).then_inc(stage_in.handle, 16)
            sp.sem_inc(x2_done.handle, 1)
            sp.sem_inc(stored.handle, 32)
            with sp.Fori(0, turns) as i:
                sp.wait_ge(x2_done.handle, x2_done.before(i))
                sp.dma_start(xn[:], xn_v[i]).then_inc(x_loaded.handle, 16)
                sp.wait_ge(rest_done.handle, rest_done.at(i, 1))
                sp.dma_start(an_out[:, bass.ts(i, TILE)], an[:]).then_inc(stored.handle, 16)
                sp.dma_start(rest_out[:, bass.ts(i, TILE)], rest[:]).then_inc(stored.handle, 16)
            sp.wait_ge(stored.handle, 32 * (turns + 1))

        def head(w, j, s, hh, t0, t1):
            buf, a = qk[w][j % 2], s * SEQ
            return buf[hh * HD:(hh + 1) * HD, 0, a + t0:a + t1], buf[hh * HD:(hh + 1) * HD, 1, a + t0:a + t1]

        @block.tensor
        def _(te):
            pe = nc.tensor
            te.wait_ge(w_ready.handle, len(loads))
            te.wait_ge(ready.handle, 5)
            xs = (xT[:, 0, :], xT[:, 1, :])
            with te.Fori(0, turns) as i:
                te.wait_ge(x2_done.handle, x2_done.at(i, 1))
                for t in range(TB):
                    last = pe.transpose(pa[:, t * P:(t + 1) * P], x2[:, t, :], eye32[:])
                last.then_inc(x2_ps.handle, 1)
                te.wait_ge(xT_lo.handle, xT_lo.at(i, 1))
                for n in range(2 * TB):
                    t, half = n // 2, n % 2
                    bank = (pt + cx)[n % 4]
                    if n >= 4:
                        te.wait_ge(v_out.handle, v_out.at(i, n - 3))
                    split_product(pe, bank[:], (xT[:, 0, t * P:(t + 1) * P], xT[:, 1, t * P:(t + 1) * P]),
                                  (vw[:, 0, half * 512:(half + 1) * 512], vw[:, 1, half * 512:(half + 1) * 512]))\
                        .then_inc(v_ps.handle, 1)

                def project(w, j):
                    n = 2 * j + w
                    for kind, bank, done, read in ((2 * w, pa, a_ps, a_rope), (2 * w + 1, pb, b_ps, b_rope)):
                        if n:
                            te.wait_ge(read.handle, read.at(i, n))
                        at = kind * 1024 + j * P
                        split_product(pe, bank[:], (qkw[:, 0, at:at + P], qkw[:, 1, at:at + P]), xs)\
                            .then_inc(done.handle, 1)

                def scores(u):
                    j, s, hh = u // 4, u // 2 % 2, u % 2
                    bank = sc[u % 2]
                    if u % 4 == 0:
                        te.wait_ge(qk_lo.handle, qk_lo.at(i, 2 * j + 2))
                        te.wait_ge(qk_hi.handle, qk_hi.at(i, 2 * j + 2))
                    if u >= 2:
                        te.wait_ge(exp_done.handle, exp_done.at(i, u - 1))
                    split_product(pe, bank[:, 0:128], head(0, j, s, hh, 0, 128), head(1, j, s, hh, 0, 128), stop=False)
                    pe.matmul(bank[:, 0:128], eyeb[:], futureb[:], start=False, stop=True, skip_group_check=True)
                    split_product(pe, bank[:, 128:384], head(0, j, s, hh, 128, 256), head(1, j, s, hh, 0, 256), stop=False)
                    pe.matmul(bank[:, 256:384], eyeb[:], futureb[:], start=False, stop=True, skip_group_check=True)\
                        .then_inc(sc_ps.handle, 1)

                def turn_over(u):
                    te.wait_ge(exp_done.handle, exp_done.at(i, u + 1))
                    if u >= 2:
                        read = (pt_even, pt_odd)[u % 2]
                        te.wait_ge(read.handle, read.at(i, u // 2))
                    if u < 2:
                        te.wait_ge(v_out.handle, v_out.at(i, 2 * TB))
                    for k in range(3):
                        last = pe.transpose(pt[u % 2][:, k * P:(k + 1) * P], prob[u % 2][:, k * P:(k + 1) * P], eye32[:])
                    last.then_inc(pt_ps.handle, 1)

                def mix(u):
                    j, s, hh = u // 4, u // 2 % 2, u % 2
                    h = 2 * j + hh
                    read = (pt_even, pt_odd)[u % 2]
                    te.wait_ge(read.handle, read.at(i, u // 2 + 1))
                    if u % 2 == 0 and j:
                        te.wait_ge(norm_done.handle, norm_done.at(i, 2 * j + s - 1))
                    W = HD + 1
                    o0, o1 = (cx[s][:, (2 * hh + b) * W:(2 * hh + b + 1) * W] for b in range(2))
                    pe.matmul(o0, probT[u % 2][:, 0:128], V[:, 2 * s, h, :], start=True, stop=True, skip_group_check=True)
                    pe.matmul(o1, probT[u % 2][:, 128:256], V[:, 2 * s, h, :], start=True, stop=False, skip_group_check=True)
                    pe.matmul(o1, probT[u % 2][:, 256:384], V[:, 2 * s + 1, h, :], start=False, stop=True,
                              skip_group_check=True).then_inc(pv_done.handle, 1)

                def turn_ctx(j):
                    te.wait_ge(norm_done.handle, norm_done.at(i, 2 * j + 2))
                    te.wait_ge(a_rope.handle, a_rope.at(i, min(2 * PAIRS, 2 * (j + 3) + 1)))
                    for s in range(SEQS):
                        for b in range(2):
                            at = (2 * s + b) * P
                            last = pe.transpose(pa[:, at:at + P], ctxn[j % 2][:, s, b, :], eye32[:])
                    last.then_inc(ct_ps.handle, 1)

                project(0, 0)
                project(1, 0)
                for u in range(UNITS + 12):
                    j = u // 4
                    if u < UNITS:
                        scores(u)
                    if 2 <= u < UNITS + 2:
                        turn_over(u - 2)
                    if 3 <= u < UNITS + 3:
                        mix(u - 3)
                    if u % 4 == 0 and j + 1 < PAIRS:
                        if j >= 3:
                            te.wait_ge(ct_lo.handle, ct_lo.at(i, j - 2))
                        project(0, j + 1)
                    if u % 4 == 1 and 0 <= j - 2 < PAIRS:
                        if j - 2 >= 6:
                            te.wait_ge(ct_lo.handle, ct_lo.at(i, j - 2))
                        turn_ctx(j - 2)
                    if u % 4 == 2 and j + 1 < PAIRS:
                        if j >= 2:
                            te.wait_ge(ct_lo.handle, ct_lo.at(i, j - 1))
                        project(1, j + 1)
                te.wait_ge(ct_lo.handle, ct_lo.at(i, PAIRS))
                for j in range(PAIRS):
                    last = split_product(pe, sc[0][:], (ow[:, 0, j * P:(j + 1) * P], ow[:, 1, j * P:(j + 1) * P]),
                                         (ctxT[:, 0, j, :], ctxT[:, 1, j, :]), start=(j == 0), stop=(j == PAIRS - 1))
                last.then_inc(o_ps.handle, 1)
                te.wait_ge(asq_done.handle, asq_done.at(i, 1))
                for t in range(TB):
                    last = pe.matmul(sc[1][:, t:t + 1], asq[:, t * P:(t + 1) * P], ones[:, 0:1], start=True, stop=True)
                last.then_inc(asum_ps.handle, 1)
                te.wait_ge(diag_done.handle, diag_done.at(i, 1))
                pe.matmul(pt[0][:], ones[:], diag[:], start=True, stop=True).then_inc(bc_ps.handle, 1)
                te.wait_ge(an_done.handle, an_done.at(i, 1))

        @block.scalar
        def _(ac):
            act = nc.scalar.activation
            ac.wait_ge(const_in.handle, 16 * len(consts))
            act(eyeb[:], eye32[:], ACT.Copy).then_inc(ready.handle, 1)
            act(futureb[:], future_m[:], ACT.Copy).then_inc(ready.handle, 1)
            for n, (src, dst) in enumerate(loads):
                ac.wait_ge(stage_in.handle, 16 * (n + 1))
                act(dst[:, 0, :], stage[:, 0:dst.shape[2]], ACT.Copy).then_inc(stage_hi.handle, 1)
            ac.wait_ge(tab.handle, 10)
            act(ang[2][:], ang[2][:], ACT.Sin).then_inc(act_tab.handle, 1)
            act(ang[3][:], ang[3][:], ACT.Sin).then_inc(act_tab.handle, 1)
            ac.wait_ge(ready.handle, 5)

            def rope_high(n):
                ac.wait_ge(rot_done.handle, rot_done.at(i, n + 1))
                if n >= 4:
                    ac.wait_ge(sc_ps.handle, sc_ps.at(i, 4 * (n // 2 - 1)))
                act(qk[n % 2][n // 2 % 2][:, 0, :], rot[n % 2][:], ACT.Copy).then_inc(qk_hi.handle, 1)

            with ac.Fori(0, turns) as i:
                ac.wait_ge(x_loaded.handle, x_loaded.at(i, 16))
                act(sq[:], xn[:].rearrange("p t d -> p (t d)"), ACT.Square).then_inc(sq_done.handle, 1)
                ac.wait_ge(ss_done.handle, ss_done.at(i, 1))
                act(std[:], ss[:], ACT.Sqrt, bias=eps[:], scale=1.0 / P).then_inc(std_done.handle, 1)
                ac.wait_ge(x2T_done.handle, x2T_done.at(i, 1))
                act(xT[:, 0, :], x2T[:], ACT.Copy).then_inc(xT_hi.handle, 1)
                for n in range(2 * TB):
                    t, half = n // 2, n % 2
                    ac.wait_ge(v_ps.handle, v_ps.at(i, n + 1))
                    act(V[:, t, half * 8:(half + 1) * 8, 0:HD], (pt + cx)[n % 4][:].rearrange("p (h d) -> p h d", d=HD),
                        ACT.Copy).then_inc(v_out.handle, 1)
                rope_high(0)
                rope_high(1)
                for u in range(UNITS + 12):
                    j = u // 4
                    if u < UNITS:
                        ac.wait_ge(nmax_done.handle, nmax_done.at(i, u + 1))
                        if u >= 2:
                            ac.wait_ge(pt_ps.handle, pt_ps.at(i, u - 1))
                        act(prob[u % 2][:, 0:128], sc[u % 2][:, 0:128], ACT.Exp, bias=nmax[u % 2][:, 0:1])
                        act(prob[u % 2][:, 128:384], sc[u % 2][:, 128:384], ACT.Exp, bias=nmax[u % 2][:, 1:2])\
                            .then_inc(exp_done.handle, 1)
                    if 2 <= u < UNITS + 2 and u % 2:
                        ac.wait_ge(pt_ps.handle, pt_ps.at(i, u - 1))
                        if u >= 4:
                            ac.wait_ge(pv_done.handle, pv_done.at(i, u - 3))
                        act(probT[1][:], pt[1][:, 0:384], ACT.Copy).then_inc(pt_odd.handle, 1)
                    if u % 4 == 1 and j + 1 < PAIRS:
                        rope_high(2 * (j + 1))
                    if u % 4 == 3 and j + 1 < PAIRS:
                        rope_high(2 * (j + 1) + 1)
                    if u % 4 == 1 and 0 <= j - 2 < PAIRS:
                        ac.wait_ge(ct_ps.handle, ct_ps.at(i, j - 1))
                        act(ctxT[:, 0, j - 2, :], pa[:], ACT.Identity, bias=vb[:, j - 2:j - 1]).then_inc(ct_hi.handle, 1)
                ac.wait_ge(attn_done.handle, attn_done.at(i, 1))
                act(asq[:], attn[:], ACT.Square).then_inc(asq_done.handle, 1)
                ac.wait_ge(asum_ps.handle, asum_ps.at(i, 1))
                act(astd[:], sc[1][:, 0:TB], ACT.Sqrt, bias=eps[:], scale=1.0 / P).then_inc(astd_done.handle, 1)

        @block.vector
        def _(ve):
            vec = nc.vector
            vec.memset(eps[:], EPS).then_inc(ready.handle, 1)
            vec.memset(ones[:], 1.0).then_inc(ready.handle, 1)
            vec.memset(V[:, :, :, HD:HD + 1], 1.0).then_inc(ready.handle, 1)
            for n, (src, dst) in enumerate(loads):
                ve.wait_ge(stage_hi.handle, n + 1)
                vec.tensor_tensor(dst[:, 1, :], stage[:, 0:dst.shape[2]], dst[:, 0, :], ALU.subtract)\
                   .then_inc(w_ready.handle, 1)
            ve.wait_ge(const_in.handle, 16 * len(consts))

            def step(ins):
                step.n += 1
                ins.then_inc(tab.handle, 1)
                ve.wait_ge(tab.handle, step.n)

            step.n = 0
            turns_of, red, sine, cosine = ang
            step(vec.tensor_scalar(red[:], pos[:], th[:], None, ALU.mult))
            step(vec.tensor_scalar(turns_of[:], red[:], 1.0 / TWO_PI, None, ALU.mult))
            step(vec.tensor_scalar(turns_of[:], turns_of[:], ROUND, None, ALU.add))
            step(vec.tensor_scalar(turns_of[:], turns_of[:], -ROUND, None, ALU.add))
            for part in (C1, C2, C3):
                step(vec.scalar_tensor_tensor(out=red[:], in0=turns_of[:], scalar=-part, in1=red[:], op0=ALU.mult, op1=ALU.add))
            step(vec.tensor_scalar(sine[:], red[:], 3.1415925, -3.1415925, ALU.min, ALU.max))
            step(vec.scalar_tensor_tensor(out=cosine[:], in0=sine[:], scalar=-1.0, in1=sine[:], op0=ALU.mult, op1=ALU.max))
            step(vec.tensor_scalar(cosine[:], cosine[:], -1.0, TWO_PI / 4, ALU.mult, ALU.add))
            ve.wait_ge(act_tab.handle, 2)
            scale = 1.0 / HD ** 0.5
            vec.tensor_scalar(table[:, 1, 0, :], cosine[:], 1.0, None, ALU.mult).then_inc(table_done.handle, 1)
            vec.tensor_scalar(table[:, 0, 0, :], cosine[:], scale, None, ALU.mult).then_inc(table_done.handle, 1)
            vec.tensor_scalar(table[:, 1, 1, :], sine[:], sign[:], None, ALU.mult).then_inc(table_done.handle, 1)
            vec.tensor_scalar(table[:, 0, 1, :], sine[:], sign[:], scale, ALU.mult, ALU.mult).then_inc(table_done.handle, 1)
            ve.wait_ge(table_done.handle, 4)

            with ve.Fori(0, turns) as i:
                ve.wait_ge(sq_done.handle, sq_done.at(i, 1))
                vec.tensor_reduce(ss[:], sq[:].rearrange("p (t d) -> p t d", t=TB), AX, ALU.add).then_inc(ss_done.handle, 1)
                ve.wait_ge(std_done.handle, std_done.at(i, 1))
                vec.reciprocal(rr[:], std[:]).then_inc(rr_done.handle, 1)
                ve.wait_ge(rr_done.handle, rr_done.at(i, 1))
                vec.tensor_tensor(x2[:], xn[:], over(rr[:], P, 2), ALU.mult).then_inc(x2_done.handle, 1)
                ve.wait_ge(x2_ps.handle, x2_ps.at(i, 1))
                vec.tensor_scalar(x2T[:], pa[:], gam1[:], None, ALU.mult).then_inc(x2T_done.handle, 1)
                ve.wait_ge(xT_hi.handle, xT_hi.at(i, 1))
                vec.tensor_tensor(xT[:, 1, :], x2T[:], xT[:, 0, :], ALU.subtract).then_inc(xT_lo.handle, 1)

                def rope(n):
                    w, j = n % 2, n // 2
                    for kind, bank, out, got, done in ((0, pa, rope1, a_ps, a_rope), (1, pb, rope2, b_ps, b_rope)):
                        ve.wait_ge(got.handle, got.at(i, n + 1))
                        if kind == 0:
                            ve.wait_ge(rot_done.handle, rot_done.at(i, n - 1))
                        vec.scalar_tensor_tensor(out=out[w][:].rearrange("p (s n) -> p s n", s=SEQS),
                                                 in0=bank[:].rearrange("p (s n) -> p s n", s=SEQS),
                                                 scalar=qkb[:, 2 * w + kind, j:j + 1], in1=over(table[:, w, kind, :], SEQS),
                                                 op0=ALU.add, op1=ALU.mult).then_inc(done.handle, 1)

                rope(0)
                rope(1)
                for u in range(UNITS + 12):
                    j = u // 4
                    if u < UNITS:
                        b = u % 2
                        ve.wait_ge(sc_ps.handle, sc_ps.at(i, u + 1))
                        if u >= 2:
                            ve.wait_ge(exp_done.handle, exp_done.at(i, u - 1))
                        vec.tensor_reduce(nmax[b][:], sc[b][:, 0:384].rearrange("p (k n) -> p k n", k=3), AX, ALU.max,
                                          negate=True).then_inc(max_done.handle, 1)
                        ve.wait_ge(max_done.handle, max_done.at(i, u + 1))
                        vec.tensor_tensor(nmax[b][:, 1:2], nmax[b][:, 1:2], nmax[b][:, 2:3], ALU.min)\
                           .then_inc(nmax_done.handle, 1)
                    if 2 <= u < UNITS + 2 and u % 2 == 0:
                        ve.wait_ge(pt_ps.handle, pt_ps.at(i, u - 1))
                        if u >= 4:
                            ve.wait_ge(pv_done.handle, pv_done.at(i, u - 3))
                        vec.tensor_copy(probT[0][:], pt[0][:, 0:384]).then_inc(pt_even.handle, 1)
                    if u % 4 == 0 and j + 1 < PAIRS:
                        rope(2 * (j + 1))
                    if u % 4 == 2 and 0 <= j - 2 < PAIRS:
                        ve.wait_ge(ct_hi.handle, ct_hi.at(i, j - 1))
                        vec.scalar_tensor_tensor(out=ctxT[:, 1, j - 2, :], in0=pa[:], scalar=vb[:, j - 2:j - 1],
                                                 in1=ctxT[:, 0, j - 2, :], op0=ALU.add, op1=ALU.subtract)\
                           .then_inc(ct_lo.handle, 1)
                    if u % 4 == 2 and j + 1 < PAIRS:
                        rope(2 * (j + 1) + 1)
                    if u >= 4 and u % 2 == 1 and u - 4 < UNITS:
                        k = (u - 5) // 2
                        jj, s = k // 2, k % 2
                        ve.wait_ge(pv_done.handle, pv_done.at(i, 2 * k + 2))
                        got = cx[s][:, 0:4 * (HD + 1)].rearrange("p (h b d) -> p h b d", h=2, b=2)
                        vec.reciprocal(rden[:, s, :].rearrange("p (h b a) -> p h b a", h=2, a=1), got[:, :, :, HD:HD + 1]).then_inc(rden_done.handle, 1)
                        ve.wait_ge(rden_done.handle, rden_done.at(i, k + 1))
                        if jj >= 2 and s == 0:
                            ve.wait_ge(ct_ps.handle, ct_ps.at(i, jj - 1))
                        vec.tensor_tensor(ctxn[jj % 2][:, s, :, :].rearrange("p b (h d) -> p h b d", h=2), got[:, :, :, 0:HD],
                                          over(rden[:, s, :].rearrange("p (h b) -> p h b", h=2), HD, 3), ALU.mult)\
                           .then_inc(norm_done.handle, 1)
                ve.wait_ge(o_ps.handle, o_ps.at(i, 1))
                vec.scalar_tensor_tensor(out=attn[:], in0=sc[0][:], scalar=ob[:], in1=x2T[:], op0=ALU.add, op1=ALU.add)\
                   .then_inc(attn_done.handle, 1)
                ve.wait_ge(astd_done.handle, astd_done.at(i, 1))
                vec.reciprocal(arr[:], astd[:]).then_inc(arr_done.handle, 1)
                ve.wait_ge(arr_done.handle, arr_done.at(i, 1))
                vec.tensor_tensor(diag[:].rearrange("p (t n) -> p t n", t=TB), over(eye32[:], TB), over(arr[:], P, 2), ALU.mult)\
                   .then_inc(diag_done.handle, 1)
                ve.wait_ge(bc_ps.handle, bc_ps.at(i, 1))
                ve.wait_ge(stored.handle, stored.before(i))
                vec.scalar_tensor_tensor(out=an[:], in0=attn[:], scalar=gam2[:], in1=pt[0][:], op0=ALU.mult, op1=ALU.mult)\
                   .then_inc(an_done.handle, 1)
                ve.wait_ge(an_done.handle, an_done.at(i, 1))
                vec.tensor_tensor(rest[:], an[:], attn[:], ALU.add).then_inc(rest_done.handle, 1)

        @block.gpsimd
        def _(po):
            po.sem_inc(rot_done.handle, 2)
            po.sem_inc(qk_hi.handle, 2)
            with po.Fori(0, turns) as i:
                for n in range(2 * PAIRS):
                    w, j = n % 2, n // 2
                    po.wait_ge(b_rope.handle, b_rope.at(i, n + 1))
                    po.wait_ge(qk_hi.handle, qk_hi.at(i, n - 1))
                    if n >= 2:
                        po.wait_ge(qk_lo.handle, qk_lo.at(i, n - 1))
                    nc.gpsimd.tensor_tensor(rot[w][:], rope1[w][:], rope2[w][:], ALU.add).then_inc(rot_done.handle, 1)
                    po.wait_ge(qk_hi.handle, qk_hi.at(i, n + 1))
                    nc.gpsimd.tensor_tensor(qk[w][j % 2][:, 1, :], rot[w][:], qk[w][j % 2][:, 0, :], ALU.subtract)\
                        .then_inc(qk_lo.handle, 1)


def experts_phase(nc, an_in, rest_in, s_in, x_in, router_w, router_b, w1, b1, w2, b2, spread, number, eye,
                  x1_out, turns):
    E, ER, TOP = 32, 31, 3
    LAG = 3
    HB, TBUF = 3, 4
    HEAD, TAIL = 6, 2
    SLOTS = E + LAG
    x_v = x_in.rearrange("(n t p) d -> n p t d", t=TB, p=P)
    x1_v = x1_out.rearrange("(n t p) d -> n p t d", t=TB, p=P)

    with ExitStack() as ctx:
        m = Memory(nc, ctx, "moe")
        eye32, eye16 = m.sbuf("eye32", [P, P]), m.sbuf("eye16", [P, P], F16)
        stage = m.sbuf("w_stage", [P, E * P])
        w1_s, w2_s = m.sbuf("w1", [P, 2, E * P], F16), m.sbuf("w2", [P, 2, E * P], F16)
        small = m.sbuf("small", [P, P + ER])
        small16 = m.sbuf("small16", [P, 2, P + ER], F16)
        b1_s = m.sbuf("b1", [P, E])
        rb = m.sbuf("rb", [P, ER])
        num = m.sbuf("num", [P, ER])
        spread_s = m.sbuf("spread", [64, E * P], F16)

        an_f = m.sbuf("an_f", [P, TILE])
        an_next, an = m.sbuf("an_next", [P, 2, TILE], F16), m.sbuf("an", [P, 2, TILE], F16)
        lg, ex, pr = m.sbuf("lg", [P, TB, ER]), m.sbuf("ex", [P, TB, ER]), m.sbuf("pr", [P, TB, ER])
        mx, sm = m.sbuf("mx", [P, TB]), m.sbuf("sm", [P, TB])
        top, top_i, top_f = m.sbuf("top", [P, TB, 8]), m.sbuf("top_i", [P, TB, 8], mybir.dt.uint32), m.sbuf("top_f", [P, TB, 8])
        hit, chosen = m.sbuf("hit", [P, TB, TOP, ER]), m.sbuf("chosen", [P, TB, ER])
        gates = m.sbuf("gates", [P, TB, ER])
        gate16 = m.sbuf("gate16", [P, TB, 64], F16)
        gates_next, gatesT = m.sbuf("gates_next", [64, TILE], F16), m.sbuf("gatesT", [64, TILE], F16)
        h32 = [m.sbuf(f"h32_{k}", [P, TILE]) for k in range(2)]
        t32 = [m.sbuf(f"t32_{k}", [P, TILE]) for k in range(3)]
        t16 = [m.sbuf(f"t16_{k}", [P, 2, TILE], F16) for k in range(TBUF)]
        rest, sT, x_s = m.sbuf("rest", [P, TILE]), m.sbuf("sT", [P, TILE]), m.sbuf("x_s", [P, TB, P])
        y, sl, ys = m.sbuf("y", [P, TILE]), m.sbuf("sl", [P, TILE]), m.sbuf("ys", [P, TILE])
        x1 = m.sbuf("x1", [P, TB, P])

        H, G, (Y,), (m0, m1) = m.banks("h", HB), m.banks("g", 2), m.banks("y", 1), m.banks("misc", 2)

        S = m.count
        const_in, stage_in, stage_hi, w_ready, ready = S("const_in"), S("stage_in"), S("stage_hi"), S("w_ready"), S("ready")
        an_loaded, an_hi, an_lo = S("an_loaded", 16), S("an_hi"), S("an_lo", 1, 1)
        lg_ps, lg_done, ex_done = S("lg_ps"), S("lg_done"), S("ex_done")
        CHAIN = 13
        chain = S("chain", CHAIN)
        gate_split, gT_ps, gT_copied = S("gate_split"), S("gT_ps"), S("gT_copied")
        moved = S("moved")
        h_ps, gelu_done, g_ps, t_done = S("h_ps", E), S("gelu_done", E), S("g_ps", E), S("t_done", E)
        t_hi, t_lo, y_step = S("t_hi", E), S("t_lo", E), S("y_step", E)
        rest_loaded, s_loaded, x_loaded = S("rest_loaded", 16), S("s_loaded", 16), S("x_loaded", 16)
        y_done, sl_done, ys_done = S("y_done", 1, 1), S("sl_done"), S("ys_done", 1, 1)
        yT_ps, x1_done, x1_stored = S("yT_ps"), S("x1_done", 1, 1), S("x1_stored", 16, 16)
        order = S("order")

        block = ctx.enter_context(nc.Block())
        consts = [(eye32, eye), (small[0:64, 0:P], b2), (small[:, P:], router_w), (b1_s, b1),
                  (rb, router_b.rearrange("(a e) -> a e", a=1).to_broadcast([P, ER])), (num, number.to_broadcast([P, ER])),
                  (spread_s, spread)]
        loads = [(w1, w1_s), (w2, w2_s)]
        LAST = turns - 1

        @block.sync
        def _(sp):
            for dst, src in consts:
                sp.dma_start(dst[:], src).then_inc(const_in.handle, 16)
            for n, (src, dst) in enumerate(loads):
                if n:
                    sp.wait_ge(w_ready.handle, n)
                sp.dma_start(stage[:].rearrange("p (e h) -> p e h", e=E), src.rearrange("e p h -> p e h"))\
                    .then_inc(stage_in.handle, 16)
            sp.sem_inc(an_lo.handle, 1)
            sp.sem_inc(y_done.handle, 1)
            sp.sem_inc(ys_done.handle, 1)
            sp.sem_inc(x1_done.handle, 1)
            sp.sem_inc(x1_stored.handle, 16)

            def load_an(k):
                sp.wait_ge(an_lo.handle, an_lo.before(k))
                sp.dma_start(an_f[:], an_in[:, bass.ts(k, TILE)]).then_inc(an_loaded.handle, 16)

            def load_rest(k):
                sp.wait_ge(y_done.handle, y_done.before(k))
                sp.dma_start(rest[:], rest_in[:, bass.ts(k, TILE)]).then_inc(rest_loaded.handle, 16)
                sp.wait_ge(ys_done.handle, ys_done.before(k))
                sp.dma_start(sT[:], s_in[:, bass.ts(k, TILE)]).then_inc(s_loaded.handle, 16)
                sp.wait_ge(x1_done.handle, x1_done.before(k))
                sp.dma_start(x_s[:], x_v[k]).then_inc(x_loaded.handle, 16)

            def store(k):
                sp.wait_ge(x1_done.handle, x1_done.at(k, 1))
                sp.dma_start(x1_v[k], x1[:]).then_inc(x1_stored.handle, 16)

            load_an(0)
            load_rest(0)
            load_an(1)
            with sp.Fori(1, LAST) as i:
                load_an(i + 1)
                store(i - 1)
                load_rest(i)
            store(LAST - 1)
            load_rest(LAST)
            store(LAST)
            sp.wait_ge(x1_stored.handle, 16 * (turns + 1))

        @block.tensor
        def _(te):
            pe = nc.tensor
            te.wait_ge(w_ready.handle, 2)
            te.wait_ge(ready.handle, 5)

            def logits(k):
                te.wait_ge(an_lo.handle, an_lo.at(k, 1))
                te.wait_ge(an_hi.handle, an_hi.at(k, 1))
                for t in range(TB):
                    last = split_product(pe, m0[:, t * 32:t * 32 + ER],
                                         (an_next[:, 0, t * P:(t + 1) * P], an_next[:, 1, t * P:(t + 1) * P]),
                                         (small16[:, 0, P:], small16[:, 1, P:]))
                last.then_inc(lg_ps.handle, 1)

            def turn_gates(k):
                te.wait_ge(gate_split.handle, gate_split.at(k, 1))
                te.sem_inc(order.handle, 1)
                for t in range(TB):
                    last = pe.transpose(m0[0:64, :].bitcast(F16)[:, t * P:(t + 1) * P], gate16[:, t, :], eye16[:])
                last.then_inc(gT_ps.handle, 1)

            def turn_y(k):
                te.wait_ge(ys_done.handle, ys_done.at(k, 1))
                for t in range(TB):
                    last = pe.transpose(m1[:, t * P:(t + 1) * P], ys[:, t * P:(t + 1) * P], eye32[:])
                last.then_inc(yT_ps.handle, 1)

            def body(i, ahead, behind):
                te.wait_ge(moved.handle, moved.at(i, 1))
                for e in range(SLOTS):
                    if e < E:
                        if e >= HB:
                            te.wait_ge(gelu_done.handle, gelu_done.at(i, e - HB + 1))
                        split_product(pe, H[e % HB][:], (w1_s[:, 0, e * P:(e + 1) * P], w1_s[:, 1, e * P:(e + 1) * P]),
                                      (an[:, 0, :], an[:, 1, :])).then_inc(h_ps.handle, 1)
                        if e >= 2:
                            te.wait_ge(t_done.handle, t_done.at(i, e - 1))
                        pe.matmul(G[e % 2][:], spread_s[:, e * P:(e + 1) * P], gatesT[:], start=True, stop=True)\
                            .then_inc(g_ps.handle, 1)
                    if e == LAG - 1:
                        te.wait_ge(y_done.handle, y_done.before(i))
                        pe.matmul(Y[:], small16[0:64, 1, 0:P], gatesT[:], start=True, stop=False, skip_group_check=True)
                        pe.matmul(Y[:], small16[0:64, 0, 0:P], gatesT[:], start=False, stop=False, skip_group_check=True)
                    if e >= LAG:
                        k = e - LAG
                        te.wait_ge(t_hi.handle, t_hi.at(i, k + 1))
                        te.wait_ge(t_lo.handle, t_lo.at(i, k + 1))
                        split_product(pe, Y[:], (w2_s[:, 0, k * P:(k + 1) * P], w2_s[:, 1, k * P:(k + 1) * P]),
                                      (t16[k % TBUF][:, 0, :], t16[k % TBUF][:, 1, :]), start=False, stop=(k == E - 1))\
                            .then_inc(y_step.handle, 1)
                    if behind and e == TAIL + 2:
                        turn_y(i - 1)
                    if ahead and e == HEAD:
                        logits(i + 1)
                    if ahead and e == HEAD + 14:
                        turn_gates(i + 1)

            logits(0)
            turn_gates(0)
            body(0, True, False)
            with te.Fori(1, LAST) as i:
                body(i, True, True)
            body(LAST, False, True)
            turn_y(LAST)

        @block.scalar
        def _(ac):
            act = nc.scalar.activation
            ac.wait_ge(const_in.handle, 16 * len(consts))
            act(eye16[:], eye32[:], ACT.Copy).then_inc(ready.handle, 1)
            act(small16[:, 0, P:], small[:, P:], ACT.Copy)
            act(small16[0:64, 0, 0:P], small[0:64, 0:P], ACT.Copy).then_inc(ready.handle, 1)
            for n, (src, dst) in enumerate(loads):
                ac.wait_ge(stage_in.handle, 16 * (n + 1))
                act(dst[:, 0, :], stage[:], ACT.Copy).then_inc(stage_hi.handle, 1)

            def high(k):
                ac.wait_ge(an_loaded.handle, an_loaded.at(k, 16))
                act(an_next[:, 0, :], an_f[:], ACT.Copy).then_inc(an_hi.handle, 1)

            def exps(k):
                ac.wait_ge(lg_done.handle, lg_done.at(k, 1))
                act(ex[:], lg[:], ACT.Exp).then_inc(ex_done.handle, 1)

            def copy_gates(k):
                ac.wait_ge(gT_ps.handle, gT_ps.at(k, 1))
                act(gates_next[:], m0[0:64, :].bitcast(F16)[:, 0:TILE], ACT.Copy).then_inc(gT_copied.handle, 1)

            def gate_y(k):
                ac.wait_ge(y_done.handle, y_done.at(k, 1))
                act(sl[:], y[:], ACT.Silu).then_inc(sl_done.handle, 1)

            def body(i, ahead, behind):
                for e in range(E):
                    if behind and e == 0:
                        gate_y(i - 1)
                    ac.wait_ge(h_ps.handle, h_ps.at(i, e + 1))
                    if e >= 2:
                        ac.wait_ge(t_done.handle, t_done.at(i, e - 1))
                    act(h32[e % 2][:], H[e % HB][:], ACT.Gelu, bias=b1_s[:, e:e + 1]).then_inc(gelu_done.handle, 1)
                    if ahead and e == HEAD - 4:
                        ac.wait_ge(moved.handle, moved.at(i, 1))
                        high(i + 1)
                    if ahead and e == HEAD + 3:
                        exps(i + 1)
                    if ahead and e == HEAD + 16:
                        copy_gates(i + 1)

            high(0)
            exps(0)
            copy_gates(0)
            body(0, True, False)
            with ac.Fori(1, LAST) as i:
                body(i, True, True)
            body(LAST, False, True)
            gate_y(LAST)

        @block.vector
        def _(ve):
            vec = nc.vector
            ve.wait_ge(const_in.handle, 16 * len(consts))
            vec.memset(gate16[:, :, ER:ER + 1], 1.0).then_inc(ready.handle, 1)
            vec.memset(gate16[:, :, 63:64], 0.0).then_inc(ready.handle, 1)
            ve.wait_ge(ready.handle, 4)
            vec.tensor_tensor(small16[:, 1, P:], small[:, P:], small16[:, 0, P:], ALU.subtract)
            vec.tensor_tensor(small16[0:64, 1, 0:P], small[0:64, 0:P], small16[0:64, 0, 0:P], ALU.subtract)\
               .then_inc(ready.handle, 1)
            for n, (src, dst) in enumerate(loads):
                ve.wait_ge(stage_hi.handle, n + 1)
                vec.tensor_tensor(dst[:, 1, :], stage[:], dst[:, 0, :], ALU.subtract).then_inc(w_ready.handle, 1)

            def router(k):
                steps = [0]

                def step(ins):
                    steps[0] += 1
                    ins.then_inc(chain.handle, 1)
                    ve.wait_ge(chain.handle, chain.at(k, steps[0]))

                ve.wait_ge(lg_ps.handle, lg_ps.at(k, 1))
                step(vec.tensor_tensor(lg[:], m0[:, 0:TB * 32].rearrange("p (t e) -> p t e", t=TB)[:, :, 0:ER],
                                       over(rb[:], TB), ALU.add))
                step(vec.tensor_reduce(mx[:], lg[:], AX, ALU.max))
                vec.tensor_tensor(lg[:], lg[:], over(mx[:], ER, 2), ALU.subtract).then_inc(lg_done.handle, 1)
                yield
                ve.wait_ge(ex_done.handle, ex_done.at(k, 1))
                step(vec.tensor_reduce(sm[:], ex[:], AX, ALU.add))
                step(vec.reciprocal(sm[:], sm[:]))
                step(vec.tensor_tensor(pr[:], ex[:], over(sm[:], ER, 2), ALU.mult))
                yield
                ve.sem_inc(order.handle, 1)
                for t in range(TB):
                    last = vec.max(top[:, t, :], pr[:, t, :])
                step(last)
                ve.sem_inc(order.handle, 1)
                yield
                for t in range(TB):
                    last = vec.max_index(top_i[:, t, :], top[:, t, :], pr[:, t, :])
                step(last)
                yield
                step(vec.tensor_copy(top_f[:], top_i[:]))
                step(vec.tensor_tensor(hit[:], over(over(num[:], TOP), TB), over(top_f[:, :, 0:TOP], ER, 3), ALU.is_equal))
                yield
                step(vec.tensor_reduce(chosen[:], hit[:].rearrange("p t k e -> p t e k"), AX, ALU.add))
                step(vec.tensor_tensor(gates[:], pr[:], chosen[:], ALU.mult))
                yield
                step(vec.tensor_copy(gate16[:, :, 0:ER], gates[:]))
                step(vec.tensor_tensor(chosen[:], gates[:], gate16[:, :, 0:ER], ALU.subtract))
                vec.tensor_copy(gate16[:, :, 32:32 + ER], chosen[:]).then_inc(gate_split.handle, 1)
                assert steps[0] == CHAIN
                yield

            def move(k):
                ve.wait_ge(gT_copied.handle, gT_copied.at(k, 1))
                vec.tensor_copy(an[:], an_next[:])
                vec.tensor_copy(gatesT[:], gates_next[:]).then_inc(moved.handle, 1)

            def add_x(k):
                ve.wait_ge(yT_ps.handle, yT_ps.at(k, 1))
                ve.wait_ge(x_loaded.handle, x_loaded.at(k, 16))
                ve.wait_ge(x1_stored.handle, x1_stored.before(k))
                vec.tensor_tensor(x1[:].rearrange("p t d -> p (t d)"), m1[:], x_s[:].rearrange("p t d -> p (t d)"), ALU.add)\
                   .then_inc(x1_done.handle, 1)

            def body(i, ahead, behind):
                part = router(i + 1) if ahead else iter(())
                for e in range(E + 1):
                    if e < E:
                        ve.wait_ge(g_ps.handle, g_ps.at(i, e + 1))
                        ve.wait_ge(gelu_done.handle, gelu_done.at(i, e + 1))
                        if e >= 3:
                            ve.wait_ge(t_lo.handle, t_lo.at(i, e - 2))
                        vec.tensor_tensor(t32[e % 3][:], G[e % 2][:], h32[e % 2][:], ALU.mult).then_inc(t_done.handle, 1)
                    if e:
                        ve.wait_ge(t_done.handle, t_done.at(i, e))
                        if e > TBUF:
                            ve.wait_ge(y_step.handle, y_step.at(i, e - TBUF))
                        vec.tensor_copy(t16[(e - 1) % TBUF][:, 0, :], t32[(e - 1) % 3][:]).then_inc(t_hi.handle, 1)
                    if behind and e == TAIL + 4:
                        add_x(i - 1)
                    if e >= HEAD + 2:
                        next(part, None)
                if ahead:
                    for _ in part:
                        pass
                    move(i + 1)
                ve.wait_ge(y_step.handle, y_step.at(i, E))
                ve.wait_ge(rest_loaded.handle, rest_loaded.at(i, 16))
                vec.tensor_tensor(y[:], Y[:], rest[:], ALU.add).then_inc(y_done.handle, 1)

            for _ in router(0):
                pass
            move(0)
            body(0, True, False)
            with ve.Fori(1, LAST) as i:
                body(i, True, True)
            body(LAST, False, True)
            add_x(LAST)

        @block.gpsimd
        def _(po):
            pool = nc.gpsimd

            def low(k):
                po.wait_ge(an_hi.handle, an_hi.at(k, 1))
                pool.tensor_tensor(an_next[:, 1, :], an_f[:], an_next[:, 0, :], ALU.subtract).then_inc(an_lo.handle, 1)

            def scale_s(k):
                po.wait_ge(sl_done.handle, sl_done.at(k, 1))
                po.wait_ge(s_loaded.handle, s_loaded.at(k, 16))
                pool.tensor_tensor(ys[:], sl[:], sT[:], ALU.mult).then_inc(ys_done.handle, 1)

            def body(i, ahead, behind):
                for e in range(E):
                    if behind and e == 1:
                        scale_s(i - 1)
                    po.wait_ge(t_hi.handle, t_hi.at(i, e + 1))
                    pool.tensor_tensor(t16[e % TBUF][:, 1, :], t32[e % 3][:], t16[e % TBUF][:, 0, :], ALU.subtract)\
                        .then_inc(t_lo.handle, 1)
                    if ahead and e == HEAD - 4:
                        low(i + 1)

            low(0)
            body(0, True, False)
            with po.Fori(1, LAST) as i:
                body(i, True, True)
            body(LAST, False, True)
            scale_s(LAST)


def second_layer_phase(nc, x_in, wqkvo, bo, gate_w, wg, wu, wd, spread, number, block_mask, head_mask, eye,
                       s_tmp, out, turns):
    HEADS, HD, ER, TOP = 16, 8, 8, 2
    HT = wg.shape[1] // P
    LAG, TBUF = 3, 4
    SLOTS = HT + LAG
    x_v = x_in.rearrange("(n t p) d -> n p t d", t=TB, p=P)
    out_v = out.rearrange("(n t p) d -> n p t d", t=TB, p=P)
    KX = P + HEADS

    with ExitStack() as ctx:
        m = Memory(nc, ctx, "second")
        eye32, eye16 = m.sbuf("eye32", [P, P]), m.sbuf("eye16", [P, P], F16)
        eps = m.sbuf("eps", [P, 1])
        stage = m.sbuf("w_stage", [P, HT * P])
        wg_s, wu_s, wd_s = (m.sbuf(n, [P, 2, HT * P], F16) for n in ("wg", "wu", "wd"))
        small, small16 = m.sbuf("small", [P, 4 * P + ER]), m.sbuf("small16", [P, 2, 4 * P + ER], F16)
        bo_s = m.sbuf("bo", [P, 1])
        num = m.sbuf("num", [P, ER])
        spread_s = m.sbuf("spread", [64, HT * P], F16)
        bmask, hmask = m.sbuf("bmask", [P, P]), m.sbuf("hmask", [P, HEADS])

        def w(a, b):
            return small16[:, 0, a:b], small16[:, 1, a:b]

        x_s = m.sbuf("x_s", [P, TB, P])
        stats, mean_var = m.sbuf("stats", [P, TB, 6]), m.sbuf("mean_var", [P, TB, 2])
        std, rstd = m.sbuf("std", [P, TB]), m.sbuf("rstd", [P, TB])
        xn = m.sbuf("xn", [P, TB, P])
        x_next, x_cur = m.sbuf("x_next", [P, 2, TILE], F16), m.sbuf("x_cur", [P, 2, TILE], F16)
        arg, ex = m.sbuf("arg", [P, 2 * TILE + TB * TOP]), m.sbuf("ex", [P, 2 * TILE + TB * TOP])
        pos_part = m.sbuf("pos_part", [P, 2 * TILE])
        feat = m.sbuf("feat", [P, 2 * TILE])
        v1 = m.sbuf("v1", [P, TB, P + 1])
        kvx = m.sbuf("kvx", [P, SEQS, KX])
        den = m.sbuf("den", [P, TB, HEADS])
        rden = m.sbuf("rden", [P, TB, HEADS])
        mixed = m.sbuf("mixed", [P, TB, P])
        mT = m.sbuf("mT", [P, 2, TILE], F16)
        s_next, s_cur = m.sbuf("s_next", [P, TILE]), m.sbuf("s_cur", [P, TILE])
        lg = m.sbuf("lg", [P, TB, ER])
        top, top_i, top_f = m.sbuf("top", [P, TB, 8]), m.sbuf("top_i", [P, TB, 8], mybir.dt.uint32), m.sbuf("top_f", [P, TB, 8])
        wsum = m.sbuf("wsum", [P, TB])
        share = m.sbuf("share", [P, TB, TOP])
        hit = m.sbuf("hit", [P, TB, TOP, ER])
        gates = m.sbuf("gates", [P, TB, ER])
        gate16 = m.sbuf("gate16", [P, TB, 64], F16)
        gates_next, gatesT = m.sbuf("gates_next", [64, TILE], F16), m.sbuf("gatesT", [64, TILE], F16)
        s32 = [m.sbuf(f"s32_{k}", [P, TILE]) for k in range(2)]
        a32 = [m.sbuf(f"a32_{k}", [P, TILE]) for k in range(2)]
        t32 = [m.sbuf(f"t32_{k}", [P, TILE]) for k in range(3)]
        t16 = [m.sbuf(f"t16_{k}", [P, 2, TILE], F16) for k in range(TBUF)]
        x_r, y = m.sbuf("x_r", [P, TB, P]), m.sbuf("y", [P, TB, P])
        sl, ys = m.sbuf("sl", [P, TILE]), m.sbuf("ys", [P, TILE])

        G, U, (C,), (Y,), (m0, m1) = m.banks("g", 2), m.banks("u", 2), m.banks("c", 1), m.banks("y", 1), m.banks("misc", 2)

        S = m.count
        const_in, stage_in, stage_hi, w_ready, ready = S("const_in"), S("stage_in"), S("stage_hi"), S("w_ready"), S("ready")
        x_loaded, stats_done, aggr_done, std_done, rstd_done = S("x_loaded", 16), S("stats_done"), S("aggr_done"), S("std_done"), S("rstd_done")
        xn_done, xT_ps, xT_hi, xT_lo = S("xn_done", 1, 1), S("xT_ps"), S("xT_hi"), S("xT_lo")
        lg_ps, q_ps, q_min, q_max = S("lg_ps"), S("q_ps"), S("q_min"), S("q_max")
        kv_ps, k_min, kv_out = S("kv_ps", 2), S("k_min", 2), S("kv_out", 2)
        arg_done, ex_done, feat_done = S("arg_done"), S("ex_done"), S("feat_done")
        sum_ps, kvx_done, mix_ps = S("sum_ps", SEQS), S("kvx_done", SEQS), S("mix_ps", 2)
        den_done, rden_done, mix_done = S("den_done", 2), S("rden_done"), S("mix_done", 2)
        mT_ps, mT_hi, mT_lo, s_ps, s_done = S("mT_ps"), S("mT_hi"), S("mT_lo"), S("s_ps"), S("s_done")
        s_stored = S("s_stored", 16, 16)
        CHAIN = 11
        chain = S("chain", CHAIN)
        gate_split, gT_ps, gT_copied, moved = S("gate_split"), S("gT_ps"), S("gT_copied"), S("moved")
        g_ps, u_ps, c_ps = S("g_ps", HT), S("u_ps", HT), S("c_ps", HT)
        silu_done, a_done, t_done, t_hi, t_lo, y_step = (S(n, HT) for n in ("silu_done", "a_done", "t_done", "t_hi", "t_lo", "y_step"))
        s_loaded, xr_loaded = S("s_loaded", 16), S("xr_loaded", 16)
        sl_done, ys_done, yT_ps, y_done, y_stored = S("sl_done", 1, 1), S("ys_done", 1, 1), S("yT_ps"), S("y_done", 1, 1), S("y_stored", 16, 16)
        order = S("order")

        block = ctx.enter_context(nc.Block())
        consts = [(eye32, eye), (small[:, 0:4 * P], wqkvo), (small[:, 4 * P:], gate_w),
                  (bo_s, bo.rearrange("(p a) -> p a", a=1)), (num, number[:, 0:ER].to_broadcast([P, ER])),
                  (spread_s, spread), (bmask, block_mask), (hmask, head_mask)]
        loads = [(wg, wg_s), (wu, wu_s), (wd.rearrange("(j p) n -> p j n", p=P), wd_s)]
        LAST = turns - 1

        @block.sync
        def _(sp):
            for dst, src in consts:
                sp.dma_start(dst[:], src).then_inc(const_in.handle, 16)
            for n, (src, dst) in enumerate(loads):
                if n:
                    sp.wait_ge(w_ready.handle, n)
                to = stage[:] if len(src.shape) == 2 else stage[:].rearrange("p (j n) -> p j n", n=P)
                sp.dma_start(to, src).then_inc(stage_in.handle, 16)
            sp.sem_inc(xn_done.handle, 1)
            sp.sem_inc(sl_done.handle, 1)
            sp.sem_inc(ys_done.handle, 1)
            sp.sem_inc(y_done.handle, 1)
            sp.sem_inc(s_stored.handle, 16)
            sp.sem_inc(y_stored.handle, 16)

            def load_x(k):
                sp.wait_ge(xn_done.handle, xn_done.before(k))
                sp.dma_start(x_s[:], x_v[k]).then_inc(x_loaded.handle, 16)

            def load_end(k):
                sp.wait_ge(s_stored.handle, s_stored.at(k, 16))
                sp.wait_ge(ys_done.handle, ys_done.before(k))
                sp.dma_start(s_cur[:], s_tmp[:, bass.ts(k, TILE)]).then_inc(s_loaded.handle, 16)
                sp.wait_ge(y_done.handle, y_done.before(k))
                sp.dma_start(x_r[:], x_v[k]).then_inc(xr_loaded.handle, 16)

            def store_s(k):
                sp.wait_ge(s_done.handle, s_done.at(k, 1))
                sp.dma_start(s_tmp[:, bass.ts(k, TILE)], s_next[:]).then_inc(s_stored.handle, 16)

            def store(k):
                sp.wait_ge(y_done.handle, y_done.at(k, 1))
                sp.dma_start(out_v[k], y[:]).then_inc(y_stored.handle, 16)

            load_x(0)
            store_s(0)
            load_x(1)
            load_end(0)
            store_s(1)
            with sp.Fori(1, LAST) as i:
                load_x(i + 1)
                store(i - 1)
                load_end(i)
                store_s(i + 1)
            store(LAST - 1)
            load_end(LAST)
            store(LAST)
            sp.wait_ge(y_stored.handle, 16 * (turns + 1))
            sp.wait_ge(s_stored.handle, 16 * (turns + 1))

        @block.tensor
        def _(te):
            pe = nc.tensor
            te.wait_ge(w_ready.handle, len(loads))
            te.wait_ge(ready.handle, 6)

            def tok(pair, t):
                return pair[:, 0, t * P:(t + 1) * P], pair[:, 1, t * P:(t + 1) * P]

            def turn_x(k):
                te.wait_ge(xn_done.handle, xn_done.at(k, 1))
                for t in range(TB):
                    last = pe.transpose(m0[:, t * P:(t + 1) * P], xn[:, t, :], eye32[:])
                last.then_inc(xT_ps.handle, 1)

            def queries(k):
                te.wait_ge(xT_lo.handle, xT_lo.at(k, 1))
                for t in range(TB):
                    last = split_product(pe, m1[:, t * ER:(t + 1) * ER], tok(x_next, t), w(4 * P, 4 * P + ER))
                last.then_inc(lg_ps.handle, 1)
                split_product(pe, m0[:], w(0, P), (x_next[:, 0, :], x_next[:, 1, :])).then_inc(q_ps.handle, 1)

            def keys_values(k):
                te.wait_ge(q_min.handle, q_min.at(k, 1))
                te.wait_ge(q_max.handle, q_max.at(k, 1))
                te.wait_ge(chain.handle, chain.at(k, 1))
                for s, bank in enumerate((m0, m1)):
                    for b in range(2):
                        last = split_product(pe, bank[:, b * 2 * P:(b + 1) * 2 * P], tok(x_next, 2 * s + b), w(P, 3 * P))
                    last.then_inc(kv_ps.handle, 1)

            def sums(k):
                te.wait_ge(feat_done.handle, feat_done.at(k, 1))
                te.wait_ge(kv_out.handle, kv_out.at(k, 2))
                te.wait_ge(k_min.handle, k_min.at(k, 2))
                for s, bank in enumerate((m0, m1)):
                    for b in range(2):
                        t = 2 * s + b
                        last = pe.matmul(bank[:, 0:P + 1], feat[:, TILE + t * P:TILE + (t + 1) * P], v1[:, t, :],
                                         start=(b == 0), stop=(b == 1), skip_group_check=True)
                    last.then_inc(sum_ps.handle, 1)

            def mix(k):
                for s, bank in enumerate((m0, m1)):
                    te.wait_ge(kvx_done.handle, kvx_done.at(k, s + 1))
                    for b in range(2):
                        t = 2 * s + b
                        last = pe.matmul(bank[:, b * KX:(b + 1) * KX], feat[:, t * P:(t + 1) * P], kvx[:, s, :],
                                         start=True, stop=True, skip_group_check=True)
                    last.then_inc(mix_ps.handle, 1)

            def turn_mixed(k):
                te.wait_ge(mix_done.handle, mix_done.at(k, 2))
                for t in range(TB):
                    last = pe.transpose(m0[:, t * P:(t + 1) * P], mixed[:, t, :], eye32[:])
                last.then_inc(mT_ps.handle, 1)

            def project(k):
                te.wait_ge(mT_lo.handle, mT_lo.at(k, 1))
                split_product(pe, m1[:], w(3 * P, 4 * P), (mT[:, 0, :], mT[:, 1, :])).then_inc(s_ps.handle, 1)

            def turn_gates(k):
                te.wait_ge(gate_split.handle, gate_split.at(k, 1))
                te.sem_inc(order.handle, 1)
                for t in range(TB):
                    last = pe.transpose(m0[0:64, :].bitcast(F16)[:, t * P:(t + 1) * P], gate16[:, t, :], eye16[:])
                last.then_inc(gT_ps.handle, 1)

            def turn_y(k):
                te.wait_ge(ys_done.handle, ys_done.at(k, 1))
                te.wait_ge(s_done.handle, s_done.at(k, 1) if isinstance(k, int) and k == LAST else s_done.at(k + 1, 1))
                for t in range(TB):
                    last = pe.transpose(m1[:, t * P:(t + 1) * P], ys[:, t * P:(t + 1) * P], eye32[:])
                last.then_inc(yT_ps.handle, 1)

            ahead_of = {3: turn_x, 6: queries, 8: keys_values, 13: sums, 15: mix, 18: turn_mixed, 20: project, 21: turn_gates}

            def body(i, ahead, behind):
                te.wait_ge(moved.handle, moved.at(i, 1))
                for j in range(SLOTS):
                    if j < HT:
                        at = slice(j * P, (j + 1) * P)
                        xs = (x_cur[:, 0, :], x_cur[:, 1, :])
                        if j >= 2:
                            te.wait_ge(silu_done.handle, silu_done.at(i, j - 1))
                        split_product(pe, G[j % 2][:], (wg_s[:, 0, at], wg_s[:, 1, at]), xs).then_inc(g_ps.handle, 1)
                        if j >= 2:
                            te.wait_ge(a_done.handle, a_done.at(i, j - 1))
                        split_product(pe, U[j % 2][:], (wu_s[:, 0, at], wu_s[:, 1, at]), xs).then_inc(u_ps.handle, 1)
                    if j >= LAG:
                        k = j - LAG
                        at = slice(k * P, (k + 1) * P)
                        if k == 0:
                            te.wait_ge(sl_done.handle, sl_done.before(i))
                        te.wait_ge(t_hi.handle, t_hi.at(i, k + 1))
                        te.wait_ge(t_lo.handle, t_lo.at(i, k + 1))
                        split_product(pe, Y[:], (wd_s[:, 0, at], wd_s[:, 1, at]),
                                      (t16[k % TBUF][:, 0, :], t16[k % TBUF][:, 1, :]), start=(k == 0), stop=(k == HT - 1))\
                            .then_inc(y_step.handle, 1)
                    if j < HT:
                        if j:
                            te.wait_ge(t_done.handle, t_done.at(i, j))
                        pe.matmul(C[:], spread_s[:, j * P:(j + 1) * P], gatesT[:], start=True, stop=True)\
                            .then_inc(c_ps.handle, 1)
                    if behind and j == 2:
                        turn_y(i - 1)
                    if ahead and j in ahead_of:
                        ahead_of[j](i + 1)

            for part in ahead_of.values():
                part(0)
            body(0, True, False)
            with te.Fori(1, LAST) as i:
                body(i, True, True)
            body(LAST, False, True)
            turn_y(LAST)

        @block.scalar
        def _(ac):
            act = nc.scalar.activation
            ac.wait_ge(const_in.handle, 16 * len(consts))
            act(eye16[:], eye32[:], ACT.Copy).then_inc(ready.handle, 1)
            act(small16[:, 0, :], small[:], ACT.Copy).then_inc(ready.handle, 1)
            for n, (src, dst) in enumerate(loads):
                ac.wait_ge(stage_in.handle, 16 * (n + 1))
                act(dst[:, 0, :], stage[:], ACT.Copy).then_inc(stage_hi.handle, 1)
            ac.wait_ge(ready.handle, 6)

            def root(k):
                ac.wait_ge(aggr_done.handle, aggr_done.at(k, 1))
                act(std[:], mean_var[:, :, 1], ACT.Sqrt, bias=eps[:]).then_inc(std_done.handle, 1)

            def x_high(k):
                ac.wait_ge(xT_ps.handle, xT_ps.at(k, 1))
                act(x_next[:, 0, :], m0[:], ACT.Copy).then_inc(xT_hi.handle, 1)

            def q_part(k):
                ac.wait_ge(q_ps.handle, q_ps.at(k, 1))
                act(pos_part[:, 0:TILE], m0[:], ACT.Relu).then_inc(q_max.handle, 1)

            def kv_part(k):
                for s, bank in enumerate((m0, m1)):
                    kv = bank[:].rearrange("p (b c n) -> p b c n", b=2, c=2)
                    ac.wait_ge(kv_ps.handle, kv_ps.at(k, s + 1))
                    act(pos_part[:, TILE + s * 256:TILE + (s + 1) * 256].rearrange("p (b n) -> p b n", b=2), kv[:, :, 0, :],
                        ACT.Relu)
                    act(v1[:, 2 * s:2 * s + 2, 0:P], kv[:, :, 1, :], ACT.Copy).then_inc(kv_out.handle, 1)

            def exps(k):
                ac.wait_ge(arg_done.handle, arg_done.at(k, 1))
                ac.wait_ge(k_min.handle, k_min.at(k, 2))
                ac.wait_ge(q_min.handle, q_min.at(k, 1))
                act(ex[:], arg[:], ACT.Exp).then_inc(ex_done.handle, 1)

            def m_high(k):
                ac.wait_ge(mT_ps.handle, mT_ps.at(k, 1))
                act(mT[:, 0, :], m0[:], ACT.Copy).then_inc(mT_hi.handle, 1)

            def s_copy(k):
                ac.wait_ge(s_ps.handle, s_ps.at(k, 1))
                ac.wait_ge(s_stored.handle, s_stored.before(k))
                act(s_next[:], m1[:], ACT.Identity, bias=bo_s[:]).then_inc(s_done.handle, 1)

            def copy_gates(k):
                ac.wait_ge(gT_ps.handle, gT_ps.at(k, 1))
                act(gates_next[:], m0[0:64, :].bitcast(F16)[:, 0:TILE], ACT.Copy).then_inc(gT_copied.handle, 1)

            def gate_y(k):
                ac.wait_ge(y_step.handle, y_step.at(k, HT))
                ac.wait_ge(ys_done.handle, ys_done.before(k))
                act(sl[:], Y[:], ACT.Silu).then_inc(sl_done.handle, 1)

            ahead_of = {1: root, 4: x_high, 7: q_part, 9: kv_part, 11: exps, 19: m_high, 21: s_copy, 22: copy_gates}

            def body(i, ahead, behind):
                for j in range(HT + 1):
                    if behind and j == 0:
                        gate_y(i - 1)
                    if j < HT:
                        ac.wait_ge(g_ps.handle, g_ps.at(i, j + 1))
                        if j >= 2:
                            ac.wait_ge(a_done.handle, a_done.at(i, j - 1))
                        act(s32[j % 2][:], G[j % 2][:], ACT.Silu).then_inc(silu_done.handle, 1)
                    if j:
                        ac.wait_ge(t_done.handle, t_done.at(i, j))
                        if j > TBUF:
                            ac.wait_ge(y_step.handle, y_step.at(i, j - TBUF))
                        act(t16[(j - 1) % TBUF][:, 0, :], t32[(j - 1) % 3][:], ACT.Copy).then_inc(t_hi.handle, 1)
                    if ahead and j in ahead_of:
                        ahead_of[j](i + 1)

            for part in ahead_of.values():
                part(0)
            body(0, True, False)
            with ac.Fori(1, LAST) as i:
                body(i, True, True)
            body(LAST, False, True)
            gate_y(LAST)

        @block.vector
        def _(ve):
            vec = nc.vector
            ve.wait_ge(const_in.handle, 16 * len(consts))
            vec.memset(gate16[:], 0.0).then_inc(ready.handle, 1)
            ve.wait_ge(ready.handle, 3)
            vec.memset(gate16[:, :, ER:ER + 1], 1.0)
            vec.memset(eps[:], EPS)
            vec.memset(v1[:, :, P:P + 1], 1.0).then_inc(ready.handle, 2)
            vec.tensor_tensor(small16[:, 1, :], small[:], small16[:, 0, :], ALU.subtract).then_inc(ready.handle, 1)
            for n, (src, dst) in enumerate(loads):
                ve.wait_ge(stage_hi.handle, n + 1)
                vec.tensor_tensor(dst[:, 1, :], stage[:], dst[:, 0, :], ALU.subtract).then_inc(w_ready.handle, 1)

            def norm_stats(k):
                ve.wait_ge(x_loaded.handle, x_loaded.at(k, 16))
                for t in range(TB):
                    last = vec.bn_stats(stats[:, t, :], x_s[:, t, :])
                last.then_inc(stats_done.handle, 1)
                ve.wait_ge(stats_done.handle, stats_done.at(k, 1))
                ve.sem_inc(order.handle, 1)
                for t in range(TB):
                    last = vec.bn_aggr(mean_var[:, t, :], stats[:, t, :])
                last.then_inc(aggr_done.handle, 1)

            def norm(k):
                ve.wait_ge(std_done.handle, std_done.at(k, 1))
                vec.reciprocal(rstd[:], std[:]).then_inc(rstd_done.handle, 1)
                ve.wait_ge(rstd_done.handle, rstd_done.at(k, 1))
                for t in range(TB):
                    last = vec.tensor_scalar(xn[:, t, :], x_s[:, t, :], mean_var[:, t, 0:1], rstd[:, t:t + 1],
                                             ALU.subtract, ALU.mult)
                last.then_inc(xn_done.handle, 1)

            def x_low(k):
                ve.wait_ge(xT_hi.handle, xT_hi.at(k, 1))
                vec.tensor_tensor(x_next[:, 1, :], m0[:], x_next[:, 0, :], ALU.subtract).then_inc(xT_lo.handle, 1)

            steps = {}

            def step(k, ins):
                n = steps[id(k)] = steps.get(id(k), 0) + 1
                ins.then_inc(chain.handle, 1)
                ve.wait_ge(chain.handle, chain.at(k, n))

            def q_neg(k):
                steps[id(k)] = 0
                ve.wait_ge(lg_ps.handle, lg_ps.at(k, 1))
                step(k, vec.tensor_copy(lg[:], m1[:, 0:TB * ER].rearrange("p (t e) -> p t e", t=TB)))
                ve.wait_ge(q_max.handle, q_max.at(k, 1))
                vec.tensor_scalar(arg[:, 0:TILE], m0[:], 0.0, None, ALU.min).then_inc(q_min.handle, 1)
                ve.sem_inc(order.handle, 1)
                for t in range(TB):
                    last = vec.max(top[:, t, :], lg[:, t, :])
                step(k, last)
                ve.sem_inc(order.handle, 1)

            def k_neg(k):
                for t in range(TB):
                    last = vec.max_index(top_i[:, t, :], top[:, t, :], lg[:, t, :])
                step(k, last)
                vec.tensor_tensor(arg[:, 2 * TILE:].rearrange("p (t k) -> p t k", t=TB), top[:, :, 0:TOP],
                                  top[:, :, 0:1].to_broadcast([P, TB, TOP]), ALU.subtract).then_inc(arg_done.handle, 1)
                for s, bank in enumerate((m0, m1)):
                    ve.wait_ge(kv_out.handle, kv_out.at(k, s + 1))
                    vec.tensor_scalar(arg[:, TILE + s * 256:TILE + (s + 1) * 256].rearrange("p (b n) -> p b n", b=2),
                                      bank[:].rearrange("p (b c n) -> p b c n", b=2, c=2)[:, :, 0, :], 0.0, None, ALU.min)\
                       .then_inc(k_min.handle, 1)

            def choose(k):
                e3 = ex[:, 2 * TILE:].rearrange("p (t k) -> p t k", t=TB)
                ve.wait_ge(ex_done.handle, ex_done.at(k, 1))
                step(k, vec.tensor_reduce(wsum[:], e3, AX, ALU.add))
                step(k, vec.reciprocal(wsum[:], wsum[:]))
                step(k, vec.tensor_tensor(share[:], e3, over(wsum[:], TOP, 2), ALU.mult))
                step(k, vec.tensor_copy(top_f[:], top_i[:]))
                step(k, vec.tensor_tensor(hit[:], over(over(num[:], TOP), TB), over(top_f[:, :, 0:TOP], ER, 3), ALU.is_equal))

            def choose_more(k):
                step(k, vec.tensor_tensor(hit[:], hit[:], over(share[:], ER, 3), ALU.mult))
                step(k, vec.tensor_reduce(gates[:], hit[:].rearrange("p t k e -> p t e k"), AX, ALU.add))
                step(k, vec.tensor_copy(gate16[:, :, 0:ER], gates[:]))
                assert steps[id(k)] == CHAIN
                vec.tensor_tensor(gate16[:, :, 32:32 + ER], gates[:], gate16[:, :, 0:ER], ALU.subtract)\
                   .then_inc(gate_split.handle, 1)

            def mask_sums(k):
                for s, bank in enumerate((m0, m1)):
                    ve.wait_ge(sum_ps.handle, sum_ps.at(k, s + 1))
                    vec.tensor_tensor(kvx[:, s, 0:P], bank[:, 0:P], bmask[:], ALU.mult)
                    vec.tensor_scalar(kvx[:, s, P:], hmask[:], bank[:, P:P + 1], None, ALU.mult).then_inc(kvx_done.handle, 1)

            def divide(k):
                for s, bank in enumerate((m0, m1)):
                    ve.wait_ge(mix_ps.handle, mix_ps.at(k, s + 1))
                    got = bank[:, 0:2 * KX].rearrange("p (b n) -> p b n", b=2)
                    vec.tensor_scalar(den[:, 2 * s:2 * s + 2, :], got[:, :, P:], 1e-6, None, ALU.add).then_inc(den_done.handle, 1)
                ve.wait_ge(den_done.handle, den_done.at(k, 2))
                vec.reciprocal(rden[:], den[:]).then_inc(rden_done.handle, 1)
                ve.wait_ge(rden_done.handle, rden_done.at(k, 1))
                for s, bank in enumerate((m0, m1)):
                    for b in range(2):
                        t = 2 * s + b
                        last = vec.tensor_tensor(mixed[:, t, :].rearrange("p (h d) -> p h d", d=HD),
                                                 bank[:, b * KX:b * KX + P].rearrange("p (h d) -> p h d", d=HD),
                                                 over(rden[:, t, :], HD, 2), ALU.mult)
                    last.then_inc(mix_done.handle, 1)

            def m_low(k):
                ve.wait_ge(mT_hi.handle, mT_hi.at(k, 1))
                vec.tensor_tensor(mT[:, 1, :], m0[:], mT[:, 0, :], ALU.subtract).then_inc(mT_lo.handle, 1)

            def move(k):
                ve.wait_ge(gT_copied.handle, gT_copied.at(k, 1))
                vec.tensor_copy(x_cur[:], x_next[:])
                vec.tensor_copy(gatesT[:], gates_next[:]).then_inc(moved.handle, 1)

            def add_x(k):
                ve.wait_ge(yT_ps.handle, yT_ps.at(k, 1))
                ve.wait_ge(xr_loaded.handle, xr_loaded.at(k, 16))
                ve.wait_ge(y_stored.handle, y_stored.before(k))
                vec.tensor_tensor(y[:].rearrange("p t d -> p (t d)"), m1[:], x_r[:].rearrange("p t d -> p (t d)"), ALU.add)\
                   .then_inc(y_done.handle, 1)

            ahead_of = {0: norm_stats, 2: norm, 5: x_low, 7: q_neg, 9: k_neg, 12: choose, 14: mask_sums, 16: divide,
                        17: choose_more, 20: m_low}

            def body(i, ahead, behind):
                nxt = i + 1
                for j in range(HT + 1):
                    if j:
                        ve.wait_ge(c_ps.handle, c_ps.at(i, j))
                        ve.wait_ge(a_done.handle, a_done.at(i, j))
                        if j > 3:
                            ve.wait_ge(t_lo.handle, t_lo.at(i, j - 3))
                        vec.tensor_tensor(t32[(j - 1) % 3][:], C[:], a32[(j - 1) % 2][:], ALU.mult).then_inc(t_done.handle, 1)
                    if j < HT:
                        ve.wait_ge(u_ps.handle, u_ps.at(i, j + 1))
                        ve.wait_ge(silu_done.handle, silu_done.at(i, j + 1))
                        vec.tensor_tensor(a32[j % 2][:], U[j % 2][:], s32[j % 2][:], ALU.mult).then_inc(a_done.handle, 1)
                    if behind and j == 4:
                        add_x(i - 1)
                    if ahead and j in ahead_of:
                        ahead_of[j](nxt)
                if ahead:
                    move(nxt)

            first = 0
            for part in ahead_of.values():
                part(first)
            move(first)
            body(0, True, False)
            with ve.Fori(1, LAST) as i:
                body(i, True, True)
            body(LAST, False, True)
            add_x(LAST)

        @block.gpsimd
        def _(po):
            pool = nc.gpsimd

            def features(k):
                po.wait_ge(ex_done.handle, ex_done.at(k, 1))
                pool.tensor_tensor(feat[:], ex[:, 0:2 * TILE], pos_part[:], ALU.add).then_inc(feat_done.handle, 1)

            def scale_s(k):
                po.wait_ge(sl_done.handle, sl_done.at(k, 1))
                po.wait_ge(s_loaded.handle, s_loaded.at(k, 16))
                pool.tensor_tensor(ys[:], sl[:], s_cur[:], ALU.mult).then_inc(ys_done.handle, 1)

            def body(i, ahead, behind):
                for j in range(HT):
                    if behind and j == 1:
                        scale_s(i - 1)
                    po.wait_ge(t_hi.handle, t_hi.at(i, j + 1))
                    pool.tensor_tensor(t16[j % TBUF][:, 1, :], t32[j % 3][:], t16[j % TBUF][:, 0, :], ALU.subtract)\
                        .then_inc(t_lo.handle, 1)
                    if ahead and j == 11:
                        features(i + 1)

            features(0)
            body(0, True, False)
            with po.Fori(1, LAST) as i:
                body(i, True, True)
            body(LAST, False, True)
            scale_s(LAST)


def recurrent_depth_two_kernel(nc, x, wq, wk, wvgb, wo, norm_w, qk_w, qk_b, v_w, v_b, o_w, o_b, gamma1, gamma2, theta,
                               position, half_sign, router_w, router_b, w1, b1, w2, b2, wqkvo, bo, gate_w, wg, wu, wd,
                               eye, below, upto, future, spread1, spread2, number, block_mask, head_mask, out):
    tokens = x.shape[0]
    turns = tokens // TILE

    def activation(name, shape):
        return nc.dram_tensor(name, shape, F32, kind="Internal").ap()

    xn, x1 = activation("xn", (tokens, P)), activation("x1", (tokens, P))
    mixer, an, rest, mixer2 = (activation(n, (P, tokens)) for n in ("mixer", "an", "rest", "mixer2"))
    delta_phase(nc, x, wq, wk, wvgb, wo, norm_w, eye, below, upto, xn, mixer)
    attention_phase(nc, xn, qk_w, qk_b, v_w, v_b, o_w, o_b, gamma1, gamma2, theta, position, half_sign, eye, future,
                    an, rest, turns)
    experts_phase(nc, an, rest, mixer, x, router_w, router_b, w1, b1, w2, b2, spread1, number, eye, x1, turns)
    second_layer_phase(nc, x1, wqkvo, bo, gate_w, wg, wu, wd, spread2, number, block_mask, head_mask, eye, mixer2, out,
                       turns)


def kernel(**inputs):
    import concourse.bacc as bacc
    from concourse.bass_utils import run_bass_kernel_spmd

    L0 = {k[3:]: np.asarray(v) for k, v in inputs.items() if k.startswith("L0_")}
    L1 = {k[3:]: np.asarray(v) for k, v in inputs.items() if k.startswith("L1_")}
    x = L0["attn_x"]
    heads, hd = 16, 64

    even_odd = np.concatenate([np.arange(0, hd, 2), np.arange(1, hd, 2)])
    odd_even = np.concatenate([even_odd[hd // 2:], even_odd[:hd // 2]])

    def columns(w, order):
        return w.reshape(w.shape[:-1] + (heads, hd))[..., order].reshape(w.shape)

    def four(q, k):
        return [columns(q, even_odd), columns(q, odd_even), columns(k, even_odd), columns(k, odd_even)]

    ne = L0["ffn_re_w1"].shape[0]
    b2 = np.zeros((64, P), np.float32)
    b2[:ne], b2[ne], b2[32:32 + ne] = L0["ffn_re_b2"], L0["ffn_sh_b2"], L0["ffn_re_b2"]
    spread1 = np.zeros((64, ne + 1, P), np.float16)
    for e in range(ne + 1):
        spread1[e, e] = spread1[32 + e, e] = 1

    experts, _, inter = L1["ffn_Wg"].shape
    units = experts * inter + L1["ffn_Sg"].shape[1]
    padded = -(-units // P) * P

    def stack(w, shared):
        return np.concatenate([w.transpose(1, 0, 2).reshape(P, -1), shared, np.zeros((P, padded - units), np.float32)], 1)

    owner = np.minimum(np.arange(padded) // inter, experts)
    spread2 = np.zeros((64, padded), np.float16)
    spread2[owner, np.arange(padded)] = 1
    spread2[32 + owner[owner < experts], np.arange(padded)[owner < experts]] = 1

    args = {
        "x": x.reshape(-1, P), "wq": L0["attn_Wq"], "wk": L0["attn_Wk"],
        "wvgb": np.concatenate([L0["attn_Wv"], L0["attn_Wg"], L0["attn_Wb"]], 1),
        "wo": L0["attn_Wo"], "norm_w": L0["attn_norm_w"],
        "qk_w": np.concatenate(four(L0["ffn_q_w"], L0["ffn_k_w"]), 1),
        "qk_b": np.stack(four(L0["ffn_q_b"], L0["ffn_k_b"])).reshape(4, 8, P).transpose(2, 0, 1),
        "v_w": L0["ffn_v_w"], "v_b": L0["ffn_v_b"].reshape(8, P).T, "o_w": L0["ffn_o_w"], "o_b": L0["ffn_o_b"],
        "gamma1": L0["ffn_gamma1"], "gamma2": L0["ffn_gamma2"], "theta": np.tile(L0["ffn_theta"], 4)[:, None],
        "position": np.arange(SEQ, dtype=np.float32)[None],
        "half_sign": np.where((np.arange(P) // 32) % 2, 1, -1).astype(np.float32)[:, None],
        "router_w": L0["ffn_router_w"], "router_b": L0["ffn_router_b"],
        "w1": np.concatenate([L0["ffn_re_w1"], L0["ffn_sh_w1"][None]]),
        "b1": np.concatenate([L0["ffn_re_b1"], L0["ffn_sh_b1"][None]]).T,
        "w2": np.concatenate([L0["ffn_re_w2"], L0["ffn_sh_w2"][None]]), "b2": b2,
        "wqkvo": np.concatenate([L1["attn_wq"].T, L1["attn_wk"].T, L1["attn_wv"].T, L1["attn_wo"].T], 1),
        "bo": L1["attn_bo"], "gate_w": L1["ffn_gate_w"],
        "wg": stack(L1["ffn_Wg"], L1["ffn_Sg"]), "wu": stack(L1["ffn_Wu"], L1["ffn_Su"]),
        "wd": np.concatenate([L1["ffn_Wd"].reshape(-1, P), L1["ffn_Sd"], np.zeros((padded - units, P), np.float32)]),
        "eye": np.eye(P, dtype=np.float32), "below": np.tril(np.ones((P, P), np.float32), -1),
        "upto": np.triu(np.ones((P, P), np.float32)), "future": np.triu(np.full((P, P), -1e30, np.float32), 1),
        "spread1": spread1.reshape(64, -1), "spread2": spread2,
        "number": np.arange(ne, dtype=np.float32)[None],
        "block_mask": np.kron(np.eye(16), np.ones((8, 8))).astype(np.float32),
        "head_mask": np.kron(np.eye(16), np.ones((8, 1))).astype(np.float32),
    }
    nc = bacc.Bacc("TRN2", target_bir_lowering=False, num_devices=1)
    arrays, aps = {}, {}
    for name, a in args.items():
        arrays[f"in_{name}"] = np.ascontiguousarray(a)
        aps[name] = nc.dram_tensor(f"in_{name}", a.shape, mybir.dt.from_np(a.dtype), kind="ExternalInput").ap()
    out = nc.dram_tensor("out", (x.shape[0] * x.shape[1], P), F32, kind="ExternalOutput").ap()
    recurrent_depth_two_kernel(nc, out=out, **aps)
    result = run_bass_kernel_spmd(nc, [arrays], core_ids=[0])
    return result.results[0]["out"].reshape(x.shape)
```

```python
from contextlib import ExitStack

import concourse.bass as bass
import numpy as np
from concourse import mybir

ALU = mybir.AluOpType
ACT = mybir.ActivationFunctionType
F32 = mybir.dt.float32
F16 = mybir.dt.float16
BF16 = mybir.dt.bfloat16
AX = mybir.AxisListType.X

P = 128
SEQ = 256
TILE = 512
TB = TILE // P
SEQS = TILE // SEQ
EPS = 1e-5


class Signal:

    def __init__(self, handle, per, first=0):
        self.handle, self.per, self.first = handle, per, first

    def at(self, turn, n):
        return turn * self.per + (self.first + n)

    def before(self, turn, n=None):
        return turn * self.per + (self.first + (self.per if n is None else n) - self.per)


class Memory:

    def __init__(self, nc, ctx, name):
        self.nc, self.ctx, self.name, self.handles = nc, ctx, name, []
        ctx.callback(self.clear_semaphores)

    def sbuf(self, name, shape, dtype=F32):
        return self.ctx.enter_context(self.nc.sbuf_tensor(f"{self.name}_{name}", shape, dtype))

    def banks(self, name, n):
        return [self.ctx.enter_context(self.nc.psum_tensor(f"{self.name}_{name}_bank{k}", [P, 512], F32)) for k in range(n)]

    def count(self, name, per=1, first=0):
        self.handles.append(self.nc.alloc_semaphore(f"{self.name}_{name}"))
        return Signal(self.handles[-1], per, first)

    def clear_semaphores(self):
        self.nc.clear_and_free_semaphores(self.handles)
        self.nc.all_engine_barrier()


def split_product(pe, out, left, right, start=True, stop=True):
    (lh, ll), (rh, rl) = left, right
    pe.matmul(out, ll, rh, start=start, stop=False, skip_group_check=True)
    pe.matmul(out, lh, rl, start=False, stop=False, skip_group_check=True)
    return pe.matmul(out, lh, rh, start=False, stop=stop, skip_group_check=True)


def over(ap, n, axis=1):
    ap = ap.unsqueeze(axis)
    shape = list(ap.shape)
    shape[axis] = n
    return ap.to_broadcast(shape)


def delta_phase(nc, x, wq, wk, wvgb, wo, norm_w, eye, below, upto, xn_out, s_out):
    H, DK, DV = 4, 128, 32
    turns = x.shape[0] // TILE
    LEVELS = 7
    SCALE = DK ** -0.5
    x_v = x.rearrange("(n t p) d -> n p t d", t=TB, p=P)
    xn_v = xn_out.rearrange("(n t p) d -> n p t d", t=TB, p=P)
    nv = wvgb.shape[1]

    with ExitStack() as ctx:
        m = Memory(nc, ctx, "delta")
        eye32, eye16 = m.sbuf("eye32", [P, P]), m.sbuf("eye16", [P, P], F16)
        below_m, upto_m = m.sbuf("below", [P, P]), m.sbuf("upto", [P, P])
        eps = m.sbuf("eps", [P, 2])
        norm_row = m.sbuf("norm_row", [P, DV])
        stage = m.sbuf("w_stage", [P, 512 + 512 + nv + 128])
        w_pair = m.sbuf("w_pair", [P, 2, 512 + 512 + nv + 128], F16)
        cut = {"q": (0, 512), "k": (512, 1024), "vgb": (1024, 1024 + nv), "o": (1024 + nv, 1152 + nv)}

        def weight(name, a=0, b=None):
            lo, hi = cut[name]
            b = hi - lo if b is None else b
            return w_pair[:, 0, lo + a:lo + b], w_pair[:, 1, lo + a:lo + b]

        x_in = m.sbuf("x_in", [P, TB, P])
        stats = m.sbuf("stats", [P, TB, 6])
        mean_var = m.sbuf("mean_var", [P, TB, 2])
        std = m.sbuf("std", [P, TB])
        rstd = m.sbuf("rstd", [P, TB])
        xn = m.sbuf("xn", [P, TB, P])
        xT = m.sbuf("xT", [P, 2, TILE], F16)
        ksq = m.sbuf("ksq", [P, TB, H * DK])
        kss = m.sbuf("kss", [P, TB * H])
        knorm = m.sbuf("knorm", [P, TB * H])
        krn = m.sbuf("krn", [P, TB * H])
        khat = m.sbuf("khat", [P, TB, H * DK])
        kT = m.sbuf("kT", [P, 2, TB, H * P], F16)
        qT = m.sbuf("qT", [P, 2, H, TILE], F16)
        v = m.sbuf("v", [P, TB, H * DV])
        g = m.sbuf("g", [P, TB, H * DV])
        gate = m.sbuf("gate", [P, TB, H * DV])
        beta = m.sbuf("beta", [P, TB, H])
        neg_beta = m.sbuf("neg_beta", [P, TB, H])
        b32 = [m.sbuf(f"b32_{s}", [P, H * P]) for s in range(SEQS)]
        power = [[m.sbuf(f"power{s}_{k}", [P, 2, H * P], F16) for k in range(2)] for s in range(SEQS)]
        powerT = [[m.sbuf(f"powerT{s}_{k}", [P, 2, H * P], F16) for k in range(2)] for s in range(SEQS)]
        rhs32 = [m.sbuf(f"rhs32_{s}", [P, H * DV]) for s in range(SEQS)]
        rhs = [m.sbuf(f"rhs{s}", [P, 2, H * DV], F16) for s in range(SEQS)]
        qk = [m.sbuf(f"qk{s}", [P, H * P]) for s in range(SEQS)]
        upd = [m.sbuf(f"upd{s}", [P, H * DV]) for s in range(SEQS)]
        state = [m.sbuf(f"state{s}", [P, 2, H * DV], F16) for s in range(SEQS)]
        o = m.sbuf("o", [P, TB, H * DV])
        osq = m.sbuf("osq", [P, TB * H * DV])
        oss = m.sbuf("oss", [P, TB * H])
        ostd = m.sbuf("ostd", [P, TB * H])
        orn = m.sbuf("orn", [P, TB * H])
        og = m.sbuf("og", [P, TB * H * DV])
        oT = m.sbuf("oT", [P, 2, TILE], F16)
        sT = m.sbuf("sT", [P, TILE])

        pow_ps, powT_ps = m.banks("pow", 2), m.banks("powT", 2)
        rhs_ps, misc_ps = m.banks("rhs", 2), m.banks("misc", 2)
        prep = pow_ps + powT_ps

        S = m.count
        const_in = S("const_in")
        w_ready = S("w_ready")
        x_loaded = S("x_loaded", 16)
        stats_done, aggr_done = S("stats_done"), S("aggr_done")
        std_done, rstd_done = S("std_done"), S("rstd_done")
        xn_done, xn_stored = S("xn_done", 1, 1), S("xn_stored", 16, 16)
        xT_ps_done, xT_hi, xT_lo = S("xT_ps_done"), S("xT_hi"), S("xT_lo")
        k_ps, ksq_done, kss_done = S("k_ps", TB), S("ksq_done", TB), S("kss_done", 1)
        knorm_done, krn_done, khat_done = S("knorm_done"), S("krn_done"), S("khat_done", TB)
        kT_ps, kT_hi, kT_lo = S("kT_ps", TB), S("kT_hi", TB), S("kT_lo", TB)
        q_ps, q_hi, q_lo = S("q_ps", H), S("q_hi", H), S("q_lo", H)
        v_ps, g_sig, gate_half, gate_done = S("v_ps", TB), S("g_sig", TB), S("gate_half"), S("gate_done")
        negb_done = S("negb_done", 1)
        gram_ps, b32_done, b_hi, b_lo = S("gram_ps", TB), S("b32_done", TB), S("b_hi", TB), S("b_lo", TB)
        qk_ps, qk_done = S("qk_ps", TB), S("qk_done", TB)
        bT_ps, bT_done = S("bT_ps", TB), S("bT_done", TB)
        ks_ps, rhs_sub, rhs32_done = S("ks_ps", SEQS), S("rhs_sub", SEQS), S("rhs32_done", TB)
        NR = TB * LEVELS
        rhs_hi, rhs_lo = S("rhs_hi", NR), S("rhs_lo", NR)
        rhs_step = S("rhs_step", TB * LEVELS)
        NP = TB * (LEVELS - 2)
        NT = TB * (LEVELS - 1)
        pow_step, pow_hi, pow_lo = S("pow_step", NP), S("pow_hi", NP), S("pow_lo", NP)
        powT_step, powT_hi, powT_lo = S("powT_step", NT), S("powT_hi", NT), S("powT_lo", NT)
        upd_done = S("upd_done", TB)
        state_ps, state_hi, state_lo = S("state_ps", SEQS), S("state_hi", SEQS), S("state_lo", SEQS)
        o_ps, o_out = S("o_ps", TB), S("o_out", TB)
        osq_done, oss_done, ostd_done, orn_done = S("osq_done"), S("oss_done"), S("ostd_done"), S("orn_done")
        on_done, og_done = S("on_done"), S("og_done", 1)
        oT_ps, oT_hi, oT_lo = S("oT_ps"), S("oT_hi"), S("oT_lo")
        s_ps, s_copied, s_stored = S("s_ps"), S("s_copied"), S("s_stored", 16, 16)
        order = S("order")

        block = ctx.enter_context(nc.Block())

        @block.sync
        def _(sp):
            for dst, src in ((stage[:, 0:512], wq), (stage[:, 512:1024], wk), (stage[:, 1024:1024 + nv], wvgb),
                             (stage[:, 1024 + nv:], wo), (eye32[:], eye), (below_m[:], below), (upto_m[:], upto),
                             (norm_row[:], norm_w.rearrange("(a d) -> a d", a=1).to_broadcast([P, DV]))):
                sp.dma_start(dst, src).then_inc(const_in.handle, 16)
            sp.sem_inc(xn_stored.handle, 16)
            sp.sem_inc(s_stored.handle, 16)
            sp.sem_inc(xn_done.handle, 1)
            with sp.Fori(0, turns) as i:
                sp.wait_ge(xn_done.handle, xn_done.before(i))
                sp.dma_start(x_in[:], x_v[i]).then_inc(x_loaded.handle, 16)
                sp.wait_ge(xn_done.handle, xn_done.at(i, 1))
                sp.dma_start(xn_v[i], xn[:]).then_inc(xn_stored.handle, 16)
            sp.wait_ge(xn_stored.handle, 16 * (turns + 1))
            sp.wait_ge(s_stored.handle, 16 * (turns + 1))

        @block.tensor
        def _(te):
            pe = nc.tensor
            te.wait_ge(const_in.handle, 16 * 8)
            te.wait_ge(w_ready.handle, 3)
            with te.Fori(0, turns) as i:
                te.wait_ge(xn_done.handle, xn_done.at(i, 1))
                for t in range(TB):
                    last = pe.transpose(misc_ps[0][:, t * P:(t + 1) * P], xn[:, t, :], eye32[:])
                last.then_inc(xT_ps_done.handle, 1)
                te.wait_ge(xT_lo.handle, xT_lo.at(i, 1))
                for t in range(TB):
                    split_product(pe, prep[t][:], (xT[:, 0, t * P:(t + 1) * P], xT[:, 1, t * P:(t + 1) * P]),
                                  weight("k")).then_inc(k_ps.handle, 1)
                for t in range(TB):
                    bank = misc_ps[t % 2]
                    if t >= 2:
                        te.wait_ge(g_sig.handle, g_sig.at(i, t - 1))
                    split_product(pe, bank[:, 0:nv], (xT[:, 0, t * P:(t + 1) * P], xT[:, 1, t * P:(t + 1) * P]),
                                  weight("vgb")).then_inc(v_ps.handle, 1)
                for t in range(TB):
                    te.wait_ge(khat_done.handle, khat_done.at(i, t + 1))
                    for h in range(H):
                        last = pe.transpose(prep[t][:, h * P:(h + 1) * P], khat[:, t, h * DK:(h + 1) * DK], eye32[:])
                    last.then_inc(kT_ps.handle, 1)
                for h in range(H):
                    bank = rhs_ps[h % 2]
                    if h >= 2:
                        te.wait_ge(q_lo.handle, q_lo.at(i, h - 1))
                    split_product(pe, bank[:], weight("q", h * DK, (h + 1) * DK),
                                  (xT[:, 0, :], xT[:, 1, :])).then_inc(q_ps.handle, 1)
                for c in range(2):
                    for s in range(SEQS):
                        t, n = 2 * s + c, 2 * c + s
                        kt = [(kT[:, 0, t, h * P:(h + 1) * P], kT[:, 1, t, h * P:(h + 1) * P]) for h in range(H)]
                        if c == 0:
                            te.wait_ge(kT_lo.handle, kT_lo.at(i, TB))
                        for h in range(H):
                            last = split_product(pe, pow_ps[s][:, h * P:(h + 1) * P], kt[h], kt[h])
                        last.then_inc(gram_ps.handle, 1)
                        te.wait_ge(q_lo.handle, q_lo.at(i, H))
                        for h in range(H):
                            q = (qT[:, 0, h, t * P:(t + 1) * P], qT[:, 1, h, t * P:(t + 1) * P])
                            last = split_product(pe, powT_ps[s][:, h * P:(h + 1) * P], kt[h], q)
                        last.then_inc(qk_ps.handle, 1)
                        if c == 1:
                            te.wait_ge(state_lo.handle, state_lo.at(i, s + 1))
                            for h in range(H):
                                st = (state[s][:, 0, h * DV:(h + 1) * DV], state[s][:, 1, h * DV:(h + 1) * DV])
                                last = split_product(pe, rhs_ps[s][:, h * DV:(h + 1) * DV], kt[h], st)
                            last.then_inc(ks_ps.handle, 1)
                    for s in range(SEQS):
                        n = 2 * c + s
                        te.wait_ge(b_lo.handle, b_lo.at(i, n + 1))
                        if c == 0 and s == 0:
                            te.wait_ge(g_sig.handle, g_sig.at(i, TB))
                        if c == 1:
                            te.wait_ge(o_out.handle, o_out.at(i, s + 1))
                        tr = misc_ps[s][:].bitcast(F16)
                        for half in range(2):
                            for h in range(H):
                                at = (half * H + h) * P
                                last = pe.transpose(tr[:, at:at + P], power[s][0][:, half, h * P:(h + 1) * P], eye16[:])
                        last.then_inc(bT_ps.handle, 1)
                        te.wait_ge(rhs_lo.handle, rhs_lo.at(i, c * SEQS * LEVELS + s + 1))
                        pe.matmul(rhs_ps[s][:, 0:H * DV], eye16[:], rhs[s][:, 1, :], start=True, stop=False,
                                  skip_group_check=True)
                        pe.matmul(rhs_ps[s][:, 0:H * DV], eye16[:], rhs[s][:, 0, :], start=False, stop=False,
                                  skip_group_check=True)
                    for level in range(LEVELS):
                        cur = level % 2
                        for s in range(SEQS):
                            n = 2 * c + s
                            pw, pT = power[s][cur], powerT[s][cur]
                            done = c * SEQS * LEVELS + level * SEQS + s + 1
                            if level == 0:
                                te.wait_ge(bT_done.handle, bT_done.at(i, n + 1))
                            else:
                                te.wait_ge(powT_lo.handle, powT_lo.at(i, c * SEQS * (LEVELS - 1) + (level - 1) * SEQS + s + 1))
                                te.wait_ge(rhs_lo.handle, rhs_lo.at(i, done))
                            for h in range(H):
                                last = split_product(pe, rhs_ps[s][:, h * DV:(h + 1) * DV],
                                                     (pT[:, 0, h * P:(h + 1) * P], pT[:, 1, h * P:(h + 1) * P]),
                                                     (rhs[s][:, 0, h * DV:(h + 1) * DV], rhs[s][:, 1, h * DV:(h + 1) * DV]),
                                                     start=False, stop=(level == LEVELS - 1))
                            last.then_inc(rhs_step.handle, 1)
                            if level == LEVELS - 1:
                                continue
                            if level == 0:
                                te.wait_ge(b_lo.handle, b_lo.at(i, n + 1))
                                te.wait_ge(qk_done.handle, qk_done.at(i, n + 1))
                            else:
                                te.wait_ge(pow_lo.handle, pow_lo.at(i, c * SEQS * (LEVELS - 2) + (level - 1) * SEQS + s + 1))
                            ph = [(pw[:, 0, h * P:(h + 1) * P], pw[:, 1, h * P:(h + 1) * P]) for h in range(H)]
                            pt = [(pT[:, 0, h * P:(h + 1) * P], pT[:, 1, h * P:(h + 1) * P]) for h in range(H)]
                            for h in range(H):
                                last = split_product(pe, powT_ps[s][:, h * P:(h + 1) * P], ph[h], pt[h])
                            last.then_inc(powT_step.handle, 1)
                            if level < LEVELS - 2:
                                for h in range(H):
                                    last = split_product(pe, pow_ps[s][:, h * P:(h + 1) * P], pt[h], ph[h])
                                last.then_inc(pow_step.handle, 1)
                    for s in range(SEQS):
                        t, n = 2 * s + c, 2 * c + s
                        te.wait_ge(upd_done.handle, upd_done.at(i, n + 1))
                        for h in range(H):
                            out = misc_ps[s][:, h * DV:(h + 1) * DV]
                            if c == 1:
                                q = (qT[:, 0, h, t * P:(t + 1) * P], qT[:, 1, h, t * P:(t + 1) * P])
                                st = (state[s][:, 0, h * DV:(h + 1) * DV], state[s][:, 1, h * DV:(h + 1) * DV])
                                split_product(pe, out, q, st, stop=False)
                            last = pe.matmul(out, qk[s][:, h * P:(h + 1) * P], upd[s][:, h * DV:(h + 1) * DV],
                                             start=(c == 0), stop=True, skip_group_check=True)
                        last.then_inc(o_ps.handle, 1)
                        if c == 0:
                            for h in range(H):
                                last = pe.matmul(rhs_ps[s][:, h * DV:(h + 1) * DV], khat[:, t, h * DK:(h + 1) * DK],
                                                 upd[s][:, h * DV:(h + 1) * DV], start=True, stop=True)
                            last.then_inc(state_ps.handle, 1)
                te.wait_ge(og_done.handle, og_done.at(i, 1))
                for t in range(TB):
                    last = pe.transpose(misc_ps[0][:, t * P:(t + 1) * P], og[:, t * P:(t + 1) * P], eye32[:])
                last.then_inc(oT_ps.handle, 1)
                te.wait_ge(oT_lo.handle, oT_lo.at(i, 1))
                split_product(pe, misc_ps[1][:], weight("o"), (oT[:, 0, :], oT[:, 1, :])).then_inc(s_ps.handle, 1)
                te.wait_ge(s_copied.handle, s_copied.at(i, 1))

        @block.scalar
        def _(ac):
            act = nc.scalar.activation
            ac.wait_ge(const_in.handle, 16 * 8)
            act(w_pair[:, 0, :], stage[:], ACT.Copy).then_inc(w_ready.handle, 1)
            act(eye16[:], eye32[:], ACT.Copy).then_inc(w_ready.handle, 1)
            ac.wait_ge(order.handle, 2)
            with ac.Fori(0, turns) as i:
                ac.wait_ge(aggr_done.handle, aggr_done.at(i, 1))
                act(std[:], mean_var[:, :, 1], ACT.Sqrt, bias=eps[:, 0:1]).then_inc(std_done.handle, 1)
                ac.wait_ge(xT_ps_done.handle, xT_ps_done.at(i, 1))
                act(xT[:, 0, :], misc_ps[0][:], ACT.Copy).then_inc(xT_hi.handle, 1)
                for t in range(TB):
                    ac.wait_ge(k_ps.handle, k_ps.at(i, t + 1))
                    act(ksq[:, t, :], prep[t][:], ACT.Square).then_inc(ksq_done.handle, 1)
                ac.wait_ge(kss_done.handle, kss_done.at(i, 1))
                act(knorm[:], kss[:], ACT.Sqrt, bias=eps[:, 1:2]).then_inc(knorm_done.handle, 1)
                for t in range(TB):
                    bank = misc_ps[t % 2]
                    ac.wait_ge(v_ps.handle, v_ps.at(i, t + 1))
                    act(v[:, t, :], bank[:, 0:128], ACT.Copy)
                    act(g[:, t, :], bank[:, 128:256], ACT.Copy)
                    act(gate[:, t, :], bank[:, 128:256], ACT.Sigmoid)
                    act(beta[:, t, :], bank[:, 256:260], ACT.Sigmoid).then_inc(g_sig.handle, 1)
                for t in range(TB):
                    ac.wait_ge(kT_ps.handle, kT_ps.at(i, t + 1))
                    act(kT[:, 0, t, :], prep[t][:], ACT.Copy).then_inc(kT_hi.handle, 1)
                for h in range(H):
                    ac.wait_ge(q_ps.handle, q_ps.at(i, h + 1))
                    act(qT[:, 0, h, :], rhs_ps[h % 2][:], ACT.Copy, scale=SCALE).then_inc(q_hi.handle, 1)
                for c in range(2):
                    for s in range(SEQS):
                        n = 2 * c + s
                        ac.wait_ge(b32_done.handle, b32_done.at(i, n + 1))
                        act(power[s][0][:, 0, :], b32[s][:], ACT.Copy).then_inc(b_hi.handle, 1)
                        ac.wait_ge(rhs32_done.handle, rhs32_done.at(i, n + 1))
                        act(rhs[s][:, 0, :], rhs32[s][:], ACT.Copy).then_inc(rhs_hi.handle, 1)
                    for s in range(SEQS):
                        n = 2 * c + s
                        ac.wait_ge(bT_ps.handle, bT_ps.at(i, n + 1))
                        act(powerT[s][0][:].rearrange("p a n -> p (a n)"), misc_ps[s][:].bitcast(F16), ACT.Copy).then_inc(bT_done.handle, 1)
                    for level in range(LEVELS):
                        new = (level + 1) % 2
                        for s in range(SEQS):
                            ac.wait_ge(rhs_step.handle, rhs_step.at(i, c * SEQS * LEVELS + level * SEQS + s + 1))
                            if level == LEVELS - 1:
                                act(upd[s][:], rhs_ps[s][:, 0:H * DV], ACT.Copy).then_inc(upd_done.handle, 1)
                                continue
                            act(rhs[s][:, 0, :], rhs_ps[s][:, 0:H * DV], ACT.Copy).then_inc(rhs_hi.handle, 1)
                            ac.wait_ge(powT_step.handle, powT_step.at(i, c * SEQS * (LEVELS - 1) + level * SEQS + s + 1))
                            act(powerT[s][new][:, 0, :], powT_ps[s][:], ACT.Copy).then_inc(powT_hi.handle, 1)
                            if level < LEVELS - 2:
                                ac.wait_ge(pow_step.handle, pow_step.at(i, c * SEQS * (LEVELS - 2) + level * SEQS + s + 1))
                                act(power[s][new][:, 0, :], pow_ps[s][:], ACT.Copy).then_inc(pow_hi.handle, 1)
                    for s in range(SEQS):
                        t, n = 2 * s + c, 2 * c + s
                        if c == 0:
                            ac.wait_ge(state_ps.handle, state_ps.at(i, s + 1))
                            act(state[s][:, 0, :], rhs_ps[s][:, 0:H * DV], ACT.Copy).then_inc(state_hi.handle, 1)
                        ac.wait_ge(o_ps.handle, o_ps.at(i, n + 1))
                        act(o[:, t, :], misc_ps[s][:, 0:H * DV], ACT.Copy).then_inc(o_out.handle, 1)
                ac.wait_ge(o_out.handle, o_out.at(i, TB))
                act(osq[:], o[:].rearrange("p t n -> p (t n)"), ACT.Square).then_inc(osq_done.handle, 1)
                ac.wait_ge(oss_done.handle, oss_done.at(i, 1))
                act(ostd[:], oss[:], ACT.Sqrt, bias=eps[:, 0:1], scale=1.0 / DV).then_inc(ostd_done.handle, 1)
                ac.wait_ge(oT_ps.handle, oT_ps.at(i, 1))
                act(oT[:, 0, :], misc_ps[0][:], ACT.Copy).then_inc(oT_hi.handle, 1)
                ac.wait_ge(s_ps.handle, s_ps.at(i, 1))
                ac.wait_ge(s_stored.handle, s_stored.before(i))
                act(sT[:], misc_ps[1][:], ACT.Copy).then_inc(s_copied.handle, 1)
                ac.wait_ge(s_copied.handle, s_copied.at(i, 1))
                ac.dma_start(s_out[:, bass.ts(i, TILE)], sT[:]).then_inc(s_stored.handle, 16)

        @block.vector
        def _(ve):
            vec = nc.vector
            vec.memset(eps[:, 0:1], EPS).then_inc(order.handle, 1)
            vec.memset(eps[:, 1:2], 1e-12).then_inc(order.handle, 1)
            ve.wait_ge(w_ready.handle, 2)
            ve.wait_ge(const_in.handle, 16 * 8)
            vec.tensor_tensor(w_pair[:, 1, :], stage[:], w_pair[:, 0, :], ALU.subtract).then_inc(w_ready.handle, 1)

            def low(out, exact, high):
                return vec.tensor_tensor(out, exact, high, ALU.subtract)

            with ve.Fori(0, turns) as i:
                ve.wait_ge(x_loaded.handle, x_loaded.at(i, 16))
                for t in range(TB):
                    last = vec.bn_stats(stats[:, t, :], x_in[:, t, :])
                last.then_inc(stats_done.handle, 1)
                ve.wait_ge(stats_done.handle, stats_done.at(i, 1))
                ve.sem_inc(order.handle, 1)
                for t in range(TB):
                    last = vec.bn_aggr(mean_var[:, t, :], stats[:, t, :])
                last.then_inc(aggr_done.handle, 1)
                ve.wait_ge(std_done.handle, std_done.at(i, 1))
                vec.reciprocal(rstd[:], std[:]).then_inc(rstd_done.handle, 1)
                ve.wait_ge(rstd_done.handle, rstd_done.at(i, 1))
                ve.wait_ge(xn_stored.handle, xn_stored.before(i))
                for t in range(TB):
                    last = vec.tensor_scalar(xn[:, t, :], x_in[:, t, :], mean_var[:, t, 0:1], rstd[:, t:t + 1],
                                             ALU.subtract, ALU.mult)
                last.then_inc(xn_done.handle, 1)
                ve.wait_ge(xT_hi.handle, xT_hi.at(i, 1))
                low(xT[:, 1, :], misc_ps[0][:], xT[:, 0, :]).then_inc(xT_lo.handle, 1)
                for t in range(TB):
                    ve.wait_ge(ksq_done.handle, ksq_done.at(i, t + 1))
                    last = vec.tensor_reduce(kss[:, t * H:(t + 1) * H], ksq[:, t, :].rearrange("p (h d) -> p h d", h=H),
                                             AX, ALU.add)
                last.then_inc(kss_done.handle, 1)
                ve.wait_ge(knorm_done.handle, knorm_done.at(i, 1))
                vec.reciprocal(krn[:], knorm[:]).then_inc(krn_done.handle, 1)
                ve.wait_ge(krn_done.handle, krn_done.at(i, 1))
                for t in range(TB):
                    vec.tensor_tensor(khat[:, t, :].rearrange("p (h d) -> p h d", h=H),
                                      prep[t][:].rearrange("p (h d) -> p h d", h=H),
                                      over(krn[:, t * H:(t + 1) * H], DK, 2), ALU.mult).then_inc(khat_done.handle, 1)
                ve.wait_ge(g_sig.handle, g_sig.at(i, TB))
                vec.tensor_scalar(neg_beta[:], beta[:], -1.0, None, ALU.mult).then_inc(negb_done.handle, 1)
                for t in range(TB):
                    ve.wait_ge(kT_hi.handle, kT_hi.at(i, t + 1))
                    low(kT[:, 1, t, :], prep[t][:], kT[:, 0, t, :]).then_inc(kT_lo.handle, 1)
                for h in range(H):
                    ve.wait_ge(q_hi.handle, q_hi.at(i, h + 1))
                    vec.scalar_tensor_tensor(out=qT[:, 1, h, :], in0=rhs_ps[h % 2][:], scalar=SCALE, in1=qT[:, 0, h, :],
                                             op0=ALU.mult, op1=ALU.subtract).then_inc(q_lo.handle, 1)
                for c in range(2):
                    for s in range(SEQS):
                        t, n = 2 * s + c, 2 * c + s
                        bt = over(beta[:, t, :], DV, 2)
                        r3 = rhs32[s][:].rearrange("p (h d) -> p h d", h=H)
                        v3 = v[:, t, :].rearrange("p (h d) -> p h d", h=H)
                        ve.wait_ge(gram_ps.handle, gram_ps.at(i, n + 1))
                        if c == 0 and s == 0:
                            ve.wait_ge(negb_done.handle, negb_done.at(i, 1))
                        for h in range(H):
                            last = vec.scalar_tensor_tensor(out=b32[s][:, h * P:(h + 1) * P],
                                                            in0=pow_ps[s][:, h * P:(h + 1) * P],
                                                            scalar=neg_beta[:, t, h:h + 1], in1=below_m[:],
                                                            op0=ALU.mult, op1=ALU.mult)
                        last.then_inc(b32_done.handle, 1)
                        if c == 0:
                            vec.tensor_tensor(r3, v3, bt, ALU.mult).then_inc(rhs32_done.handle, 1)
                        else:
                            ve.wait_ge(ks_ps.handle, ks_ps.at(i, s + 1))
                            vec.tensor_tensor(rhs32[s][:], v[:, t, :], rhs_ps[s][:, 0:H * DV], ALU.subtract)\
                               .then_inc(rhs_sub.handle, 1)
                            ve.wait_ge(rhs_sub.handle, rhs_sub.at(i, s + 1))
                            vec.tensor_tensor(r3, r3, bt, ALU.mult).then_inc(rhs32_done.handle, 1)
                        ve.wait_ge(qk_ps.handle, qk_ps.at(i, n + 1))
                        vec.tensor_tensor(qk[s][:].rearrange("p (h n) -> p h n", h=H),
                                          powT_ps[s][:].rearrange("p (h n) -> p h n", h=H),
                                          over(upto_m[:], H), ALU.mult).then_inc(qk_done.handle, 1)
                        ve.wait_ge(b_hi.handle, b_hi.at(i, n + 1))
                        low(power[s][0][:, 1, :], b32[s][:], power[s][0][:, 0, :]).then_inc(b_lo.handle, 1)
                        ve.wait_ge(rhs_hi.handle, rhs_hi.at(i, c * SEQS * LEVELS + s + 1))
                        low(rhs[s][:, 1, :], rhs32[s][:], rhs[s][:, 0, :]).then_inc(rhs_lo.handle, 1)
                    for level in range(LEVELS - 1):
                        new = (level + 1) % 2
                        for s in range(SEQS):
                            ve.wait_ge(rhs_hi.handle, rhs_hi.at(i, c * SEQS * LEVELS + (level + 1) * SEQS + s + 1))
                            low(rhs[s][:, 1, :], rhs_ps[s][:, 0:H * DV], rhs[s][:, 0, :]).then_inc(rhs_lo.handle, 1)
                            ve.wait_ge(powT_hi.handle, powT_hi.at(i, c * SEQS * (LEVELS - 1) + level * SEQS + s + 1))
                            low(powerT[s][new][:, 1, :], powT_ps[s][:], powerT[s][new][:, 0, :])\
                                .then_inc(powT_lo.handle, 1)
                            if level < LEVELS - 2:
                                ve.wait_ge(pow_hi.handle, pow_hi.at(i, c * SEQS * (LEVELS - 2) + level * SEQS + s + 1))
                                low(power[s][new][:, 1, :], pow_ps[s][:], power[s][new][:, 0, :])\
                                    .then_inc(pow_lo.handle, 1)
                    if c == 0:
                        for s in range(SEQS):
                            ve.wait_ge(state_hi.handle, state_hi.at(i, s + 1))
                            low(state[s][:, 1, :], rhs_ps[s][:, 0:H * DV], state[s][:, 0, :])\
                                .then_inc(state_lo.handle, 1)
                ve.wait_ge(osq_done.handle, osq_done.at(i, 1))
                vec.tensor_reduce(oss[:], osq[:].rearrange("p (n d) -> p n d", d=DV), AX, ALU.add)\
                   .then_inc(oss_done.handle, 1)
                ve.wait_ge(ostd_done.handle, ostd_done.at(i, 1))
                vec.reciprocal(orn[:], ostd[:]).then_inc(orn_done.handle, 1)
                ve.wait_ge(orn_done.handle, orn_done.at(i, 1))
                ve.wait_ge(gate_done.handle, gate_done.at(i, 1))
                vec.tensor_tensor(og[:].rearrange("p (n d) -> p n d", d=DV),
                                  o[:].rearrange("p t (h d) -> p (t h) d", d=DV), over(orn[:], DV, 2), ALU.mult)\
                   .then_inc(on_done.handle, 1)
                ve.wait_ge(on_done.handle, on_done.at(i, 1))
                vec.tensor_tensor(og[:], og[:], gate[:].rearrange("p t n -> p (t n)"), ALU.mult)\
                   .then_inc(og_done.handle, 1)
                ve.wait_ge(oT_hi.handle, oT_hi.at(i, 1))
                low(oT[:, 1, :], misc_ps[0][:], oT[:, 0, :]).then_inc(oT_lo.handle, 1)

        @block.gpsimd
        def _(po):
            with po.Fori(0, turns) as i:
                po.wait_ge(g_sig.handle, g_sig.at(i, TB))
                nc.gpsimd.tensor_tensor(gate[:], gate[:], g[:], ALU.mult).then_inc(gate_half.handle, 1)
                po.wait_ge(gate_half.handle, gate_half.at(i, 1))
                nc.gpsimd.tensor_tensor(gate[:].rearrange("p t (h d) -> p (t h) d", d=DV),
                                        gate[:].rearrange("p t (h d) -> p (t h) d", d=DV),
                                        over(norm_row[:], TB * H), ALU.mult).then_inc(gate_done.handle, 1)


def attention_phase(nc, xn_in, qk_w, qk_b, v_w, v_b, o_w, o_b, gamma1, gamma2, theta, position, half_sign,
                    eye, future, an_out, rest_out, turns):
    HEADS, HD, PAIRS = 16, 64, 8
    xn_v = xn_in.rearrange("(n t p) d -> n p t d", t=TB, p=P)
    TWO_PI = 6.283185307179586
    C1 = 6.28125
    C2 = float(np.float32(np.round((TWO_PI - C1) * 2 ** 21) / 2 ** 21))
    C3 = TWO_PI - C1 - C2
    ROUND = 1.5 * 2.0 ** 23
    UNITS = PAIRS * SEQS * 2
    NP = 2 * PAIRS
    RING = 4
    LAST = turns - 1
    CLOSE_O, CLOSE_SQUARE, CLOSE_SUM, ROOTS, RECIPROCALS, SCALES = 7, 9, 11, 12, 13, 14
    TURN_X, X_SPLIT = 19, 23
    V_SLOTS = {25: 0, 27: 1, 29: 2, 31: 3, 5: 4, 9: 5, 13: 6, 15: 7}

    with ExitStack() as ctx:
        m = Memory(nc, ctx, "attn")
        eye32, future_m = m.sbuf("eye32", [P, P]), m.sbuf("future32", [P, P])
        eyeb, futureb = m.sbuf("eyeb", [P, P], BF16), m.sbuf("futureb", [P, P], BF16)
        ones = m.sbuf("ones", [P, P])
        eps = m.sbuf("eps", [P, 1])
        gam1, gam2, ob = m.sbuf("gam1", [P, 1]), m.sbuf("gam2", [P, 1]), m.sbuf("ob", [P, 1])
        vb = m.sbuf("vb", [P, PAIRS])
        qkb = m.sbuf("qkb", [P, 4, PAIRS])
        th, sign = m.sbuf("th", [P, 1]), m.sbuf("sign", [P, 1])
        pos = m.sbuf("pos", [P, SEQ])
        ang = [m.sbuf(f"ang{k}", [P, SEQ]) for k in range(4)]
        table = m.sbuf("table", [P, 2, 2, SEQ])
        stage = m.sbuf("w_stage", [P, 2048])
        qkw = m.sbuf("qkw", [P, 2, 4 * 1024], F16)
        vw = m.sbuf("vw", [P, 2, 1024], F16)
        ow = m.sbuf("ow", [P, 2, 1024], F16)

        xn = m.sbuf("xn", [P, TB, P])
        sq = m.sbuf("sq", [P, TB * P])
        ss = m.sbuf("ss", [P, TB])
        std, rr = m.sbuf("std", [P, 2 * TB]), m.sbuf("rr", [P, 2 * TB])
        x2 = m.sbuf("x2", [P, TB, P])
        x2T, res = m.sbuf("x2T", [P, TILE]), m.sbuf("res", [P, TILE])
        xT = m.sbuf("xT", [P, 2, TILE], F16)
        V = m.sbuf("V", [P, TB, HEADS, HD + 1])
        rope1 = [m.sbuf(f"rope1{w}", [P, TILE]) for w in range(2)]
        rope2 = [m.sbuf(f"rope2{w}", [P, TILE]) for w in range(2)]
        rot = [m.sbuf(f"rot{w}", [P, TILE]) for w in range(2)]
        qk = [[m.sbuf(f"qk{w}_{k}", [P, 2, TILE], F16) for k in range(RING)] for w in range(2)]
        nmax = [m.sbuf(f"nmax{k}", [P, 3]) for k in range(RING)]
        prob = [m.sbuf(f"prob{k}", [P, 384]) for k in range(RING)]
        probT = [m.sbuf(f"probT{k}", [P, 384]) for k in range(RING)]
        rden = m.sbuf("rden", [P, SEQS, 4])
        ctxn = [m.sbuf(f"ctxn{k}", [P, SEQS, 2, P]) for k in range(2)]
        ctxT = m.sbuf("ctxT", [P, 2, PAIRS, TILE], F16)
        attn = m.sbuf("attn", [P, TILE])
        asq = m.sbuf("asq", [P, TILE])
        diag = m.sbuf("diag", [P, TILE])
        an = m.sbuf("an", [P, TILE])
        rest = m.sbuf("rest", [P, TILE])

        (pa, pb), sc, pt, cx = m.banks("proj", 2), m.banks("score", 2), m.banks("probT", 2), m.banks("ctx", 2)

        S = m.count
        const_in, stage_in, stage_hi, w_ready = S("const_in"), S("stage_in"), S("stage_hi"), S("w_ready")
        ready, table_done = S("ready"), S("table_done")
        tab, act_tab = S("tab"), S("act_tab")
        x_loaded = S("x_loaded", 16)
        sq_done, ss_done, std_done, rr_done, x2_done = S("sq_done"), S("ss_done"), S("std_done"), S("rr_done"), S("x2_done")
        x2_ps, x2T_done, res_done, xT_hi, xT_lo = S("x2_ps"), S("x2T_done"), S("res_done"), S("xT_hi"), S("xT_lo")
        v_ps, v_out = S("v_ps", 2 * TB), S("v_out", 2 * TB)
        a_ps, a_rope = S("a_ps", 2 * PAIRS), S("a_rope", 2 * PAIRS)
        b_ps, b_rope = S("b_ps", 2 * PAIRS), S("b_rope", 2 * PAIRS)
        rot_done, qk_hi, qk_lo = S("rot_done", 2 * PAIRS), S("qk_hi", 2 * PAIRS), S("qk_lo", 2 * PAIRS)
        sc_ps, max_done, nmax_done, exp_done = S("sc_ps", UNITS), S("max_done", UNITS), S("nmax_done", UNITS), S("exp_done", UNITS)
        pt_ps = S("pt_ps", UNITS)
        pt_even, pt_odd = S("pt_even", UNITS // 2), S("pt_odd", UNITS // 2)
        pv_done, rden_done, norm_done = S("pv_done", UNITS), S("rden_done", UNITS // 2), S("norm_done", UNITS // 2)
        ct_ps, ct_hi, ct_lo = S("ct_ps", PAIRS), S("ct_hi", PAIRS), S("ct_lo", PAIRS)
        o_ps, attn_done, asq_done = S("o_ps"), S("attn_done"), S("asq_done")
        asum_ps, diag_done = S("asum_ps"), S("diag_done")
        bc_ps, an_done, rest_done, stored = S("bc_ps"), S("an_done"), S("rest_done"), S("stored", 32, 32)

        block = ctx.enter_context(nc.Block())
        consts = [(eye32, eye), (future_m, future), (gam1, gamma1.rearrange("(p a) -> p a", a=1)),
                  (gam2, gamma2.rearrange("(p a) -> p a", a=1)), (ob, o_b.rearrange("(p a) -> p a", a=1)),
                  (vb, v_b), (qkb, qk_b), (th, theta), (sign, half_sign),
                  (pos, position.to_broadcast([P, SEQ]))]
        loads = [(qk_w[:, 0:2048], qkw[:, :, 0:2048]), (qk_w[:, 2048:4096], qkw[:, :, 2048:4096]),
                 (v_w, vw[:]), (o_w.rearrange("(j p) n -> p j n", p=P), ow[:])]

        @block.sync
        def _(sp):
            for dst, src in consts:
                sp.dma_start(dst[:], src).then_inc(const_in.handle, 16)
            for n, (src, dst) in enumerate(loads):
                if n:
                    sp.wait_ge(w_ready.handle, n)
                width = dst.shape[2]
                to = stage[:, 0:width]
                if len(src.shape) == 3:
                    to = to.rearrange("p (j n) -> p j n", j=PAIRS)
                sp.dma_start(to, src).then_inc(stage_in.handle, 16)
            sp.sem_inc(stored.handle, 32)

            def load(k):
                sp.dma_start(xn[:], xn_v[k]).then_inc(x_loaded.handle, 16)

            def store(k):
                sp.wait_ge(rest_done.handle, rest_done.at(k, 1))
                sp.dma_start(an_out[:, bass.ts(k, TILE)], an[:]).then_inc(stored.handle, 16)
                sp.dma_start(rest_out[:, bass.ts(k, TILE)], rest[:]).then_inc(stored.handle, 16)

            load(0)
            sp.wait_ge(x2_done.handle, x2_done.at(0, 1))
            load(1)
            with sp.Fori(1, LAST) as i:
                sp.wait_ge(x2_done.handle, x2_done.at(i, 1))
                load(i + 1)
                store(i - 1)
            store(LAST - 1)
            store(LAST)
            sp.wait_ge(stored.handle, 32 * (turns + 1))

        def turn_by_turn(eng, body):
            body(-1, now=False, ahead=True, behind=False)
            body(0, now=True, ahead=True, behind=False)
            with eng.Fori(1, LAST) as i:
                body(i, now=True, ahead=True, behind=True)
            body(LAST, now=True, ahead=False, behind=True)
            body(turns, now=False, ahead=False, behind=True)

        def made(n, now, ahead, behind, per):
            return behind if n < 0 else now if n < per else ahead

        def projection(u):
            return 2 * (u // 4 + 2) + u % 4 // 2

        def values_before(u):
            return V_SLOTS[u % UNITS] + (2 * TB if u > UNITS // 2 else 0)

        def head(w, j, s, hh, t0, t1):
            buf, a = qk[w][j % RING], s * SEQ
            return buf[hh * HD:(hh + 1) * HD, 0, a + t0:a + t1], buf[hh * HD:(hh + 1) * HD, 1, a + t0:a + t1]

        @block.tensor
        def _(te):
            pe = nc.tensor
            te.wait_ge(w_ready.handle, len(loads))
            te.wait_ge(ready.handle, 5)
            xs = (xT[:, 0, :], xT[:, 1, :])

            def body(i, now, ahead, behind):

                def project(u):
                    n = projection(u)
                    if now or n > NP:
                        te.wait_ge(b_rope.handle, b_rope.at(i, n))
                    if u % 4 == 2 and made(u // 4 - 2, now, ahead, behind, PAIRS):
                        te.wait_ge(ct_lo.handle, ct_lo.at(i, u // 4 - 1))
                    if u == CLOSE_O + 1 and behind:
                        te.wait_ge(attn_done.handle, attn_done.at(i, 0))
                    if u == ROOTS and behind:
                        te.wait_ge(std_done.handle, std_done.at(i + 1, 1))
                    if u == TURN_X + 1 and ahead:
                        te.wait_ge(x2T_done.handle, x2T_done.at(i + 1, 1))
                    if u == TURN_X + 1 and behind:
                        te.wait_ge(an_done.handle, an_done.at(i, 0))
                    if (u - 1) % UNITS in V_SLOTS and (now or u > UNITS // 2):
                        te.wait_ge(v_out.handle, v_out.at(i, values_before(u - 1) + 1))
                    if n == NP:
                        te.wait_ge(xT_lo.handle, xT_lo.at(i + 1, 1))
                    w, j = n % 2, n // 2 % PAIRS
                    for kind, bank, done in ((2 * w, pa, a_ps), (2 * w + 1, pb, b_ps)):
                        at = kind * 1024 + j * P
                        split_product(pe, bank[:], (qkw[:, 0, at:at + P], qkw[:, 1, at:at + P]), xs).then_inc(done.handle, 1)

                def values(u):
                    half, t = V_SLOTS[u] // TB, V_SLOTS[u] % TB
                    te.wait_ge(b_rope.handle, b_rope.at(i, projection(u - 1) + 1))
                    split_product(pe, pb[:], (xT[:, 0, t * P:(t + 1) * P], xT[:, 1, t * P:(t + 1) * P]),
                                  (vw[:, 0, half * 512:(half + 1) * 512], vw[:, 1, half * 512:(half + 1) * 512]))\
                        .then_inc(v_ps.handle, 1)

                def scores(u):
                    j, s, hh = u // 4, u // 2 % 2, u % 2
                    bank = sc[u % 2]
                    if u % 4 == 0:
                        te.wait_ge(qk_lo.handle, qk_lo.at(i, 2 * j + 2))
                    if behind or u >= 2:
                        te.wait_ge(exp_done.handle, exp_done.at(i, u - 1))
                    split_product(pe, bank[:, 0:128], head(0, j, s, hh, 0, 128), head(1, j, s, hh, 0, 128), stop=False)
                    pe.matmul(bank[:, 0:128], eyeb[:], futureb[:], start=False, stop=True, skip_group_check=True)
                    split_product(pe, bank[:, 128:384], head(0, j, s, hh, 128, 256), head(1, j, s, hh, 0, 256), stop=False)
                    pe.matmul(bank[:, 256:384], eyeb[:], futureb[:], start=False, stop=True, skip_group_check=True)\
                        .then_inc(sc_ps.handle, 1)

                def turn_over(v):
                    te.wait_ge(exp_done.handle, exp_done.at(i, v + 1))
                    if behind or v >= 2:
                        read = (pt_even, pt_odd)[v % 2]
                        te.wait_ge(read.handle, read.at(i, v // 2))
                    for k in range(3):
                        last = pe.transpose(pt[v % 2][:, k * P:(k + 1) * P], prob[v % RING][:, k * P:(k + 1) * P], eye32[:])
                    last.then_inc(pt_ps.handle, 1)

                def mix(v):
                    v_abs = v % UNITS
                    j, s, hh = v_abs // 4, v_abs // 2 % 2, v_abs % 2
                    h = 2 * j + hh
                    read = (pt_even, pt_odd)[v % 2]
                    te.wait_ge(read.handle, read.at(i, v // 2 + 1))
                    if v in (0, UNITS // 2):
                        te.wait_ge(v_out.handle, v_out.at(i, TB if v == 0 else 2 * TB))
                    if hh == 0 and (behind or v >= 4):
                        te.wait_ge(norm_done.handle, norm_done.at(i, 2 * (v // 4) + s - 1))
                    W = HD + 1
                    o0, o1 = (cx[s][:, (2 * hh + b) * W:(2 * hh + b + 1) * W] for b in range(2))
                    pT = probT[v % RING]
                    pe.matmul(o0, pT[:, 0:128], V[:, 2 * s, h, :], start=True, stop=True, skip_group_check=True)
                    pe.matmul(o1, pT[:, 128:256], V[:, 2 * s, h, :], start=True, stop=False, skip_group_check=True)
                    pe.matmul(o1, pT[:, 256:384], V[:, 2 * s + 1, h, :], start=False, stop=True,
                              skip_group_check=True).then_inc(pv_done.handle, 1)

                def turn_ctx(u, j):
                    te.wait_ge(norm_done.handle, norm_done.at(i, 2 * j + 2))
                    if made(projection(u - 1), now, ahead, behind, NP):
                        te.wait_ge(a_rope.handle, a_rope.at(i, projection(u - 1) + 1))
                    else:
                        te.wait_ge(ct_lo.handle, ct_lo.at(i, j))
                    for s in range(SEQS):
                        for b in range(2):
                            at = (2 * s + b) * P
                            last = pe.transpose(pa[:, at:at + P], ctxn[j % 2][:, s, b, :], eye32[:])
                    last.then_inc(ct_ps.handle, 1)

                for u in range(UNITS):
                    if now:
                        scores(u)
                    if made(u - 2, now, ahead, behind, UNITS):
                        turn_over(u - 2)
                    if made(u - 4, now, ahead, behind, UNITS):
                        mix(u - 4)
                    if u % 2 == 0 and made(projection(u), now, ahead, behind, NP) and (now or u >= TURN_X):
                        project(u)
                    if u % 4 == 1 and made(u // 4 - 2, now, ahead, behind, PAIRS):
                        turn_ctx(u, u // 4 - 2)
                    if u in V_SLOTS and (ahead if V_SLOTS[u] < TB else now):
                        values(u)
                    if u in (CLOSE_O, CLOSE_SUM, TURN_X) and now:
                        te.wait_ge(b_rope.handle, b_rope.at(i, projection(u - 1) + 1))
                    if u == CLOSE_O and behind:
                        te.wait_ge(ct_lo.handle, ct_lo.at(i, 0))
                        for j in range(PAIRS):
                            last = split_product(pe, pa[:], (ow[:, 0, j * P:(j + 1) * P], ow[:, 1, j * P:(j + 1) * P]),
                                                 (ctxT[:, 0, j, :], ctxT[:, 1, j, :]), start=(j == 0), stop=(j == PAIRS - 1))
                        last.then_inc(o_ps.handle, 1)
                    if u == CLOSE_SUM and behind:
                        te.wait_ge(asq_done.handle, asq_done.at(i, 0))
                        for t in range(TB):
                            last = pe.matmul(pa[:, t:t + 1], asq[:, t * P:(t + 1) * P], ones[:, 0:1], start=True, stop=True)
                        last.then_inc(asum_ps.handle, 1)
                    if u == TURN_X and ahead:
                        te.wait_ge(x2_done.handle, x2_done.at(i + 1, 1))
                        for t in range(TB):
                            last = pe.transpose(pa[:, t * P:(t + 1) * P], x2[:, t, :], eye32[:])
                        last.then_inc(x2_ps.handle, 1)
                    if u == TURN_X and behind:
                        te.wait_ge(diag_done.handle, diag_done.at(i, 0))
                        pe.matmul(pb[:], ones[:], diag[:], start=True, stop=True).then_inc(bc_ps.handle, 1)

            turn_by_turn(te, body)

        @block.scalar
        def _(ac):
            act = nc.scalar.activation
            ac.wait_ge(const_in.handle, 16 * len(consts))
            act(eyeb[:], eye32[:], ACT.Copy).then_inc(ready.handle, 1)
            act(futureb[:], future_m[:], ACT.Copy).then_inc(ready.handle, 1)
            for n, (src, dst) in enumerate(loads):
                ac.wait_ge(stage_in.handle, 16 * (n + 1))
                act(dst[:, 0, :], stage[:, 0:dst.shape[2]], ACT.Copy).then_inc(stage_hi.handle, 1)
            ac.wait_ge(tab.handle, 10)
            act(ang[2][:], ang[2][:], ACT.Sin).then_inc(act_tab.handle, 1)
            act(ang[3][:], ang[3][:], ACT.Sin).then_inc(act_tab.handle, 1)
            ac.wait_ge(ready.handle, 5)

            def body(i, now, ahead, behind):

                def rope_high(n):
                    j = n // 2
                    ac.wait_ge(rot_done.handle, rot_done.at(i, n + 1))
                    if (now and j >= RING) or behind:
                        ac.wait_ge(sc_ps.handle, sc_ps.at(i, 4 * (j - RING + 1)))
                    act(qk[n % 2][j % RING][:, 0, :], rot[n % 2][:], ACT.Copy).then_inc(qk_hi.handle, 1)

                def values_out(u):
                    half, t = V_SLOTS[u % UNITS] // TB, V_SLOTS[u % UNITS] % TB
                    n = values_before(u)
                    ac.wait_ge(v_ps.handle, v_ps.at(i, n + 1))
                    if n == 2 * TB and now:
                        ac.wait_ge(pv_done.handle, pv_done.at(i, UNITS // 2))
                    if n == TB and behind:
                        ac.wait_ge(pv_done.handle, pv_done.at(i, 0))
                    act(V[:, t, half * 8:(half + 1) * 8, 0:HD], pb[:].rearrange("p (h d) -> p h d", d=HD), ACT.Copy)\
                        .then_inc(v_out.handle, 1)

                for u in range(UNITS):
                    j = u // 4
                    if u % 2 == 1 and made(u - 3, now, ahead, behind, UNITS):
                        ac.wait_ge(pt_ps.handle, pt_ps.at(i, u - 2))
                        if behind or u - 3 >= RING:
                            ac.wait_ge(pv_done.handle, pv_done.at(i, u - 2 - RING))
                        act(probT[(u - 3) % RING][:], pt[0][:, 0:384], ACT.Copy).then_inc(pt_even.handle, 1)
                    if u % 4 == 3 and made(2 * j + 4, now, ahead, behind, NP) and (now or u > TURN_X):
                        rope_high(2 * j + 4)
                    if u % 4 == 1 and made(2 * j + 3, now, ahead, behind, NP) and (now or u > 25):
                        rope_high(2 * j + 3)
                    if u == TURN_X + 1 and ahead:
                        ac.wait_ge(x2_ps.handle, x2_ps.at(i + 1, 1))
                        if now:
                            ac.wait_ge(res_done.handle, res_done.at(i, 1))
                        act(x2T[:], pa[:], ACT.Copy, scale=gam1[:]).then_inc(x2T_done.handle, 1)
                    if (u - 1) % UNITS in V_SLOTS and (now if u <= UNITS // 2 else ahead):
                        values_out(u - 1)
                    if u % 4 == 2 and made(j - 2, now, ahead, behind, PAIRS):
                        ac.wait_ge(ct_ps.handle, ct_ps.at(i, j - 1))
                        if j == 2 and behind:
                            ac.wait_ge(o_ps.handle, o_ps.at(i, 0))
                        act(ctxT[:, 0, (j - 2) % PAIRS, :], pa[:], ACT.Identity, bias=vb[:, (j - 2) % PAIRS:(j - 2) % PAIRS + 1])\
                            .then_inc(ct_hi.handle, 1)
                    if u == X_SPLIT and ahead:
                        ac.wait_ge(x2T_done.handle, x2T_done.at(i + 1, 1))
                        if now:
                            ac.wait_ge(b_ps.handle, b_ps.at(i, NP))
                        act(xT[:, 0, :], x2T[:], ACT.Copy).then_inc(xT_hi.handle, 1)
                    if now:
                        v = u % RING
                        ac.wait_ge(nmax_done.handle, nmax_done.at(i, u + 1))
                        if behind or u >= RING:
                            ac.wait_ge(pt_ps.handle, pt_ps.at(i, u - RING + 1))
                        act(prob[v][:, 0:128], sc[u % 2][:, 0:128], ACT.Exp, bias=nmax[v][:, 0:1])
                        act(prob[v][:, 128:384], sc[u % 2][:, 128:384], ACT.Exp, bias=nmax[v][:, 1:2])\
                            .then_inc(exp_done.handle, 1)
                    if u == CLOSE_SQUARE and behind:
                        ac.wait_ge(attn_done.handle, attn_done.at(i, 0))
                        act(asq[:], attn[:], ACT.Square).then_inc(asq_done.handle, 1)
                    if u == CLOSE_SQUARE and ahead:
                        ac.wait_ge(x_loaded.handle, x_loaded.at(i + 1, 16))
                        act(sq[:], xn[:].rearrange("p t d -> p (t d)"), ACT.Square).then_inc(sq_done.handle, 1)
                    if u == ROOTS:
                        if ahead:
                            ac.wait_ge(ss_done.handle, ss_done.at(i + 1, 1))
                            last = act(std[:, 0:TB], ss[:], ACT.Sqrt, bias=eps[:], scale=1.0 / P)
                        if behind:
                            ac.wait_ge(asum_ps.handle, asum_ps.at(i, 0))
                            last = act(std[:, TB:], pa[:, 0:TB], ACT.Sqrt, bias=eps[:], scale=1.0 / P)
                        last.then_inc(std_done.handle, 1)

            turn_by_turn(ac, body)

        @block.vector
        def _(ve):
            vec = nc.vector
            vec.memset(eps[:], EPS).then_inc(ready.handle, 1)
            vec.memset(ones[:], 1.0).then_inc(ready.handle, 1)
            vec.memset(V[:, :, :, HD:HD + 1], 1.0).then_inc(ready.handle, 1)
            for n, (src, dst) in enumerate(loads):
                ve.wait_ge(stage_hi.handle, n + 1)
                vec.tensor_tensor(dst[:, 1, :], stage[:, 0:dst.shape[2]], dst[:, 0, :], ALU.subtract)\
                   .then_inc(w_ready.handle, 1)
            ve.wait_ge(const_in.handle, 16 * len(consts))

            def step(ins):
                step.n += 1
                ins.then_inc(tab.handle, 1)
                ve.wait_ge(tab.handle, step.n)

            step.n = 0
            turns_of, red, sine, cosine = ang
            step(vec.tensor_scalar(red[:], pos[:], th[:], None, ALU.mult))
            step(vec.tensor_scalar(turns_of[:], red[:], 1.0 / TWO_PI, None, ALU.mult))
            step(vec.tensor_scalar(turns_of[:], turns_of[:], ROUND, None, ALU.add))
            step(vec.tensor_scalar(turns_of[:], turns_of[:], -ROUND, None, ALU.add))
            for part in (C1, C2, C3):
                step(vec.scalar_tensor_tensor(out=red[:], in0=turns_of[:], scalar=-part, in1=red[:], op0=ALU.mult, op1=ALU.add))
            step(vec.tensor_scalar(sine[:], red[:], 3.1415925, -3.1415925, ALU.min, ALU.max))
            step(vec.scalar_tensor_tensor(out=cosine[:], in0=sine[:], scalar=-1.0, in1=sine[:], op0=ALU.mult, op1=ALU.max))
            step(vec.tensor_scalar(cosine[:], cosine[:], -1.0, TWO_PI / 4, ALU.mult, ALU.add))
            ve.wait_ge(act_tab.handle, 2)
            scale = 1.0 / HD ** 0.5
            vec.tensor_scalar(table[:, 1, 0, :], cosine[:], 1.0, None, ALU.mult).then_inc(table_done.handle, 1)
            vec.tensor_scalar(table[:, 0, 0, :], cosine[:], scale, None, ALU.mult).then_inc(table_done.handle, 1)
            vec.tensor_scalar(table[:, 1, 1, :], sine[:], sign[:], None, ALU.mult).then_inc(table_done.handle, 1)
            vec.tensor_scalar(table[:, 0, 1, :], sine[:], sign[:], scale, ALU.mult, ALU.mult).then_inc(table_done.handle, 1)
            ve.wait_ge(table_done.handle, 4)

            def body(i, now, ahead, behind):

                def rope(n):
                    w, j = n % 2, n // 2 % PAIRS
                    for kind, bank, out, got, done in ((0, pa, rope1, a_ps, a_rope), (1, pb, rope2, b_ps, b_rope)):
                        ve.wait_ge(got.handle, got.at(i, n + 1))
                        if kind == 0 and (now or n >= NP + 2):
                            ve.wait_ge(rot_done.handle, rot_done.at(i, n - 1))
                        vec.scalar_tensor_tensor(out=out[w][:].rearrange("p (s n) -> p s n", s=SEQS),
                                                 in0=bank[:].rearrange("p (s n) -> p s n", s=SEQS),
                                                 scalar=qkb[:, 2 * w + kind, j:j + 1], in1=over(table[:, w, kind, :], SEQS),
                                                 op0=ALU.add, op1=ALU.mult).then_inc(done.handle, 1)

                def normalise(k):
                    j, s = k // 2, k % 2
                    ve.wait_ge(pv_done.handle, pv_done.at(i, 2 * k + 2))
                    got = cx[s][:, 0:4 * (HD + 1)].rearrange("p (h b d) -> p h b d", h=2, b=2)
                    vec.reciprocal(rden[:, s, :].rearrange("p (h b a) -> p h b a", h=2, a=1), got[:, :, :, HD:HD + 1])\
                       .then_inc(rden_done.handle, 1)
                    ve.wait_ge(rden_done.handle, rden_done.at(i, k + 1))
                    if s == 0 and (behind or j >= 2):
                        ve.wait_ge(ct_ps.handle, ct_ps.at(i, j - 1))
                    vec.tensor_tensor(ctxn[j % 2][:, s, :, :].rearrange("p b (h d) -> p h b d", h=2), got[:, :, :, 0:HD],
                                      over(rden[:, s, :].rearrange("p (h b) -> p h b", h=2), HD, 3), ALU.mult)\
                       .then_inc(norm_done.handle, 1)

                for u in range(UNITS):
                    j = u // 4
                    if u == CLOSE_O + 1 and behind:
                        ve.wait_ge(o_ps.handle, o_ps.at(i, 0))
                        vec.tensor_tensor(attn[:], pa[:], res[:], ALU.add).then_inc(attn_done.handle, 1)
                    if u == TURN_X + 1 and behind:
                        ve.wait_ge(bc_ps.handle, bc_ps.at(i, 0))
                        ve.wait_ge(stored.handle, stored.at(i - 1, 0))
                        vec.scalar_tensor_tensor(out=an[:], in0=attn[:], scalar=gam2[:], in1=pb[:], op0=ALU.mult, op1=ALU.mult)\
                           .then_inc(an_done.handle, 1)
                    if u % 2 == 1 and made(projection(u - 1), now, ahead, behind, NP) and (now or u > TURN_X):
                        rope(projection(u - 1))
                    if u % 2 == 0 and made(u - 3, now, ahead, behind, UNITS):
                        ve.wait_ge(pt_ps.handle, pt_ps.at(i, u - 2))
                        if behind or u - 3 >= RING:
                            ve.wait_ge(pv_done.handle, pv_done.at(i, u - 2 - RING))
                        vec.tensor_copy(probT[(u - 3) % RING][:], pt[1][:, 0:384]).then_inc(pt_odd.handle, 1)
                    if now:
                        v = u % RING
                        ve.wait_ge(sc_ps.handle, sc_ps.at(i, u + 1))
                        if behind or u >= RING:
                            ve.wait_ge(exp_done.handle, exp_done.at(i, u - RING + 1))
                        vec.tensor_reduce(nmax[v][:], sc[u % 2][:, 0:384].rearrange("p (k n) -> p k n", k=3), AX, ALU.max,
                                          negate=True).then_inc(max_done.handle, 1)
                        ve.wait_ge(max_done.handle, max_done.at(i, u + 1))
                        vec.tensor_tensor(nmax[v][:, 1:2], nmax[v][:, 1:2], nmax[v][:, 2:3], ALU.min)\
                           .then_inc(nmax_done.handle, 1)
                    if u % 4 == 2 and made(j - 2, now, ahead, behind, PAIRS):
                        p = (j - 2) % PAIRS
                        ve.wait_ge(ct_hi.handle, ct_hi.at(i, j - 1))
                        vec.scalar_tensor_tensor(out=ctxT[:, 1, p, :], in0=pa[:], scalar=vb[:, p:p + 1], in1=ctxT[:, 0, p, :],
                                                 op0=ALU.add, op1=ALU.subtract).then_inc(ct_lo.handle, 1)
                    if u % 2 == 0 and made(u - 6, now, ahead, behind, UNITS):
                        normalise((u - 6) // 2)
                    if u == CLOSE_SQUARE and now:
                        ve.wait_ge(x2T_done.handle, x2T_done.at(i, 1))
                        if behind:
                            ve.wait_ge(attn_done.handle, attn_done.at(i, 0))
                        vec.tensor_scalar(res[:], x2T[:], ob[:], None, ALU.add).then_inc(res_done.handle, 1)
                    if u == CLOSE_SQUARE + 1 and ahead:
                        ve.wait_ge(sq_done.handle, sq_done.at(i + 1, 1))
                        vec.tensor_reduce(ss[:], sq[:].rearrange("p (t d) -> p t d", t=TB), AX, ALU.add)\
                           .then_inc(ss_done.handle, 1)
                    if u == RECIPROCALS:
                        ve.wait_ge(std_done.handle, std_done.at(i + 1, 1))
                        cut = slice(0 if ahead else TB, 2 * TB if behind else TB)
                        vec.reciprocal(rr[:, cut], std[:, cut]).then_inc(rr_done.handle, 1)

            turn_by_turn(ve, body)

        @block.gpsimd
        def _(po):
            pool = nc.gpsimd

            def body(i, now, ahead, behind):

                def low(n):
                    w, j = n % 2, n // 2
                    po.wait_ge(qk_hi.handle, qk_hi.at(i, n + 1))
                    pool.tensor_tensor(qk[w][j % RING][:, 1, :], rot[w][:], qk[w][j % RING][:, 0, :], ALU.subtract)\
                        .then_inc(qk_lo.handle, 1)

                for u in range(UNITS):
                    j = u // 4
                    if u % 4 == 3 and made(2 * j + 4, now, ahead, behind, NP) and (now or u > TURN_X):
                        low(2 * j + 4)
                    if u % 4 == 1 and made(2 * j + 3, now, ahead, behind, NP) and (now or u > 25):
                        low(2 * j + 3)
                    if u % 2 == 1 and made(projection(u - 1), now, ahead, behind, NP) and (now or u > TURN_X):
                        n = projection(u - 1)
                        po.wait_ge(b_rope.handle, b_rope.at(i, n + 1))
                        if now or n >= NP + 2:
                            po.wait_ge(qk_lo.handle, qk_lo.at(i, n - 1))
                        pool.tensor_tensor(rot[n % 2][:], rope1[n % 2][:], rope2[n % 2][:], ALU.add).then_inc(rot_done.handle, 1)
                    if u == SCALES:
                        po.wait_ge(rr_done.handle, rr_done.at(i + 1, 1))
                    if u == SCALES and ahead:
                        if now:
                            po.wait_ge(x2_ps.handle, x2_ps.at(i, 1))
                        pool.tensor_tensor(x2[:], xn[:], over(rr[:, 0:TB], P, 2), ALU.mult).then_inc(x2_done.handle, 1)
                    if u == SCALES and behind:
                        pool.tensor_tensor(diag[:].rearrange("p (t n) -> p t n", t=TB), over(eye32[:], TB), over(rr[:, TB:], P, 2),
                                           ALU.mult).then_inc(diag_done.handle, 1)
                    if u == TURN_X + 2 and behind:
                        po.wait_ge(an_done.handle, an_done.at(i, 0))
                        pool.tensor_tensor(rest[:], an[:], attn[:], ALU.add).then_inc(rest_done.handle, 1)
                    if u == X_SPLIT and ahead:
                        po.wait_ge(xT_hi.handle, xT_hi.at(i + 1, 1))
                        pool.tensor_tensor(xT[:, 1, :], x2T[:], xT[:, 0, :], ALU.subtract).then_inc(xT_lo.handle, 1)

            turn_by_turn(po, body)


def experts_phase(nc, an_in, rest_in, s_in, x_in, router_w, router_b, w1, b1, w2, b2, spread, number, eye,
                  x1_out, turns):
    E, ER, TOP = 32, 31, 3
    LAG = 3
    HB, TBUF = 3, 4
    HEAD, TAIL = 6, 2
    SLOTS = E + LAG
    x_v = x_in.rearrange("(n t p) d -> n p t d", t=TB, p=P)
    x1_v = x1_out.rearrange("(n t p) d -> n p t d", t=TB, p=P)

    with ExitStack() as ctx:
        m = Memory(nc, ctx, "moe")
        eye32, eye16 = m.sbuf("eye32", [P, P]), m.sbuf("eye16", [P, P], F16)
        stage = m.sbuf("w_stage", [P, E * P])
        w1_s, w2_s = m.sbuf("w1", [P, 2, E * P], F16), m.sbuf("w2", [P, 2, E * P], F16)
        small = m.sbuf("small", [P, P + ER])
        small16 = m.sbuf("small16", [P, 2, P + ER], F16)
        b1_s = m.sbuf("b1", [P, E])
        rb = m.sbuf("rb", [P, ER])
        num = m.sbuf("num", [P, ER])
        spread_s = m.sbuf("spread", [64, E * P], F16)

        an_f = m.sbuf("an_f", [P, TILE])
        an_next, an = m.sbuf("an_next", [P, 2, TILE], F16), m.sbuf("an", [P, 2, TILE], F16)
        lg, ex, pr = m.sbuf("lg", [P, TB, ER]), m.sbuf("ex", [P, TB, ER]), m.sbuf("pr", [P, TB, ER])
        mx, sm = m.sbuf("mx", [P, TB]), m.sbuf("sm", [P, TB])
        top, top_i, top_f = m.sbuf("top", [P, TB, 8]), m.sbuf("top_i", [P, TB, 8], mybir.dt.uint32), m.sbuf("top_f", [P, TB, 8])
        hit, chosen = m.sbuf("hit", [P, TB, TOP, ER]), m.sbuf("chosen", [P, TB, ER])
        gates = m.sbuf("gates", [P, TB, ER])
        gate16 = m.sbuf("gate16", [P, TB, 64], F16)
        gates_next, gatesT = m.sbuf("gates_next", [64, TILE], F16), m.sbuf("gatesT", [64, TILE], F16)
        h32 = [m.sbuf(f"h32_{k}", [P, TILE]) for k in range(2)]
        t32 = [m.sbuf(f"t32_{k}", [P, TILE]) for k in range(3)]
        t16 = [m.sbuf(f"t16_{k}", [P, 2, TILE], F16) for k in range(TBUF)]
        rest, sT, x_s = m.sbuf("rest", [P, TILE]), m.sbuf("sT", [P, TILE]), m.sbuf("x_s", [P, TB, P])
        y, sl, ys = m.sbuf("y", [P, TILE]), m.sbuf("sl", [P, TILE]), m.sbuf("ys", [P, TILE])
        x1 = m.sbuf("x1", [P, TB, P])

        H, G, (Y,), (m0, m1) = m.banks("h", HB), m.banks("g", 2), m.banks("y", 1), m.banks("misc", 2)

        S = m.count
        const_in, stage_in, stage_hi, w_ready, ready = S("const_in"), S("stage_in"), S("stage_hi"), S("w_ready"), S("ready")
        an_loaded, an_hi, an_lo = S("an_loaded", 16), S("an_hi"), S("an_lo", 1, 1)
        lg_ps, lg_done, ex_done = S("lg_ps"), S("lg_done"), S("ex_done")
        CHAIN = 13
        chain = S("chain", CHAIN)
        gate_split, gT_ps, gT_copied = S("gate_split"), S("gT_ps"), S("gT_copied")
        moved = S("moved")
        h_ps, gelu_done, g_ps, t_done = S("h_ps", E), S("gelu_done", E), S("g_ps", E), S("t_done", E)
        t_hi, t_lo, y_step = S("t_hi", E), S("t_lo", E), S("y_step", E)
        rest_loaded, s_loaded, x_loaded = S("rest_loaded", 16), S("s_loaded", 16), S("x_loaded", 16)
        y_done, sl_done, ys_done = S("y_done", 1, 1), S("sl_done"), S("ys_done", 1, 1)
        yT_ps, x1_done, x1_stored = S("yT_ps"), S("x1_done", 1, 1), S("x1_stored", 16, 16)
        order = S("order")

        block = ctx.enter_context(nc.Block())
        consts = [(eye32, eye), (small[0:64, 0:P], b2), (small[:, P:], router_w), (b1_s, b1),
                  (rb, router_b.rearrange("(a e) -> a e", a=1).to_broadcast([P, ER])), (num, number.to_broadcast([P, ER])),
                  (spread_s, spread)]
        loads = [(w1, w1_s), (w2, w2_s)]
        LAST = turns - 1

        @block.sync
        def _(sp):
            for dst, src in consts:
                sp.dma_start(dst[:], src).then_inc(const_in.handle, 16)
            for n, (src, dst) in enumerate(loads):
                if n:
                    sp.wait_ge(w_ready.handle, n)
                sp.dma_start(stage[:].rearrange("p (e h) -> p e h", e=E), src.rearrange("e p h -> p e h"))\
                    .then_inc(stage_in.handle, 16)
            sp.sem_inc(an_lo.handle, 1)
            sp.sem_inc(y_done.handle, 1)
            sp.sem_inc(ys_done.handle, 1)
            sp.sem_inc(x1_done.handle, 1)
            sp.sem_inc(x1_stored.handle, 16)

            def load_an(k):
                sp.wait_ge(an_lo.handle, an_lo.before(k))
                sp.dma_start(an_f[:], an_in[:, bass.ts(k, TILE)]).then_inc(an_loaded.handle, 16)

            def load_rest(k):
                sp.wait_ge(y_done.handle, y_done.before(k))
                sp.dma_start(rest[:], rest_in[:, bass.ts(k, TILE)]).then_inc(rest_loaded.handle, 16)
                sp.wait_ge(ys_done.handle, ys_done.before(k))
                sp.dma_start(sT[:], s_in[:, bass.ts(k, TILE)]).then_inc(s_loaded.handle, 16)
                sp.wait_ge(x1_done.handle, x1_done.before(k))
                sp.dma_start(x_s[:], x_v[k]).then_inc(x_loaded.handle, 16)

            def store(k):
                sp.wait_ge(x1_done.handle, x1_done.at(k, 1))
                sp.dma_start(x1_v[k], x1[:]).then_inc(x1_stored.handle, 16)

            load_an(0)
            load_rest(0)
            load_an(1)
            with sp.Fori(1, LAST) as i:
                load_an(i + 1)
                store(i - 1)
                load_rest(i)
            store(LAST - 1)
            load_rest(LAST)
            store(LAST)
            sp.wait_ge(x1_stored.handle, 16 * (turns + 1))

        @block.tensor
        def _(te):
            pe = nc.tensor
            te.wait_ge(w_ready.handle, 2)
            te.wait_ge(ready.handle, 5)

            def logits(k):
                te.wait_ge(an_lo.handle, an_lo.at(k, 1))
                te.wait_ge(an_hi.handle, an_hi.at(k, 1))
                for t in range(TB):
                    last = split_product(pe, m0[:, t * 32:t * 32 + ER],
                                         (an_next[:, 0, t * P:(t + 1) * P], an_next[:, 1, t * P:(t + 1) * P]),
                                         (small16[:, 0, P:], small16[:, 1, P:]))
                last.then_inc(lg_ps.handle, 1)

            def turn_gates(k):
                te.wait_ge(gate_split.handle, gate_split.at(k, 1))
                te.sem_inc(order.handle, 1)
                for t in range(TB):
                    last = pe.transpose(m0[0:64, :].bitcast(F16)[:, t * P:(t + 1) * P], gate16[:, t, :], eye16[:])
                last.then_inc(gT_ps.handle, 1)

            def turn_y(k):
                te.wait_ge(ys_done.handle, ys_done.at(k, 1))
                for t in range(TB):
                    last = pe.transpose(m1[:, t * P:(t + 1) * P], ys[:, t * P:(t + 1) * P], eye32[:])
                last.then_inc(yT_ps.handle, 1)

            def body(i, ahead, behind):
                te.wait_ge(moved.handle, moved.at(i, 1))
                for e in range(SLOTS):
                    if e < E:
                        if e >= HB:
                            te.wait_ge(gelu_done.handle, gelu_done.at(i, e - HB + 1))
                        split_product(pe, H[e % HB][:], (w1_s[:, 0, e * P:(e + 1) * P], w1_s[:, 1, e * P:(e + 1) * P]),
                                      (an[:, 0, :], an[:, 1, :])).then_inc(h_ps.handle, 1)
                        if e >= 2:
                            te.wait_ge(t_done.handle, t_done.at(i, e - 1))
                        pe.matmul(G[e % 2][:], spread_s[:, e * P:(e + 1) * P], gatesT[:], start=True, stop=True)\
                            .then_inc(g_ps.handle, 1)
                    if e == LAG - 1:
                        te.wait_ge(y_done.handle, y_done.before(i))
                        pe.matmul(Y[:], small16[0:64, 1, 0:P], gatesT[:], start=True, stop=False, skip_group_check=True)
                        pe.matmul(Y[:], small16[0:64, 0, 0:P], gatesT[:], start=False, stop=False, skip_group_check=True)
                    if e >= LAG:
                        k = e - LAG
                        te.wait_ge(t_hi.handle, t_hi.at(i, k + 1))
                        te.wait_ge(t_lo.handle, t_lo.at(i, k + 1))
                        split_product(pe, Y[:], (w2_s[:, 0, k * P:(k + 1) * P], w2_s[:, 1, k * P:(k + 1) * P]),
                                      (t16[k % TBUF][:, 0, :], t16[k % TBUF][:, 1, :]), start=False, stop=(k == E - 1))\
                            .then_inc(y_step.handle, 1)
                    if behind and e == TAIL + 2:
                        turn_y(i - 1)
                    if ahead and e == HEAD:
                        logits(i + 1)
                    if ahead and e == HEAD + 14:
                        turn_gates(i + 1)

            logits(0)
            turn_gates(0)
            body(0, True, False)
            with te.Fori(1, LAST) as i:
                body(i, True, True)
            body(LAST, False, True)
            turn_y(LAST)

        @block.scalar
        def _(ac):
            act = nc.scalar.activation
            ac.wait_ge(const_in.handle, 16 * len(consts))
            act(eye16[:], eye32[:], ACT.Copy).then_inc(ready.handle, 1)
            act(small16[:, 0, P:], small[:, P:], ACT.Copy)
            act(small16[0:64, 0, 0:P], small[0:64, 0:P], ACT.Copy).then_inc(ready.handle, 1)
            for n, (src, dst) in enumerate(loads):
                ac.wait_ge(stage_in.handle, 16 * (n + 1))
                act(dst[:, 0, :], stage[:], ACT.Copy).then_inc(stage_hi.handle, 1)

            def high(k):
                ac.wait_ge(an_loaded.handle, an_loaded.at(k, 16))
                act(an_next[:, 0, :], an_f[:], ACT.Copy).then_inc(an_hi.handle, 1)

            def exps(k):
                ac.wait_ge(lg_done.handle, lg_done.at(k, 1))
                act(ex[:], lg[:], ACT.Exp).then_inc(ex_done.handle, 1)

            def copy_gates(k):
                ac.wait_ge(gT_ps.handle, gT_ps.at(k, 1))
                act(gates_next[:], m0[0:64, :].bitcast(F16)[:, 0:TILE], ACT.Copy).then_inc(gT_copied.handle, 1)

            def gate_y(k):
                ac.wait_ge(y_done.handle, y_done.at(k, 1))
                act(sl[:], y[:], ACT.Silu).then_inc(sl_done.handle, 1)

            def body(i, ahead, behind):
                for e in range(E):
                    if behind and e == 0:
                        gate_y(i - 1)
                    ac.wait_ge(h_ps.handle, h_ps.at(i, e + 1))
                    if e >= 2:
                        ac.wait_ge(t_done.handle, t_done.at(i, e - 1))
                    act(h32[e % 2][:], H[e % HB][:], ACT.Gelu, bias=b1_s[:, e:e + 1]).then_inc(gelu_done.handle, 1)
                    if ahead and e == HEAD - 4:
                        ac.wait_ge(moved.handle, moved.at(i, 1))
                        high(i + 1)
                    if ahead and e == HEAD + 3:
                        exps(i + 1)
                    if ahead and e == HEAD + 16:
                        copy_gates(i + 1)

            high(0)
            exps(0)
            copy_gates(0)
            body(0, True, False)
            with ac.Fori(1, LAST) as i:
                body(i, True, True)
            body(LAST, False, True)
            gate_y(LAST)

        @block.vector
        def _(ve):
            vec = nc.vector
            ve.wait_ge(const_in.handle, 16 * len(consts))
            vec.memset(gate16[:, :, ER:ER + 1], 1.0).then_inc(ready.handle, 1)
            vec.memset(gate16[:, :, 63:64], 0.0).then_inc(ready.handle, 1)
            ve.wait_ge(ready.handle, 4)
            vec.tensor_tensor(small16[:, 1, P:], small[:, P:], small16[:, 0, P:], ALU.subtract)
            vec.tensor_tensor(small16[0:64, 1, 0:P], small[0:64, 0:P], small16[0:64, 0, 0:P], ALU.subtract)\
               .then_inc(ready.handle, 1)
            for n, (src, dst) in enumerate(loads):
                ve.wait_ge(stage_hi.handle, n + 1)
                vec.tensor_tensor(dst[:, 1, :], stage[:], dst[:, 0, :], ALU.subtract).then_inc(w_ready.handle, 1)

            def router(k):
                steps = [0]

                def step(ins):
                    steps[0] += 1
                    ins.then_inc(chain.handle, 1)
                    ve.wait_ge(chain.handle, chain.at(k, steps[0]))

                ve.wait_ge(lg_ps.handle, lg_ps.at(k, 1))
                step(vec.tensor_tensor(lg[:], m0[:, 0:TB * 32].rearrange("p (t e) -> p t e", t=TB)[:, :, 0:ER],
                                       over(rb[:], TB), ALU.add))
                step(vec.tensor_reduce(mx[:], lg[:], AX, ALU.max))
                vec.tensor_tensor(lg[:], lg[:], over(mx[:], ER, 2), ALU.subtract).then_inc(lg_done.handle, 1)
                yield
                ve.wait_ge(ex_done.handle, ex_done.at(k, 1))
                step(vec.tensor_reduce(sm[:], ex[:], AX, ALU.add))
                step(vec.reciprocal(sm[:], sm[:]))
                step(vec.tensor_tensor(pr[:], ex[:], over(sm[:], ER, 2), ALU.mult))
                yield
                ve.sem_inc(order.handle, 1)
                for t in range(TB):
                    last = vec.max(top[:, t, :], pr[:, t, :])
                step(last)
                ve.sem_inc(order.handle, 1)
                yield
                for t in range(TB):
                    last = vec.max_index(top_i[:, t, :], top[:, t, :], pr[:, t, :])
                step(last)
                yield
                step(vec.tensor_copy(top_f[:], top_i[:]))
                step(vec.tensor_tensor(hit[:], over(over(num[:], TOP), TB), over(top_f[:, :, 0:TOP], ER, 3), ALU.is_equal))
                yield
                step(vec.tensor_reduce(chosen[:], hit[:].rearrange("p t k e -> p t e k"), AX, ALU.add))
                step(vec.tensor_tensor(gates[:], pr[:], chosen[:], ALU.mult))
                yield
                step(vec.tensor_copy(gate16[:, :, 0:ER], gates[:]))
                step(vec.tensor_tensor(chosen[:], gates[:], gate16[:, :, 0:ER], ALU.subtract))
                vec.tensor_copy(gate16[:, :, 32:32 + ER], chosen[:]).then_inc(gate_split.handle, 1)
                assert steps[0] == CHAIN
                yield

            def move(k):
                ve.wait_ge(gT_copied.handle, gT_copied.at(k, 1))
                vec.tensor_copy(an[:], an_next[:])
                vec.tensor_copy(gatesT[:], gates_next[:]).then_inc(moved.handle, 1)

            def add_x(k):
                ve.wait_ge(yT_ps.handle, yT_ps.at(k, 1))
                ve.wait_ge(x_loaded.handle, x_loaded.at(k, 16))
                ve.wait_ge(x1_stored.handle, x1_stored.before(k))
                vec.tensor_tensor(x1[:].rearrange("p t d -> p (t d)"), m1[:], x_s[:].rearrange("p t d -> p (t d)"), ALU.add)\
                   .then_inc(x1_done.handle, 1)

            def body(i, ahead, behind):
                part = router(i + 1) if ahead else iter(())
                for e in range(E + 1):
                    if e < E:
                        ve.wait_ge(g_ps.handle, g_ps.at(i, e + 1))
                        ve.wait_ge(gelu_done.handle, gelu_done.at(i, e + 1))
                        if e >= 3:
                            ve.wait_ge(t_lo.handle, t_lo.at(i, e - 2))
                        vec.tensor_tensor(t32[e % 3][:], G[e % 2][:], h32[e % 2][:], ALU.mult).then_inc(t_done.handle, 1)
                    if e:
                        ve.wait_ge(t_done.handle, t_done.at(i, e))
                        if e > TBUF:
                            ve.wait_ge(y_step.handle, y_step.at(i, e - TBUF))
                        vec.tensor_copy(t16[(e - 1) % TBUF][:, 0, :], t32[(e - 1) % 3][:]).then_inc(t_hi.handle, 1)
                    if behind and e == TAIL + 4:
                        add_x(i - 1)
                    if e >= HEAD + 2:
                        next(part, None)
                if ahead:
                    for _ in part:
                        pass
                    move(i + 1)
                ve.wait_ge(y_step.handle, y_step.at(i, E))
                ve.wait_ge(rest_loaded.handle, rest_loaded.at(i, 16))
                vec.tensor_tensor(y[:], Y[:], rest[:], ALU.add).then_inc(y_done.handle, 1)

            for _ in router(0):
                pass
            move(0)
            body(0, True, False)
            with ve.Fori(1, LAST) as i:
                body(i, True, True)
            body(LAST, False, True)
            add_x(LAST)

        @block.gpsimd
        def _(po):
            pool = nc.gpsimd

            def low(k):
                po.wait_ge(an_hi.handle, an_hi.at(k, 1))
                pool.tensor_tensor(an_next[:, 1, :], an_f[:], an_next[:, 0, :], ALU.subtract).then_inc(an_lo.handle, 1)

            def scale_s(k):
                po.wait_ge(sl_done.handle, sl_done.at(k, 1))
                po.wait_ge(s_loaded.handle, s_loaded.at(k, 16))
                pool.tensor_tensor(ys[:], sl[:], sT[:], ALU.mult).then_inc(ys_done.handle, 1)

            def body(i, ahead, behind):
                for e in range(E):
                    if behind and e == 1:
                        scale_s(i - 1)
                    po.wait_ge(t_hi.handle, t_hi.at(i, e + 1))
                    pool.tensor_tensor(t16[e % TBUF][:, 1, :], t32[e % 3][:], t16[e % TBUF][:, 0, :], ALU.subtract)\
                        .then_inc(t_lo.handle, 1)
                    if ahead and e == HEAD - 4:
                        low(i + 1)

            low(0)
            body(0, True, False)
            with po.Fori(1, LAST) as i:
                body(i, True, True)
            body(LAST, False, True)
            scale_s(LAST)


def second_layer_phase(nc, x_in, wqkvo, bo, gate_w, wg, wu, wd, spread, number, block_mask, head_mask, eye,
                       s_tmp, out, turns):
    HEADS, HD, ER, TOP = 16, 8, 8, 2
    HT = wg.shape[1] // P
    LAG, TBUF = 3, 4
    SLOTS = HT + LAG
    x_v = x_in.rearrange("(n t p) d -> n p t d", t=TB, p=P)
    out_v = out.rearrange("(n t p) d -> n p t d", t=TB, p=P)
    KX = P + HEADS

    with ExitStack() as ctx:
        m = Memory(nc, ctx, "second")
        eye32, eye16 = m.sbuf("eye32", [P, P]), m.sbuf("eye16", [P, P], F16)
        eps = m.sbuf("eps", [P, 1])
        stage = m.sbuf("w_stage", [P, HT * P])
        wg_s, wu_s, wd_s = (m.sbuf(n, [P, 2, HT * P], F16) for n in ("wg", "wu", "wd"))
        small, small16 = m.sbuf("small", [P, 4 * P + ER]), m.sbuf("small16", [P, 2, 4 * P + ER], F16)
        bo_s = m.sbuf("bo", [P, 1])
        num = m.sbuf("num", [P, ER])
        spread_s = m.sbuf("spread", [64, HT * P], F16)
        bmask, hmask = m.sbuf("bmask", [P, P]), m.sbuf("hmask", [P, HEADS])

        def w(a, b):
            return small16[:, 0, a:b], small16[:, 1, a:b]

        x_s = m.sbuf("x_s", [P, TB, P])
        stats, mean_var = m.sbuf("stats", [P, TB, 6]), m.sbuf("mean_var", [P, TB, 2])
        std, rstd = m.sbuf("std", [P, TB]), m.sbuf("rstd", [P, TB])
        xn = m.sbuf("xn", [P, TB, P])
        x_next, x_cur = m.sbuf("x_next", [P, 2, TILE], F16), m.sbuf("x_cur", [P, 2, TILE], F16)
        arg, ex = m.sbuf("arg", [P, 2 * TILE + TB * TOP]), m.sbuf("ex", [P, 2 * TILE + TB * TOP])
        pos_part = m.sbuf("pos_part", [P, 2 * TILE])
        feat = m.sbuf("feat", [P, 2 * TILE])
        v1 = m.sbuf("v1", [P, TB, P + 1])
        kvx = m.sbuf("kvx", [P, SEQS, KX])
        den = m.sbuf("den", [P, TB, HEADS])
        rden = m.sbuf("rden", [P, TB, HEADS])
        mixed = m.sbuf("mixed", [P, TB, P])
        mT = m.sbuf("mT", [P, 2, TILE], F16)
        s_next, s_cur = m.sbuf("s_next", [P, TILE]), m.sbuf("s_cur", [P, TILE])
        lg = m.sbuf("lg", [P, TB, ER])
        top, top_i, top_f = m.sbuf("top", [P, TB, 8]), m.sbuf("top_i", [P, TB, 8], mybir.dt.uint32), m.sbuf("top_f", [P, TB, 8])
        wsum = m.sbuf("wsum", [P, TB])
        share = m.sbuf("share", [P, TB, TOP])
        hit = m.sbuf("hit", [P, TB, TOP, ER])
        gates = m.sbuf("gates", [P, TB, ER])
        gate16 = m.sbuf("gate16", [P, TB, 64], F16)
        gates_next, gatesT = m.sbuf("gates_next", [64, TILE], F16), m.sbuf("gatesT", [64, TILE], F16)
        s32 = [m.sbuf(f"s32_{k}", [P, TILE]) for k in range(2)]
        a32 = [m.sbuf(f"a32_{k}", [P, TILE]) for k in range(2)]
        t32 = [m.sbuf(f"t32_{k}", [P, TILE]) for k in range(3)]
        t16 = [m.sbuf(f"t16_{k}", [P, 2, TILE], F16) for k in range(TBUF)]
        x_r, y = m.sbuf("x_r", [P, TB, P]), m.sbuf("y", [P, TB, P])
        sl, ys = m.sbuf("sl", [P, TILE]), m.sbuf("ys", [P, TILE])

        G, U, (C,), (Y,), (m0, m1) = m.banks("g", 2), m.banks("u", 2), m.banks("c", 1), m.banks("y", 1), m.banks("misc", 2)

        S = m.count
        const_in, stage_in, stage_hi, w_ready, ready = S("const_in"), S("stage_in"), S("stage_hi"), S("w_ready"), S("ready")
        x_loaded, stats_done, aggr_done, std_done, rstd_done = S("x_loaded", 16), S("stats_done"), S("aggr_done"), S("std_done"), S("rstd_done")
        xn_done, xT_ps, xT_hi, xT_lo = S("xn_done", 1, 1), S("xT_ps"), S("xT_hi"), S("xT_lo")
        lg_ps, q_ps, q_min, q_max = S("lg_ps"), S("q_ps"), S("q_min"), S("q_max")
        kv_ps, k_min, kv_out = S("kv_ps", 2), S("k_min", 2), S("kv_out", 2)
        arg_done, ex_done, feat_done = S("arg_done"), S("ex_done"), S("feat_done")
        sum_ps, kvx_done, mix_ps = S("sum_ps", SEQS), S("kvx_done", SEQS), S("mix_ps", 2)
        den_done, rden_done, mix_done = S("den_done", 2), S("rden_done"), S("mix_done", 2)
        mT_ps, mT_hi, mT_lo, s_ps, s_done = S("mT_ps"), S("mT_hi"), S("mT_lo"), S("s_ps"), S("s_done")
        s_stored = S("s_stored", 16, 16)
        CHAIN = 11
        chain = S("chain", CHAIN)
        gate_split, gT_ps, gT_copied, moved = S("gate_split"), S("gT_ps"), S("gT_copied"), S("moved")
        g_ps, u_ps, c_ps = S("g_ps", HT), S("u_ps", HT), S("c_ps", HT)
        silu_done, a_done, t_done, t_hi, t_lo, y_step = (S(n, HT) for n in ("silu_done", "a_done", "t_done", "t_hi", "t_lo", "y_step"))
        s_loaded, xr_loaded = S("s_loaded", 16), S("xr_loaded", 16)
        sl_done, ys_done, yT_ps, y_done, y_stored = S("sl_done", 1, 1), S("ys_done", 1, 1), S("yT_ps"), S("y_done", 1, 1), S("y_stored", 16, 16)
        order = S("order")

        block = ctx.enter_context(nc.Block())
        consts = [(eye32, eye), (small[:, 0:4 * P], wqkvo), (small[:, 4 * P:], gate_w),
                  (bo_s, bo.rearrange("(p a) -> p a", a=1)), (num, number[:, 0:ER].to_broadcast([P, ER])),
                  (spread_s, spread), (bmask, block_mask), (hmask, head_mask)]
        loads = [(wg, wg_s), (wu, wu_s), (wd.rearrange("(j p) n -> p j n", p=P), wd_s)]
        LAST = turns - 1

        @block.sync
        def _(sp):
            for dst, src in consts:
                sp.dma_start(dst[:], src).then_inc(const_in.handle, 16)
            for n, (src, dst) in enumerate(loads):
                if n:
                    sp.wait_ge(w_ready.handle, n)
                to = stage[:] if len(src.shape) == 2 else stage[:].rearrange("p (j n) -> p j n", n=P)
                sp.dma_start(to, src).then_inc(stage_in.handle, 16)
            sp.sem_inc(xn_done.handle, 1)
            sp.sem_inc(sl_done.handle, 1)
            sp.sem_inc(ys_done.handle, 1)
            sp.sem_inc(y_done.handle, 1)
            sp.sem_inc(s_stored.handle, 16)
            sp.sem_inc(y_stored.handle, 16)

            def load_x(k):
                sp.wait_ge(xn_done.handle, xn_done.before(k))
                sp.dma_start(x_s[:], x_v[k]).then_inc(x_loaded.handle, 16)

            def load_end(k):
                sp.wait_ge(s_stored.handle, s_stored.at(k, 16))
                sp.wait_ge(ys_done.handle, ys_done.before(k))
                sp.dma_start(s_cur[:], s_tmp[:, bass.ts(k, TILE)]).then_inc(s_loaded.handle, 16)
                sp.wait_ge(y_done.handle, y_done.before(k))
                sp.dma_start(x_r[:], x_v[k]).then_inc(xr_loaded.handle, 16)

            def store_s(k):
                sp.wait_ge(s_done.handle, s_done.at(k, 1))
                sp.dma_start(s_tmp[:, bass.ts(k, TILE)], s_next[:]).then_inc(s_stored.handle, 16)

            def store(k):
                sp.wait_ge(y_done.handle, y_done.at(k, 1))
                sp.dma_start(out_v[k], y[:]).then_inc(y_stored.handle, 16)

            load_x(0)
            store_s(0)
            load_x(1)
            load_end(0)
            store_s(1)
            with sp.Fori(1, LAST) as i:
                load_x(i + 1)
                store(i - 1)
                load_end(i)
                store_s(i + 1)
            store(LAST - 1)
            load_end(LAST)
            store(LAST)
            sp.wait_ge(y_stored.handle, 16 * (turns + 1))
            sp.wait_ge(s_stored.handle, 16 * (turns + 1))

        @block.tensor
        def _(te):
            pe = nc.tensor
            te.wait_ge(w_ready.handle, len(loads))
            te.wait_ge(ready.handle, 6)

            def tok(pair, t):
                return pair[:, 0, t * P:(t + 1) * P], pair[:, 1, t * P:(t + 1) * P]

            def turn_x(k):
                te.wait_ge(xn_done.handle, xn_done.at(k, 1))
                for t in range(TB):
                    last = pe.transpose(m0[:, t * P:(t + 1) * P], xn[:, t, :], eye32[:])
                last.then_inc(xT_ps.handle, 1)

            def queries(k):
                te.wait_ge(xT_lo.handle, xT_lo.at(k, 1))
                for t in range(TB):
                    last = split_product(pe, m1[:, t * ER:(t + 1) * ER], tok(x_next, t), w(4 * P, 4 * P + ER))
                last.then_inc(lg_ps.handle, 1)
                split_product(pe, m0[:], w(0, P), (x_next[:, 0, :], x_next[:, 1, :])).then_inc(q_ps.handle, 1)

            def keys_values(k):
                te.wait_ge(q_min.handle, q_min.at(k, 1))
                te.wait_ge(q_max.handle, q_max.at(k, 1))
                te.wait_ge(chain.handle, chain.at(k, 1))
                for s, bank in enumerate((m0, m1)):
                    for b in range(2):
                        last = split_product(pe, bank[:, b * 2 * P:(b + 1) * 2 * P], tok(x_next, 2 * s + b), w(P, 3 * P))
                    last.then_inc(kv_ps.handle, 1)

            def sums(k):
                te.wait_ge(feat_done.handle, feat_done.at(k, 1))
                te.wait_ge(kv_out.handle, kv_out.at(k, 2))
                te.wait_ge(k_min.handle, k_min.at(k, 2))
                for s, bank in enumerate((m0, m1)):
                    for b in range(2):
                        t = 2 * s + b
                        last = pe.matmul(bank[:, 0:P + 1], feat[:, TILE + t * P:TILE + (t + 1) * P], v1[:, t, :],
                                         start=(b == 0), stop=(b == 1), skip_group_check=True)
                    last.then_inc(sum_ps.handle, 1)

            def mix(k):
                for s, bank in enumerate((m0, m1)):
                    te.wait_ge(kvx_done.handle, kvx_done.at(k, s + 1))
                    for b in range(2):
                        t = 2 * s + b
                        last = pe.matmul(bank[:, b * KX:(b + 1) * KX], feat[:, t * P:(t + 1) * P], kvx[:, s, :],
                                         start=True, stop=True, skip_group_check=True)
                    last.then_inc(mix_ps.handle, 1)

            def turn_mixed(k):
                te.wait_ge(mix_done.handle, mix_done.at(k, 2))
                for t in range(TB):
                    last = pe.transpose(m0[:, t * P:(t + 1) * P], mixed[:, t, :], eye32[:])
                last.then_inc(mT_ps.handle, 1)

            def project(k):
                te.wait_ge(mT_lo.handle, mT_lo.at(k, 1))
                split_product(pe, m1[:], w(3 * P, 4 * P), (mT[:, 0, :], mT[:, 1, :])).then_inc(s_ps.handle, 1)

            def turn_gates(k):
                te.wait_ge(gate_split.handle, gate_split.at(k, 1))
                te.sem_inc(order.handle, 1)
                for t in range(TB):
                    last = pe.transpose(m0[0:64, :].bitcast(F16)[:, t * P:(t + 1) * P], gate16[:, t, :], eye16[:])
                last.then_inc(gT_ps.handle, 1)

            def turn_y(k):
                te.wait_ge(ys_done.handle, ys_done.at(k, 1))
                te.wait_ge(s_done.handle, s_done.at(k, 1) if isinstance(k, int) and k == LAST else s_done.at(k + 1, 1))
                for t in range(TB):
                    last = pe.transpose(m1[:, t * P:(t + 1) * P], ys[:, t * P:(t + 1) * P], eye32[:])
                last.then_inc(yT_ps.handle, 1)

            ahead_of = {3: turn_x, 6: queries, 8: keys_values, 13: sums, 15: mix, 18: turn_mixed, 20: project, 21: turn_gates}

            def body(i, ahead, behind):
                te.wait_ge(moved.handle, moved.at(i, 1))
                for j in range(SLOTS):
                    if j < HT:
                        at = slice(j * P, (j + 1) * P)
                        xs = (x_cur[:, 0, :], x_cur[:, 1, :])
                        if j >= 2:
                            te.wait_ge(silu_done.handle, silu_done.at(i, j - 1))
                        split_product(pe, G[j % 2][:], (wg_s[:, 0, at], wg_s[:, 1, at]), xs).then_inc(g_ps.handle, 1)
                        if j >= 2:
                            te.wait_ge(a_done.handle, a_done.at(i, j - 1))
                        split_product(pe, U[j % 2][:], (wu_s[:, 0, at], wu_s[:, 1, at]), xs).then_inc(u_ps.handle, 1)
                    if j >= LAG:
                        k = j - LAG
                        at = slice(k * P, (k + 1) * P)
                        if k == 0:
                            te.wait_ge(sl_done.handle, sl_done.before(i))
                        te.wait_ge(t_hi.handle, t_hi.at(i, k + 1))
                        te.wait_ge(t_lo.handle, t_lo.at(i, k + 1))
                        split_product(pe, Y[:], (wd_s[:, 0, at], wd_s[:, 1, at]),
                                      (t16[k % TBUF][:, 0, :], t16[k % TBUF][:, 1, :]), start=(k == 0), stop=(k == HT - 1))\
                            .then_inc(y_step.handle, 1)
                    if j < HT:
                        if j:
                            te.wait_ge(t_done.handle, t_done.at(i, j))
                        pe.matmul(C[:], spread_s[:, j * P:(j + 1) * P], gatesT[:], start=True, stop=True)\
                            .then_inc(c_ps.handle, 1)
                    if behind and j == 2:
                        turn_y(i - 1)
                    if ahead and j in ahead_of:
                        ahead_of[j](i + 1)

            for part in ahead_of.values():
                part(0)
            body(0, True, False)
            with te.Fori(1, LAST) as i:
                body(i, True, True)
            body(LAST, False, True)
            turn_y(LAST)

        @block.scalar
        def _(ac):
            act = nc.scalar.activation
            ac.wait_ge(const_in.handle, 16 * len(consts))
            act(eye16[:], eye32[:], ACT.Copy).then_inc(ready.handle, 1)
            act(small16[:, 0, :], small[:], ACT.Copy).then_inc(ready.handle, 1)
            for n, (src, dst) in enumerate(loads):
                ac.wait_ge(stage_in.handle, 16 * (n + 1))
                act(dst[:, 0, :], stage[:], ACT.Copy).then_inc(stage_hi.handle, 1)
            ac.wait_ge(ready.handle, 6)

            def root(k):
                ac.wait_ge(aggr_done.handle, aggr_done.at(k, 1))
                act(std[:], mean_var[:, :, 1], ACT.Sqrt, bias=eps[:]).then_inc(std_done.handle, 1)

            def x_high(k):
                ac.wait_ge(xT_ps.handle, xT_ps.at(k, 1))
                act(x_next[:, 0, :], m0[:], ACT.Copy).then_inc(xT_hi.handle, 1)

            def q_part(k):
                ac.wait_ge(q_ps.handle, q_ps.at(k, 1))
                act(pos_part[:, 0:TILE], m0[:], ACT.Relu).then_inc(q_max.handle, 1)

            def kv_part(k):
                for s, bank in enumerate((m0, m1)):
                    kv = bank[:].rearrange("p (b c n) -> p b c n", b=2, c=2)
                    ac.wait_ge(kv_ps.handle, kv_ps.at(k, s + 1))
                    act(pos_part[:, TILE + s * 256:TILE + (s + 1) * 256].rearrange("p (b n) -> p b n", b=2), kv[:, :, 0, :],
                        ACT.Relu)
                    act(v1[:, 2 * s:2 * s + 2, 0:P], kv[:, :, 1, :], ACT.Copy).then_inc(kv_out.handle, 1)

            def exps(k):
                ac.wait_ge(arg_done.handle, arg_done.at(k, 1))
                ac.wait_ge(k_min.handle, k_min.at(k, 2))
                ac.wait_ge(q_min.handle, q_min.at(k, 1))
                act(ex[:], arg[:], ACT.Exp).then_inc(ex_done.handle, 1)

            def m_high(k):
                ac.wait_ge(mT_ps.handle, mT_ps.at(k, 1))
                act(mT[:, 0, :], m0[:], ACT.Copy).then_inc(mT_hi.handle, 1)

            def s_copy(k):
                ac.wait_ge(s_ps.handle, s_ps.at(k, 1))
                ac.wait_ge(s_stored.handle, s_stored.before(k))
                act(s_next[:], m1[:], ACT.Identity, bias=bo_s[:]).then_inc(s_done.handle, 1)

            def copy_gates(k):
                ac.wait_ge(gT_ps.handle, gT_ps.at(k, 1))
                act(gates_next[:], m0[0:64, :].bitcast(F16)[:, 0:TILE], ACT.Copy).then_inc(gT_copied.handle, 1)

            def gate_y(k):
                ac.wait_ge(y_step.handle, y_step.at(k, HT))
                ac.wait_ge(ys_done.handle, ys_done.before(k))
                act(sl[:], Y[:], ACT.Silu).then_inc(sl_done.handle, 1)

            ahead_of = {1: root, 4: x_high, 7: q_part, 9: kv_part, 11: exps, 19: m_high, 21: s_copy, 22: copy_gates}

            def body(i, ahead, behind):
                for j in range(HT + 1):
                    if behind and j == 0:
                        gate_y(i - 1)
                    if j < HT:
                        ac.wait_ge(g_ps.handle, g_ps.at(i, j + 1))
                        if j >= 2:
                            ac.wait_ge(a_done.handle, a_done.at(i, j - 1))
                        act(s32[j % 2][:], G[j % 2][:], ACT.Silu).then_inc(silu_done.handle, 1)
                    if j:
                        ac.wait_ge(t_done.handle, t_done.at(i, j))
                        if j > TBUF:
                            ac.wait_ge(y_step.handle, y_step.at(i, j - TBUF))
                        act(t16[(j - 1) % TBUF][:, 0, :], t32[(j - 1) % 3][:], ACT.Copy).then_inc(t_hi.handle, 1)
                    if ahead and j in ahead_of:
                        ahead_of[j](i + 1)

            for part in ahead_of.values():
                part(0)
            body(0, True, False)
            with ac.Fori(1, LAST) as i:
                body(i, True, True)
            body(LAST, False, True)
            gate_y(LAST)

        @block.vector
        def _(ve):
            vec = nc.vector
            ve.wait_ge(const_in.handle, 16 * len(consts))
            vec.memset(gate16[:], 0.0).then_inc(ready.handle, 1)
            ve.wait_ge(ready.handle, 3)
            vec.memset(gate16[:, :, ER:ER + 1], 1.0)
            vec.memset(eps[:], EPS)
            vec.memset(v1[:, :, P:P + 1], 1.0).then_inc(ready.handle, 2)
            vec.tensor_tensor(small16[:, 1, :], small[:], small16[:, 0, :], ALU.subtract).then_inc(ready.handle, 1)
            for n, (src, dst) in enumerate(loads):
                ve.wait_ge(stage_hi.handle, n + 1)
                vec.tensor_tensor(dst[:, 1, :], stage[:], dst[:, 0, :], ALU.subtract).then_inc(w_ready.handle, 1)

            def norm_stats(k):
                ve.wait_ge(x_loaded.handle, x_loaded.at(k, 16))
                for t in range(TB):
                    last = vec.bn_stats(stats[:, t, :], x_s[:, t, :])
                last.then_inc(stats_done.handle, 1)
                ve.wait_ge(stats_done.handle, stats_done.at(k, 1))
                ve.sem_inc(order.handle, 1)
                for t in range(TB):
                    last = vec.bn_aggr(mean_var[:, t, :], stats[:, t, :])
                last.then_inc(aggr_done.handle, 1)

            def norm(k):
                ve.wait_ge(std_done.handle, std_done.at(k, 1))
                vec.reciprocal(rstd[:], std[:]).then_inc(rstd_done.handle, 1)
                ve.wait_ge(rstd_done.handle, rstd_done.at(k, 1))
                for t in range(TB):
                    last = vec.tensor_scalar(xn[:, t, :], x_s[:, t, :], mean_var[:, t, 0:1], rstd[:, t:t + 1],
                                             ALU.subtract, ALU.mult)
                last.then_inc(xn_done.handle, 1)

            def x_low(k):
                ve.wait_ge(xT_hi.handle, xT_hi.at(k, 1))
                vec.tensor_tensor(x_next[:, 1, :], m0[:], x_next[:, 0, :], ALU.subtract).then_inc(xT_lo.handle, 1)

            steps = {}

            def step(k, ins):
                n = steps[id(k)] = steps.get(id(k), 0) + 1
                ins.then_inc(chain.handle, 1)
                ve.wait_ge(chain.handle, chain.at(k, n))

            def q_neg(k):
                steps[id(k)] = 0
                ve.wait_ge(lg_ps.handle, lg_ps.at(k, 1))
                step(k, vec.tensor_copy(lg[:], m1[:, 0:TB * ER].rearrange("p (t e) -> p t e", t=TB)))
                ve.wait_ge(q_max.handle, q_max.at(k, 1))
                vec.tensor_scalar(arg[:, 0:TILE], m0[:], 0.0, None, ALU.min).then_inc(q_min.handle, 1)
                ve.sem_inc(order.handle, 1)
                for t in range(TB):
                    last = vec.max(top[:, t, :], lg[:, t, :])
                step(k, last)
                ve.sem_inc(order.handle, 1)

            def k_neg(k):
                for t in range(TB):
                    last = vec.max_index(top_i[:, t, :], top[:, t, :], lg[:, t, :])
                step(k, last)
                vec.tensor_tensor(arg[:, 2 * TILE:].rearrange("p (t k) -> p t k", t=TB), top[:, :, 0:TOP],
                                  top[:, :, 0:1].to_broadcast([P, TB, TOP]), ALU.subtract).then_inc(arg_done.handle, 1)
                for s, bank in enumerate((m0, m1)):
                    ve.wait_ge(kv_out.handle, kv_out.at(k, s + 1))
                    vec.tensor_scalar(arg[:, TILE + s * 256:TILE + (s + 1) * 256].rearrange("p (b n) -> p b n", b=2),
                                      bank[:].rearrange("p (b c n) -> p b c n", b=2, c=2)[:, :, 0, :], 0.0, None, ALU.min)\
                       .then_inc(k_min.handle, 1)

            def choose(k):
                e3 = ex[:, 2 * TILE:].rearrange("p (t k) -> p t k", t=TB)
                ve.wait_ge(ex_done.handle, ex_done.at(k, 1))
                step(k, vec.tensor_reduce(wsum[:], e3, AX, ALU.add))
                step(k, vec.reciprocal(wsum[:], wsum[:]))
                step(k, vec.tensor_tensor(share[:], e3, over(wsum[:], TOP, 2), ALU.mult))
                step(k, vec.tensor_copy(top_f[:], top_i[:]))
                step(k, vec.tensor_tensor(hit[:], over(over(num[:], TOP), TB), over(top_f[:, :, 0:TOP], ER, 3), ALU.is_equal))

            def choose_more(k):
                step(k, vec.tensor_tensor(hit[:], hit[:], over(share[:], ER, 3), ALU.mult))
                step(k, vec.tensor_reduce(gates[:], hit[:].rearrange("p t k e -> p t e k"), AX, ALU.add))
                step(k, vec.tensor_copy(gate16[:, :, 0:ER], gates[:]))
                assert steps[id(k)] == CHAIN
                vec.tensor_tensor(gate16[:, :, 32:32 + ER], gates[:], gate16[:, :, 0:ER], ALU.subtract)\
                   .then_inc(gate_split.handle, 1)

            def mask_sums(k):
                for s, bank in enumerate((m0, m1)):
                    ve.wait_ge(sum_ps.handle, sum_ps.at(k, s + 1))
                    vec.tensor_tensor(kvx[:, s, 0:P], bank[:, 0:P], bmask[:], ALU.mult)
                    vec.tensor_scalar(kvx[:, s, P:], hmask[:], bank[:, P:P + 1], None, ALU.mult).then_inc(kvx_done.handle, 1)

            def divide(k):
                for s, bank in enumerate((m0, m1)):
                    ve.wait_ge(mix_ps.handle, mix_ps.at(k, s + 1))
                    got = bank[:, 0:2 * KX].rearrange("p (b n) -> p b n", b=2)
                    vec.tensor_scalar(den[:, 2 * s:2 * s + 2, :], got[:, :, P:], 1e-6, None, ALU.add).then_inc(den_done.handle, 1)
                ve.wait_ge(den_done.handle, den_done.at(k, 2))
                vec.reciprocal(rden[:], den[:]).then_inc(rden_done.handle, 1)
                ve.wait_ge(rden_done.handle, rden_done.at(k, 1))
                for s, bank in enumerate((m0, m1)):
                    for b in range(2):
                        t = 2 * s + b
                        last = vec.tensor_tensor(mixed[:, t, :].rearrange("p (h d) -> p h d", d=HD),
                                                 bank[:, b * KX:b * KX + P].rearrange("p (h d) -> p h d", d=HD),
                                                 over(rden[:, t, :], HD, 2), ALU.mult)
                    last.then_inc(mix_done.handle, 1)

            def m_low(k):
                ve.wait_ge(mT_hi.handle, mT_hi.at(k, 1))
                vec.tensor_tensor(mT[:, 1, :], m0[:], mT[:, 0, :], ALU.subtract).then_inc(mT_lo.handle, 1)

            def move(k):
                ve.wait_ge(gT_copied.handle, gT_copied.at(k, 1))
                vec.tensor_copy(x_cur[:], x_next[:])
                vec.tensor_copy(gatesT[:], gates_next[:]).then_inc(moved.handle, 1)

            def add_x(k):
                ve.wait_ge(yT_ps.handle, yT_ps.at(k, 1))
                ve.wait_ge(xr_loaded.handle, xr_loaded.at(k, 16))
                ve.wait_ge(y_stored.handle, y_stored.before(k))
                vec.tensor_tensor(y[:].rearrange("p t d -> p (t d)"), m1[:], x_r[:].rearrange("p t d -> p (t d)"), ALU.add)\
                   .then_inc(y_done.handle, 1)

            ahead_of = {0: norm_stats, 2: norm, 5: x_low, 7: q_neg, 9: k_neg, 12: choose, 14: mask_sums, 16: divide,
                        17: choose_more, 20: m_low}

            def body(i, ahead, behind):
                nxt = i + 1
                for j in range(HT + 1):
                    if j:
                        ve.wait_ge(c_ps.handle, c_ps.at(i, j))
                        ve.wait_ge(a_done.handle, a_done.at(i, j))
                        if j > 3:
                            ve.wait_ge(t_lo.handle, t_lo.at(i, j - 3))
                        vec.tensor_tensor(t32[(j - 1) % 3][:], C[:], a32[(j - 1) % 2][:], ALU.mult).then_inc(t_done.handle, 1)
                    if j < HT:
                        ve.wait_ge(u_ps.handle, u_ps.at(i, j + 1))
                        ve.wait_ge(silu_done.handle, silu_done.at(i, j + 1))
                        vec.tensor_tensor(a32[j % 2][:], U[j % 2][:], s32[j % 2][:], ALU.mult).then_inc(a_done.handle, 1)
                    if behind and j == 4:
                        add_x(i - 1)
                    if ahead and j in ahead_of:
                        ahead_of[j](nxt)
                if ahead:
                    move(nxt)

            first = 0
            for part in ahead_of.values():
                part(first)
            move(first)
            body(0, True, False)
            with ve.Fori(1, LAST) as i:
                body(i, True, True)
            body(LAST, False, True)
            add_x(LAST)

        @block.gpsimd
        def _(po):
            pool = nc.gpsimd

            def features(k):
                po.wait_ge(ex_done.handle, ex_done.at(k, 1))
                pool.tensor_tensor(feat[:], ex[:, 0:2 * TILE], pos_part[:], ALU.add).then_inc(feat_done.handle, 1)

            def scale_s(k):
                po.wait_ge(sl_done.handle, sl_done.at(k, 1))
                po.wait_ge(s_loaded.handle, s_loaded.at(k, 16))
                pool.tensor_tensor(ys[:], sl[:], s_cur[:], ALU.mult).then_inc(ys_done.handle, 1)

            def body(i, ahead, behind):
                for j in range(HT):
                    if behind and j == 1:
                        scale_s(i - 1)
                    po.wait_ge(t_hi.handle, t_hi.at(i, j + 1))
                    pool.tensor_tensor(t16[j % TBUF][:, 1, :], t32[j % 3][:], t16[j % TBUF][:, 0, :], ALU.subtract)\
                        .then_inc(t_lo.handle, 1)
                    if ahead and j == 11:
                        features(i + 1)

            features(0)
            body(0, True, False)
            with po.Fori(1, LAST) as i:
                body(i, True, True)
            body(LAST, False, True)
            scale_s(LAST)


def recurrent_depth_two_kernel(nc, x, wq, wk, wvgb, wo, norm_w, qk_w, qk_b, v_w, v_b, o_w, o_b, gamma1, gamma2, theta,
                               position, half_sign, router_w, router_b, w1, b1, w2, b2, wqkvo, bo, gate_w, wg, wu, wd,
                               eye, below, upto, future, spread1, spread2, number, block_mask, head_mask, out):
    tokens = x.shape[0]
    turns = tokens // TILE

    def activation(name, shape):
        return nc.dram_tensor(name, shape, F32, kind="Internal").ap()

    xn, x1 = activation("xn", (tokens, P)), activation("x1", (tokens, P))
    mixer, an, rest, mixer2 = (activation(n, (P, tokens)) for n in ("mixer", "an", "rest", "mixer2"))
    delta_phase(nc, x, wq, wk, wvgb, wo, norm_w, eye, below, upto, xn, mixer)
    attention_phase(nc, xn, qk_w, qk_b, v_w, v_b, o_w, o_b, gamma1, gamma2, theta, position, half_sign, eye, future,
                    an, rest, turns)
    experts_phase(nc, an, rest, mixer, x, router_w, router_b, w1, b1, w2, b2, spread1, number, eye, x1, turns)
    second_layer_phase(nc, x1, wqkvo, bo, gate_w, wg, wu, wd, spread2, number, block_mask, head_mask, eye, mixer2, out,
                       turns)


def kernel(**inputs):
    import concourse.bacc as bacc
    from concourse.bass_utils import run_bass_kernel_spmd

    L0 = {k[3:]: np.asarray(v) for k, v in inputs.items() if k.startswith("L0_")}
    L1 = {k[3:]: np.asarray(v) for k, v in inputs.items() if k.startswith("L1_")}
    x = L0["attn_x"]
    heads, hd = 16, 64

    even_odd = np.concatenate([np.arange(0, hd, 2), np.arange(1, hd, 2)])
    odd_even = np.concatenate([even_odd[hd // 2:], even_odd[:hd // 2]])

    def columns(w, order):
        return w.reshape(w.shape[:-1] + (heads, hd))[..., order].reshape(w.shape)

    def four(q, k):
        return [columns(q, even_odd), columns(q, odd_even), columns(k, even_odd), columns(k, odd_even)]

    ne = L0["ffn_re_w1"].shape[0]
    b2 = np.zeros((64, P), np.float32)
    b2[:ne], b2[ne], b2[32:32 + ne] = L0["ffn_re_b2"], L0["ffn_sh_b2"], L0["ffn_re_b2"]
    spread1 = np.zeros((64, ne + 1, P), np.float16)
    for e in range(ne + 1):
        spread1[e, e] = spread1[32 + e, e] = 1

    experts, _, inter = L1["ffn_Wg"].shape
    units = experts * inter + L1["ffn_Sg"].shape[1]
    padded = -(-units // P) * P

    def stack(w, shared):
        return np.concatenate([w.transpose(1, 0, 2).reshape(P, -1), shared, np.zeros((P, padded - units), np.float32)], 1)

    owner = np.minimum(np.arange(padded) // inter, experts)
    spread2 = np.zeros((64, padded), np.float16)
    spread2[owner, np.arange(padded)] = 1
    spread2[32 + owner[owner < experts], np.arange(padded)[owner < experts]] = 1

    args = {
        "x": x.reshape(-1, P), "wq": L0["attn_Wq"], "wk": L0["attn_Wk"],
        "wvgb": np.concatenate([L0["attn_Wv"], L0["attn_Wg"], L0["attn_Wb"]], 1),
        "wo": L0["attn_Wo"], "norm_w": L0["attn_norm_w"],
        "qk_w": np.concatenate(four(L0["ffn_q_w"], L0["ffn_k_w"]), 1),
        "qk_b": np.stack(four(L0["ffn_q_b"], L0["ffn_k_b"])).reshape(4, 8, P).transpose(2, 0, 1),
        "v_w": L0["ffn_v_w"], "v_b": L0["ffn_v_b"].reshape(8, P).T, "o_w": L0["ffn_o_w"], "o_b": L0["ffn_o_b"],
        "gamma1": L0["ffn_gamma1"], "gamma2": L0["ffn_gamma2"], "theta": np.tile(L0["ffn_theta"], 4)[:, None],
        "position": np.arange(SEQ, dtype=np.float32)[None],
        "half_sign": np.where((np.arange(P) // 32) % 2, 1, -1).astype(np.float32)[:, None],
        "router_w": L0["ffn_router_w"], "router_b": L0["ffn_router_b"],
        "w1": np.concatenate([L0["ffn_re_w1"], L0["ffn_sh_w1"][None]]),
        "b1": np.concatenate([L0["ffn_re_b1"], L0["ffn_sh_b1"][None]]).T,
        "w2": np.concatenate([L0["ffn_re_w2"], L0["ffn_sh_w2"][None]]), "b2": b2,
        "wqkvo": np.concatenate([L1["attn_wq"].T, L1["attn_wk"].T, L1["attn_wv"].T, L1["attn_wo"].T], 1),
        "bo": L1["attn_bo"], "gate_w": L1["ffn_gate_w"],
        "wg": stack(L1["ffn_Wg"], L1["ffn_Sg"]), "wu": stack(L1["ffn_Wu"], L1["ffn_Su"]),
        "wd": np.concatenate([L1["ffn_Wd"].reshape(-1, P), L1["ffn_Sd"], np.zeros((padded - units, P), np.float32)]),
        "eye": np.eye(P, dtype=np.float32), "below": np.tril(np.ones((P, P), np.float32), -1),
        "upto": np.triu(np.ones((P, P), np.float32)), "future": np.triu(np.full((P, P), -1e30, np.float32), 1),
        "spread1": spread1.reshape(64, -1), "spread2": spread2,
        "number": np.arange(ne, dtype=np.float32)[None],
        "block_mask": np.kron(np.eye(16), np.ones((8, 8))).astype(np.float32),
        "head_mask": np.kron(np.eye(16), np.ones((8, 1))).astype(np.float32),
    }
    nc = bacc.Bacc("TRN2", target_bir_lowering=False, num_devices=1)
    arrays, aps = {}, {}
    for name, a in args.items():
        arrays[f"in_{name}"] = np.ascontiguousarray(a)
        aps[name] = nc.dram_tensor(f"in_{name}", a.shape, mybir.dt.from_np(a.dtype), kind="ExternalInput").ap()
    out = nc.dram_tensor("out", (x.shape[0] * x.shape[1], P), F32, kind="ExternalOutput").ap()
    recurrent_depth_two_kernel(nc, out=out, **aps)
    result = run_bass_kernel_spmd(nc, [arrays], core_ids=[0])
    return result.results[0]["out"].reshape(x.shape)
```

```python
from contextlib import ExitStack

import concourse.bass as bass
import numpy as np
from concourse import mybir

ALU = mybir.AluOpType
ACT = mybir.ActivationFunctionType
F32 = mybir.dt.float32
F16 = mybir.dt.float16
BF16 = mybir.dt.bfloat16
AX = mybir.AxisListType.X

P = 128
SEQ = 256
TILE = 512
TB = TILE // P
SEQS = TILE // SEQ
EPS = 1e-5


class Signal:

    def __init__(self, handle, per, first=0):
        self.handle, self.per, self.first = handle, per, first

    def at(self, turn, n):
        return turn * self.per + (self.first + n)

    def before(self, turn, n=None):
        return turn * self.per + (self.first + (self.per if n is None else n) - self.per)


class Memory:

    def __init__(self, nc, ctx, name):
        self.nc, self.ctx, self.name, self.handles = nc, ctx, name, []
        ctx.callback(self.clear_semaphores)

    def sbuf(self, name, shape, dtype=F32):
        return self.ctx.enter_context(self.nc.sbuf_tensor(f"{self.name}_{name}", shape, dtype))

    def banks(self, name, n):
        return [self.ctx.enter_context(self.nc.psum_tensor(f"{self.name}_{name}_bank{k}", [P, 512], F32)) for k in range(n)]

    def count(self, name, per=1, first=0):
        self.handles.append(self.nc.alloc_semaphore(f"{self.name}_{name}"))
        return Signal(self.handles[-1], per, first)

    def clear_semaphores(self):
        self.nc.clear_and_free_semaphores(self.handles)
        self.nc.all_engine_barrier()


def split_product(pe, out, left, right, start=True, stop=True):
    (lh, ll), (rh, rl) = left, right
    pe.matmul(out, ll, rh, start=start, stop=False, skip_group_check=True)
    pe.matmul(out, lh, rl, start=False, stop=False, skip_group_check=True)
    return pe.matmul(out, lh, rh, start=False, stop=stop, skip_group_check=True)


def over(ap, n, axis=1):
    ap = ap.unsqueeze(axis)
    shape = list(ap.shape)
    shape[axis] = n
    return ap.to_broadcast(shape)


def delta_phase(nc, x, wq, wk, wvgb, wo, norm_w, eye, below, upto, xn_out, s_out):
    H, DK, DV = 4, 128, 32
    turns = x.shape[0] // TILE
    LEVELS = 7
    STEPS = LEVELS + 2
    X_STATS, X_ROOT, X_NORM, TURN_X = 0, 1, 2, 4
    KEYS, QUERIES, VALUES, TURN_KEYS = 7, 11, 15, 22
    SQUARE_O, ROOTS, RECIPROCALS, TURN_O, OUT = 3, 14, 14, 19, 21
    SCALE = DK ** -0.5
    x_v = x.rearrange("(n t p) d -> n p t d", t=TB, p=P)
    xn_v = xn_out.rearrange("(n t p) d -> n p t d", t=TB, p=P)
    s_v = s_out.rearrange("(n t p) d -> n p t d", t=TB, p=P)
    nv = wvgb.shape[1]

    with ExitStack() as ctx:
        m = Memory(nc, ctx, "delta")
        eye32, eye16 = m.sbuf("eye32", [P, P]), m.sbuf("eye16", [P, P], F16)
        below_m, upto_m = m.sbuf("below", [P, P]), m.sbuf("upto", [P, P])
        eps = m.sbuf("eps", [P, 2])
        norm_row = m.sbuf("norm_row", [P, DV])
        stage = m.sbuf("w_stage", [P, 512 + 512 + nv + 128])
        w_pair = m.sbuf("w_pair", [P, 2, 512 + 512 + nv + 128], F16)
        cut = {"q": (0, 512), "k": (512, 1024), "vgb": (1024, 1024 + nv), "o": (1024 + nv, 1152 + nv)}

        def weight(name, a=0, b=None):
            lo, hi = cut[name]
            b = hi - lo if b is None else b
            return w_pair[:, 0, lo + a:lo + b], w_pair[:, 1, lo + a:lo + b]

        x_in = m.sbuf("x_in", [P, TB, P])
        stats = m.sbuf("stats", [P, TB, 6])
        mean_var = m.sbuf("mean_var", [P, TB, 2])
        std = m.sbuf("std", [P, TB])
        rstd = m.sbuf("rstd", [P, TB])
        xn = m.sbuf("xn", [P, TB, P])
        xT = m.sbuf("xT", [P, 2, TILE], F16)
        k32 = [m.sbuf(f"k32_{t}", [P, H * DK]) for t in range(TB)]
        ksq = [m.sbuf(f"ksq{k}", [P, H * DK]) for k in range(2)]
        sums, roots, recips = (m.sbuf(n, [P, 2, TB * H]) for n in ("sums", "roots", "recips"))
        khat = [m.sbuf(f"khat{k}", [P, TB, H * DK]) for k in range(2)]
        kT = [m.sbuf(f"kT{k}", [P, 2, TB, H * P], F16) for k in range(2)]
        qT = [m.sbuf(f"qT{k}", [P, 2, H, TILE], F16) for k in range(2)]
        v = [m.sbuf(f"v{k}", [P, TB, H * DV]) for k in range(2)]
        g = m.sbuf("g", [P, TB, H * DV])
        gate = [m.sbuf(f"gate{k}", [P, TB, H * DV]) for k in range(2)]
        beta = [m.sbuf(f"beta{k}", [P, TB, H]) for k in range(2)]
        neg_beta = [m.sbuf(f"neg_beta{k}", [P, TB, H]) for k in range(2)]
        b32 = [m.sbuf(f"b32_{s}", [P, H * P]) for s in range(SEQS)]
        power = [[m.sbuf(f"power{s}_{k}", [P, 2, H * P], F16) for k in range(2)] for s in range(SEQS)]
        powerT = [[m.sbuf(f"powerT{s}_{k}", [P, 2, H * P], F16) for k in range(2)] for s in range(SEQS)]
        rhs32 = [m.sbuf(f"rhs32_{s}", [P, H * DV]) for s in range(SEQS)]
        rhs = [m.sbuf(f"rhs{s}", [P, 2, H * DV], F16) for s in range(SEQS)]
        qk = [m.sbuf(f"qk{s}", [P, H * P]) for s in range(SEQS)]
        upd = [m.sbuf(f"upd{s}", [P, H * DV]) for s in range(SEQS)]
        state = [m.sbuf(f"state{s}", [P, 2, H * DV], F16) for s in range(SEQS)]
        o = m.sbuf("o", [P, TB, H * DV])
        osq = m.sbuf("osq", [P, TB * H * DV])
        og = m.sbuf("og", [P, TB * H * DV])
        oT = m.sbuf("oT", [P, 2, TILE], F16)
        s_out_s = m.sbuf("s_out", [P, TB, P])

        pow_ps, powT_ps = m.banks("pow", 2), m.banks("powT", 2)
        rhs_ps, misc_ps = m.banks("rhs", 2), m.banks("misc", 2)

        S = m.count
        const_in = S("const_in")
        w_ready = S("w_ready")
        x_loaded = S("x_loaded", 16)
        stats_done, aggr_done = S("stats_done"), S("aggr_done")
        std_done, rstd_done = S("std_done"), S("rstd_done")
        xn_done, xn_stored = S("xn_done"), S("xn_stored", 16, 16)
        xT_ps_done, xT_hi, xT_lo = S("xT_ps_done"), S("xT_hi"), S("xT_lo")
        k_ps, k_copied, ksq_done, kss_done = (S(n, TB) for n in ("k_ps", "k_copied", "ksq_done", "kss_done"))
        roots_done, recips_done, khat_done = S("roots_done"), S("recips_done"), S("khat_done", TB)
        kT_ps, kT_hi, kT_lo = S("kT_ps", TB), S("kT_hi", TB), S("kT_lo", TB)
        q_ps, q_hi, q_lo = S("q_ps", H), S("q_hi", H), S("q_lo", H)
        v_ps, g_sig, gate_half, gate_done = S("v_ps", TB), S("g_sig", TB), S("gate_half"), S("gate_done")
        negb_done = S("negb_done", 1)
        gram_ps, b32_done, b_hi, b_lo = S("gram_ps", TB), S("b32_done", TB), S("b_hi", TB), S("b_lo", TB)
        qk_ps, qk_done = S("qk_ps", TB), S("qk_done", TB)
        bT_ps, bT_done = S("bT_ps", TB), S("bT_done", TB)
        ks_ps, rhs_sub, rhs32_done = S("ks_ps", SEQS), S("rhs_sub", SEQS), S("rhs32_done", TB)
        NR = TB * LEVELS
        rhs_hi, rhs_lo = S("rhs_hi", NR), S("rhs_lo", NR)
        rhs_step = S("rhs_step", TB * LEVELS)
        NP = TB * (LEVELS - 2)
        NT = TB * (LEVELS - 1)
        pow_step, pow_hi, pow_lo = S("pow_step", NP), S("pow_hi", NP), S("pow_lo", NP)
        powT_step, powT_hi, powT_lo = S("powT_step", NT), S("powT_hi", NT), S("powT_lo", NT)
        upd_done = S("upd_done", TB)
        state_hi, state_lo = S("state_hi", SEQS), S("state_lo", SEQS)
        o_ps, o_out = S("o_ps", TB), S("o_out", TB)
        osq_done, oss_done = S("osq_done"), S("oss_done")
        on_done, og_done = S("on_done"), S("og_done", 1)
        oT_ps, oT_hi, oT_lo = S("oT_ps"), S("oT_hi"), S("oT_lo")
        s_ps, s_copied, s_stored = S("s_ps"), S("s_copied"), S("s_stored", 16, 16)
        eps_set = S("eps_set")
        order = S("order")

        block = ctx.enter_context(nc.Block())

        @block.sync
        def _(sp):
            for dst, src in ((stage[:, 0:512], wq), (stage[:, 512:1024], wk), (stage[:, 1024:1024 + nv], wvgb),
                             (stage[:, 1024 + nv:], wo), (eye32[:], eye), (below_m[:], below), (upto_m[:], upto),
                             (norm_row[:], norm_w.rearrange("(a d) -> a d", a=1).to_broadcast([P, DV]))):
                sp.dma_start(dst, src).then_inc(const_in.handle, 16)
            sp.sem_inc(xn_stored.handle, 16)
            sp.sem_inc(s_stored.handle, 16)
            def load(k):
                sp.dma_start(x_in[:], x_v[k]).then_inc(x_loaded.handle, 16)

            def store(k):
                sp.wait_ge(xn_done.handle, xn_done.at(k, 1))
                sp.dma_start(xn_v[k], xn[:]).then_inc(xn_stored.handle, 16)

            load(0)
            store(0)
            load(1)
            store(1)
            with sp.Fori(2, turns) as i:
                load(i)
                store(i)
            sp.wait_ge(xn_stored.handle, 16 * (turns + 1))
            sp.wait_ge(s_stored.handle, 16 * (turns + 1))

        def turn_by_turn(eng, body):
            body(-1, 1, now=False, ahead=True, behind=False)
            body(0, 0, now=True, ahead=True, behind=False)
            with eng.Fori(1, turns - 1, 2) as i:
                body(i, 1, now=True, ahead=True, behind=True)
                body(i + 1, 0, now=True, ahead=True, behind=True)
            body(turns - 1, 1, now=True, ahead=False, behind=True)
            body(turns, 0, now=False, ahead=False, behind=True)

        def copies(c, level, s):
            return (c * LEVELS + level) * SEQS + s + 1

        def squares(c, level, s, levels):
            return (c * levels + level) * SEQS + s + 1

        def power_columns(level):
            return P // 2 if level == LEVELS - 1 else P

        def pair(buf, at, width=P):
            return buf[:, 0, at:at + width], buf[:, 1, at:at + width]

        @block.tensor
        def _(te):
            pe = nc.tensor
            te.wait_ge(const_in.handle, 16 * 8)
            te.wait_ge(w_ready.handle, 3)

            def body(i, odd, now, ahead, behind):
                even = 1 - odd

                def matrices(c, s):
                    t, n = 2 * s + c, 2 * c + s
                    kt = [(kT[odd][:, 0, t, h * P:(h + 1) * P], kT[odd][:, 1, t, h * P:(h + 1) * P]) for h in range(H)]
                    if n == 0:
                        te.wait_ge(kT_lo.handle, kT_lo.at(i, TB))
                        te.wait_ge(q_lo.handle, q_lo.at(i, H))
                    for h in range(H):
                        last = split_product(pe, pow_ps[s][:, h * P:(h + 1) * P], kt[h], kt[h])
                    last.then_inc(gram_ps.handle, 1)
                    for h in range(H):
                        q = (qT[odd][:, 0, h, t * P:(t + 1) * P], qT[odd][:, 1, h, t * P:(t + 1) * P])
                        last = split_product(pe, powT_ps[s][:, h * P:(h + 1) * P], kt[h], q)
                    last.then_inc(qk_ps.handle, 1)
                    if c == 1:
                        te.wait_ge(state_lo.handle, state_lo.at(i, s + 1))
                        for h in range(H):
                            last = split_product(pe, rhs_ps[s][:, h * DV:(h + 1) * DV], kt[h], pair(state[s], h * DV, DV))
                        last.then_inc(ks_ps.handle, 1)

                def begin_solving(c, s):
                    n = 2 * c + s
                    te.wait_ge(b_lo.handle, b_lo.at(i, n + 1))
                    tr = pow_ps[s][:].bitcast(F16)
                    for half in range(2):
                        for h in range(H):
                            at = (half * H + h) * P
                            last = pe.transpose(tr[:, at:at + P], power[s][0][:, half, h * P:(h + 1) * P], eye16[:])
                    last.then_inc(bT_ps.handle, 1)
                    te.wait_ge(rhs_lo.handle, rhs_lo.at(i, copies(c, 0, s)))
                    if c == 0 and behind:
                        te.wait_ge(o_out.handle, o_out.at(i, s - 1))
                    pe.matmul(rhs_ps[s][:, 0:H * DV], eye16[:], rhs[s][:, 1, :], start=True, stop=False, skip_group_check=True)
                    pe.matmul(rhs_ps[s][:, 0:H * DV], eye16[:], rhs[s][:, 0, :], start=False, stop=False, skip_group_check=True)

                def solve(c, level, s):
                    pw, pT = power[s][level % 2], powerT[s][level % 2]
                    if level == 0:
                        te.wait_ge(bT_done.handle, bT_done.at(i, 2 * c + s + 1))
                    else:
                        te.wait_ge(powT_lo.handle, powT_lo.at(i, squares(c, level - 1, s, LEVELS - 1)))
                        te.wait_ge(rhs_lo.handle, rhs_lo.at(i, copies(c, level, s)))
                    n = power_columns(level)
                    for h in range(H):
                        last = split_product(pe, rhs_ps[s][P - n:, h * DV:(h + 1) * DV], pair(pT, h * n, n),
                                             pair(rhs[s], h * DV, DV), start=False, stop=(level == LEVELS - 1))
                    last.then_inc(rhs_step.handle, 1)
                    if level == LEVELS - 1:
                        return
                    if level == 0:
                        te.wait_ge(qk_done.handle, qk_done.at(i, 2 * c + s + 1))
                    else:
                        te.wait_ge(pow_lo.handle, pow_lo.at(i, squares(c, level - 1, s, LEVELS - 2)))
                    n = power_columns(level + 1)
                    for h in range(H):
                        last = split_product(pe, powT_ps[s][:, h * n:(h + 1) * n], pair(pw, h * P), pair(pT, (h + 1) * P - n, n))
                    last.then_inc(powT_step.handle, 1)
                    if level < LEVELS - 2:
                        for h in range(H):
                            last = split_product(pe, pow_ps[s][:, h * P:(h + 1) * P], pair(pT, h * P), pair(pw, h * P))
                        last.then_inc(pow_step.handle, 1)

                def results(c, s):
                    t, n = 2 * s + c, 2 * c + s
                    te.wait_ge(upd_done.handle, upd_done.at(i, n + 1))
                    if c == 0:
                        for h in range(H):
                            pe.matmul(rhs_ps[s][:, h * DV:(h + 1) * DV], khat[odd][:, t, h * DK:(h + 1) * DK],
                                      upd[s][:, h * DV:(h + 1) * DV], start=True, stop=True)
                    for h in range(H):
                        out = rhs_ps[s][:, 2 * P + h * DV:2 * P + (h + 1) * DV]
                        if c == 1:
                            q = (qT[odd][:, 0, h, t * P:(t + 1) * P], qT[odd][:, 1, h, t * P:(t + 1) * P])
                            split_product(pe, out, q, pair(state[s], h * DV, DV), stop=False)
                        last = pe.matmul(out, qk[s][:, h * P:(h + 1) * P], upd[s][:, h * DV:(h + 1) * DV],
                                         start=(c == 0), stop=True, skip_group_check=True)
                    last.then_inc(o_ps.handle, 1)

                def extras(p):
                    bank = misc_ps[p % 2]
                    if ahead and p == TURN_X:
                        te.wait_ge(xn_done.handle, xn_done.at(i + 1, 1))
                        for t in range(TB):
                            last = pe.transpose(bank[:, t * P:(t + 1) * P], xn[:, t, :], eye32[:])
                        last.then_inc(xT_ps_done.handle, 1)
                    if ahead and KEYS <= p < KEYS + TB:
                        t = p - KEYS
                        if t == 0:
                            te.wait_ge(xT_lo.handle, xT_lo.at(i + 1, 1))
                        if t >= 2:
                            te.wait_ge(k_copied.handle, k_copied.at(i + 1, t - 1))
                        split_product(pe, bank[:], pair(xT, t * P), weight("k")).then_inc(k_ps.handle, 1)
                    if ahead and QUERIES <= p < QUERIES + H:
                        h = p - QUERIES
                        if h < 2:
                            te.wait_ge(k_copied.handle, k_copied.at(i + 1, TB - 1 + h))
                        else:
                            te.wait_ge(q_lo.handle, q_lo.at(i + 1, h - 1))
                        split_product(pe, bank[:], weight("q", h * DK, (h + 1) * DK), (xT[:, 0, :], xT[:, 1, :]))\
                            .then_inc(q_ps.handle, 1)
                    if ahead and VALUES <= p < VALUES + TB:
                        t = p - VALUES
                        if t < 2:
                            te.wait_ge(q_lo.handle, q_lo.at(i + 1, H - 1 + t))
                        else:
                            te.wait_ge(g_sig.handle, g_sig.at(i + 1, t - 1))
                        split_product(pe, bank[:, 0:nv], pair(xT, t * P), weight("vgb")).then_inc(v_ps.handle, 1)
                    if ahead and p in (TURN_O, TURN_KEYS):
                        te.wait_ge(g_sig.handle, g_sig.at(i + 1, TB))
                    if behind and p == TURN_O:
                        te.wait_ge(og_done.handle, og_done.at(i, 0))
                        for t in range(TB):
                            last = pe.transpose(bank[:, t * P:(t + 1) * P], og[:, t * P:(t + 1) * P], eye32[:])
                        last.then_inc(oT_ps.handle, 1)
                    if behind and p == OUT:
                        te.wait_ge(oT_lo.handle, oT_lo.at(i, 0))
                        for t in range(TB):
                            last = split_product(pe, bank[:, t * P:(t + 1) * P], pair(oT, t * P), weight("o"))
                        last.then_inc(s_ps.handle, 1)
                    if ahead and TURN_KEYS <= p < TURN_KEYS + TB:
                        t = p - TURN_KEYS
                        te.wait_ge(khat_done.handle, khat_done.at(i + 1, t + 1))
                        if t == 1 and behind:
                            te.wait_ge(s_copied.handle, s_copied.at(i, 0))
                        if t >= 2:
                            te.wait_ge(kT_lo.handle, kT_lo.at(i + 1, t - 1))
                        for h in range(H):
                            last = pe.transpose(bank[:, h * P:(h + 1) * P], khat[even][:, t, h * DK:(h + 1) * DK], eye32[:])
                        last.then_inc(kT_ps.handle, 1)

                for p in range(2 * STEPS * SEQS):
                    c, step, s = p // 2 // STEPS, p // 2 % STEPS, p % 2
                    if now and step == 0:
                        matrices(c, s)
                    if now and step == 1 and s == 0:
                        begin_solving(c, 0)
                        begin_solving(c, 1)
                    if now and 1 <= step <= LEVELS:
                        solve(c, step - 1, s)
                    if now and step == LEVELS + 1:
                        results(c, s)
                    extras(p)

            turn_by_turn(te, body)

        @block.scalar
        def _(ac):
            act = nc.scalar.activation
            ac.wait_ge(const_in.handle, 16 * 8)
            act(w_pair[:, 0, :], stage[:], ACT.Copy).then_inc(w_ready.handle, 1)
            act(eye16[:], eye32[:], ACT.Copy).then_inc(w_ready.handle, 1)
            ac.wait_ge(eps_set.handle, 2)

            def body(i, odd, now, ahead, behind):
                even = 1 - odd

                def extras(p):
                    if ahead and p == X_ROOT:
                        ac.wait_ge(aggr_done.handle, aggr_done.at(i + 1, 1))
                        act(std[:], mean_var[:, :, 1], ACT.Sqrt, bias=eps[:, 0:1]).then_inc(std_done.handle, 1)
                    if behind and p == SQUARE_O:
                        ac.wait_ge(o_out.handle, o_out.at(i, 0))
                        act(osq[:], o[:].rearrange("p t n -> p (t n)"), ACT.Square).then_inc(osq_done.handle, 1)
                    if ahead and p == TURN_X + 1:
                        ac.wait_ge(xT_ps_done.handle, xT_ps_done.at(i + 1, 1))
                        if now:
                            ac.wait_ge(v_ps.handle, v_ps.at(i, TB))
                        act(xT[:, 0, :], misc_ps[TURN_X % 2][:], ACT.Copy).then_inc(xT_hi.handle, 1)
                    if ahead and KEYS <= p - 1 < KEYS + TB:
                        t = p - 1 - KEYS
                        ac.wait_ge(k_ps.handle, k_ps.at(i + 1, t + 1))
                        if now:
                            ac.wait_ge(khat_done.handle, khat_done.at(i, t + 1))
                        act(k32[t][:], misc_ps[(p - 1) % 2][:], ACT.Copy).then_inc(k_copied.handle, 1)
                    if ahead and QUERIES <= p - 1 < QUERIES + H:
                        h = p - 1 - QUERIES
                        ac.wait_ge(q_ps.handle, q_ps.at(i + 1, h + 1))
                        act(qT[even][:, 0, h, :], misc_ps[(p - 1) % 2][:], ACT.Copy, scale=SCALE).then_inc(q_hi.handle, 1)
                    if p == ROOTS and ahead:
                        ac.wait_ge(kss_done.handle, kss_done.at(i + 1, TB))
                        last = act(roots[:, 0, :], sums[:, 0, :], ACT.Sqrt, bias=eps[:, 1:2])
                    if p == ROOTS and behind:
                        ac.wait_ge(oss_done.handle, oss_done.at(i, 0))
                        last = act(roots[:, 1, :], sums[:, 1, :], ACT.Sqrt, bias=eps[:, 0:1], scale=1.0 / DV)
                    if p == ROOTS and (ahead or behind):
                        last.then_inc(roots_done.handle, 1)
                    if ahead and VALUES <= p - 1 < VALUES + TB:
                        t, bank = p - 1 - VALUES, misc_ps[(p - 1) % 2]
                        ac.wait_ge(v_ps.handle, v_ps.at(i + 1, t + 1))
                        if behind and t == 0:
                            ac.wait_ge(og_done.handle, og_done.at(i, 0))
                        if now and t == 0:
                            ac.wait_ge(gate_done.handle, gate_done.at(i, 1))
                        act(v[even][:, t, :], bank[:, 0:128], ACT.Copy)
                        act(g[:, t, :], bank[:, 128:256], ACT.Copy)
                        act(gate[even][:, t, :], bank[:, 128:256], ACT.Sigmoid)
                        act(beta[even][:, t, :], bank[:, 256:260], ACT.Sigmoid).then_inc(g_sig.handle, 1)
                    if behind and p == TURN_O + 1:
                        ac.wait_ge(oT_ps.handle, oT_ps.at(i, 0))
                        act(oT[:, 0, :], misc_ps[TURN_O % 2][:], ACT.Copy).then_inc(oT_hi.handle, 1)
                    if behind and p == OUT + 1:
                        ac.wait_ge(s_ps.handle, s_ps.at(i, 0))
                        ac.wait_ge(s_stored.handle, s_stored.at(i - 1, 0))
                        act(s_out_s[:].rearrange("p t d -> p (t d)"), misc_ps[OUT % 2][:], ACT.Copy).then_inc(s_copied.handle, 1)
                        ac.wait_ge(s_copied.handle, s_copied.at(i, 0))
                        ac.dma_start(s_v[i - 1], s_out_s[:]).then_inc(s_stored.handle, 16)
                    if ahead and TURN_KEYS <= p - 1 < TURN_KEYS + TB:
                        t = p - 1 - TURN_KEYS
                        ac.wait_ge(kT_ps.handle, kT_ps.at(i + 1, t + 1))
                        act(kT[even][:, 0, t, :], misc_ps[(p - 1) % 2][:], ACT.Copy).then_inc(kT_hi.handle, 1)

                def solver(c, step, s):
                    n, level = 2 * c + s, step - 1
                    if step == 0:
                        ac.wait_ge(b32_done.handle, b32_done.at(i, n + 1))
                        act(power[s][0][:, 0, :], b32[s][:], ACT.Copy).then_inc(b_hi.handle, 1)
                        ac.wait_ge(rhs32_done.handle, rhs32_done.at(i, n + 1))
                        act(rhs[s][:, 0, :], rhs32[s][:], ACT.Copy).then_inc(rhs_hi.handle, 1)
                        return
                    if level == 0 and s == 0:
                        for other in range(SEQS):
                            ac.wait_ge(bT_ps.handle, bT_ps.at(i, 2 * c + other + 1))
                            act(powerT[other][0][:].rearrange("p a n -> p (a n)"), pow_ps[other][:].bitcast(F16), ACT.Copy)\
                                .then_inc(bT_done.handle, 1)
                    if level < LEVELS:
                        ac.wait_ge(rhs_step.handle, rhs_step.at(i, copies(c, level, s)))
                    if level < LEVELS - 1:
                        new, n = (level + 1) % 2, power_columns(level + 1)
                        act(rhs[s][:, 0, :], rhs_ps[s][:, 0:H * DV], ACT.Copy).then_inc(rhs_hi.handle, 1)
                        ac.wait_ge(powT_step.handle, powT_step.at(i, squares(c, level, s, LEVELS - 1)))
                        act(powerT[s][new][:, 0, 0:H * n], powT_ps[s][:, 0:H * n], ACT.Copy).then_inc(powT_hi.handle, 1)
                    if level < LEVELS - 2:
                        ac.wait_ge(pow_step.handle, pow_step.at(i, squares(c, level, s, LEVELS - 2)))
                        act(power[s][new][:, 0, :], pow_ps[s][:], ACT.Copy).then_inc(pow_hi.handle, 1)
                    if level == LEVELS - 1:
                        act(upd[s][:], rhs_ps[s][:, 0:H * DV], ACT.Copy).then_inc(upd_done.handle, 1)
                    if level == LEVELS:
                        ac.wait_ge(o_ps.handle, o_ps.at(i, 2 * c + s + 1))
                        if c == 0 and s == 0 and behind:
                            ac.wait_ge(og_done.handle, og_done.at(i, 0))
                        act(o[:, 2 * s + c, :], rhs_ps[s][:, 2 * P:2 * P + H * DV], ACT.Copy).then_inc(o_out.handle, 1)
                        if c == 0:
                            act(state[s][:, 0, :], rhs_ps[s][:, 0:H * DV], ACT.Copy).then_inc(state_hi.handle, 1)

                for p in range(2 * STEPS * SEQS):
                    extras(p)
                    if now:
                        solver(p // 2 // STEPS, p // 2 % STEPS, p % 2)

            turn_by_turn(ac, body)

        @block.vector
        def _(ve):
            vec = nc.vector
            vec.memset(eps[:, 0:1], EPS).then_inc(eps_set.handle, 1)
            vec.memset(eps[:, 1:2], 1e-12).then_inc(eps_set.handle, 1)
            ve.wait_ge(w_ready.handle, 2)
            ve.wait_ge(const_in.handle, 16 * 8)
            vec.tensor_tensor(w_pair[:, 1, :], stage[:], w_pair[:, 0, :], ALU.subtract).then_inc(w_ready.handle, 1)

            def low(out, exact, high):
                return vec.tensor_tensor(out, exact, high, ALU.subtract)

            def body(i, odd, now, ahead, behind):
                even = 1 - odd

                def extras(p):
                    if ahead and p == X_STATS:
                        ve.wait_ge(x_loaded.handle, x_loaded.at(i + 1, 16))
                        for t in range(TB):
                            last = vec.bn_stats(stats[:, t, :], x_in[:, t, :])
                        last.then_inc(stats_done.handle, 1)
                        ve.wait_ge(stats_done.handle, stats_done.at(i + 1, 1))
                        ve.sem_inc(order.handle, 1)
                        for t in range(TB):
                            last = vec.bn_aggr(mean_var[:, t, :], stats[:, t, :])
                        last.then_inc(aggr_done.handle, 1)
                    if ahead and p == X_NORM:
                        ve.wait_ge(std_done.handle, std_done.at(i + 1, 1))
                        vec.reciprocal(rstd[:], std[:]).then_inc(rstd_done.handle, 1)
                        ve.wait_ge(rstd_done.handle, rstd_done.at(i + 1, 1))
                        ve.wait_ge(xn_stored.handle, xn_stored.at(i + 1, 0))
                        if now:
                            ve.wait_ge(xT_ps_done.handle, xT_ps_done.at(i, 1))
                        for t in range(TB):
                            last = vec.tensor_scalar(xn[:, t, :], x_in[:, t, :], mean_var[:, t, 0:1], rstd[:, t:t + 1],
                                                     ALU.subtract, ALU.mult)
                        last.then_inc(xn_done.handle, 1)
                    if behind and p == SQUARE_O + 2:
                        ve.wait_ge(osq_done.handle, osq_done.at(i, 0))
                        vec.tensor_reduce(sums[:, 1, :], osq[:].rearrange("p (n d) -> p n d", d=DV), AX, ALU.add)\
                           .then_inc(oss_done.handle, 1)
                    if ahead and p == TURN_X + 1:
                        ve.wait_ge(xT_hi.handle, xT_hi.at(i + 1, 1))
                        low(xT[:, 1, :], misc_ps[TURN_X % 2][:], xT[:, 0, :]).then_inc(xT_lo.handle, 1)
                    if ahead and KEYS <= p - 3 < KEYS + TB:
                        t = p - 3 - KEYS
                        ve.wait_ge(ksq_done.handle, ksq_done.at(i + 1, t + 1))
                        vec.tensor_reduce(sums[:, 0, t * H:(t + 1) * H], ksq[t % 2][:].rearrange("p (h d) -> p h d", h=H),
                                          AX, ALU.add).then_inc(kss_done.handle, 1)
                    if ahead and QUERIES <= p - 1 < QUERIES + H:
                        h = p - 1 - QUERIES
                        ve.wait_ge(q_hi.handle, q_hi.at(i + 1, h + 1))
                        vec.scalar_tensor_tensor(out=qT[even][:, 1, h, :], in0=misc_ps[(p - 1) % 2][:], scalar=SCALE,
                                                 in1=qT[even][:, 0, h, :], op0=ALU.mult, op1=ALU.subtract)\
                           .then_inc(q_lo.handle, 1)
                    if p == RECIPROCALS and (ahead or behind):
                        ve.wait_ge(roots_done.handle, roots_done.at(i + 1, 1))
                        a, b = (0 if ahead else 1), (2 if behind else 1)
                        vec.reciprocal(recips[:, a:b, :], roots[:, a:b, :]).then_inc(recips_done.handle, 1)
                    if ahead and p == VALUES + TB + 1:
                        ve.wait_ge(g_sig.handle, g_sig.at(i + 1, TB))
                        vec.tensor_scalar(neg_beta[even][:], beta[even][:], -1.0, None, ALU.mult).then_inc(negb_done.handle, 1)
                    if behind and p == TURN_O + 1:
                        ve.wait_ge(oT_hi.handle, oT_hi.at(i, 0))
                        low(oT[:, 1, :], misc_ps[TURN_O % 2][:], oT[:, 0, :]).then_inc(oT_lo.handle, 1)
                    if ahead and TURN_KEYS <= p - 1 < TURN_KEYS + TB:
                        t = p - 1 - TURN_KEYS
                        ve.wait_ge(kT_hi.handle, kT_hi.at(i + 1, t + 1))
                        low(kT[even][:, 1, t, :], misc_ps[(p - 1) % 2][:], kT[even][:, 0, t, :]).then_inc(kT_lo.handle, 1)

                def matrices(c, s):
                    t, n = 2 * s + c, 2 * c + s
                    bt = over(beta[odd][:, t, :], DV, 2)
                    r3 = rhs32[s][:].rearrange("p (h d) -> p h d", h=H)
                    ve.wait_ge(gram_ps.handle, gram_ps.at(i, n + 1))
                    if n == 0:
                        ve.wait_ge(negb_done.handle, negb_done.at(i, 1))
                    for h in range(H):
                        last = vec.scalar_tensor_tensor(out=b32[s][:, h * P:(h + 1) * P], in0=pow_ps[s][:, h * P:(h + 1) * P],
                                                        scalar=neg_beta[odd][:, t, h:h + 1], in1=below_m[:],
                                                        op0=ALU.mult, op1=ALU.mult)
                    last.then_inc(b32_done.handle, 1)
                    if c == 0:
                        vec.tensor_tensor(r3, v[odd][:, t, :].rearrange("p (h d) -> p h d", h=H), bt, ALU.mult)\
                           .then_inc(rhs32_done.handle, 1)
                    else:
                        ve.wait_ge(ks_ps.handle, ks_ps.at(i, s + 1))
                        vec.tensor_tensor(rhs32[s][:], v[odd][:, t, :], rhs_ps[s][:, 0:H * DV], ALU.subtract)\
                           .then_inc(rhs_sub.handle, 1)
                        ve.wait_ge(rhs_sub.handle, rhs_sub.at(i, s + 1))
                        vec.tensor_tensor(r3, r3, bt, ALU.mult).then_inc(rhs32_done.handle, 1)
                    ve.wait_ge(qk_ps.handle, qk_ps.at(i, n + 1))
                    vec.tensor_tensor(qk[s][:].rearrange("p (h n) -> p h n", h=H), powT_ps[s][:].rearrange("p (h n) -> p h n", h=H),
                                      over(upto_m[:], H), ALU.mult).then_inc(qk_done.handle, 1)
                    ve.wait_ge(rhs_hi.handle, rhs_hi.at(i, copies(c, 0, s)))
                    low(rhs[s][:, 1, :], rhs32[s][:], rhs[s][:, 0, :]).then_inc(rhs_lo.handle, 1)

                def solver(c, step, s):
                    level, new = step - 1, step % 2
                    if step == 0:
                        matrices(c, s)
                    elif level < LEVELS - 1:
                        ve.wait_ge(rhs_hi.handle, rhs_hi.at(i, copies(c, level + 1, s)))
                        low(rhs[s][:, 1, :], rhs_ps[s][:, 0:H * DV], rhs[s][:, 0, :]).then_inc(rhs_lo.handle, 1)
                        ve.wait_ge(powT_hi.handle, powT_hi.at(i, squares(c, level, s, LEVELS - 1)))
                        cut = slice(0, H * power_columns(level + 1))
                        low(powerT[s][new][:, 1, cut], powT_ps[s][:, cut], powerT[s][new][:, 0, cut]).then_inc(powT_lo.handle, 1)
                        if level < LEVELS - 2:
                            ve.wait_ge(pow_hi.handle, pow_hi.at(i, squares(c, level, s, LEVELS - 2)))
                            low(power[s][new][:, 1, :], pow_ps[s][:], power[s][new][:, 0, :]).then_inc(pow_lo.handle, 1)
                    elif level == LEVELS and c == 0:
                        ve.wait_ge(state_hi.handle, state_hi.at(i, s + 1))
                        low(state[s][:, 1, :], rhs_ps[s][:, 0:H * DV], state[s][:, 0, :]).then_inc(state_lo.handle, 1)

                for p in range(2 * STEPS * SEQS):
                    extras(p)
                    if now:
                        solver(p // 2 // STEPS, p // 2 % STEPS, p % 2)

            turn_by_turn(ve, body)

        @block.gpsimd
        def _(po):
            pool = nc.gpsimd

            def body(i, odd, now, ahead, behind):
                even = 1 - odd
                for p in range(2 * STEPS * SEQS):
                    c, step, s = p // 2 // STEPS, p // 2 % STEPS, p % 2
                    if ahead and KEYS <= p - 1 < KEYS + TB:
                        t = p - 1 - KEYS
                        po.wait_ge(k_copied.handle, k_copied.at(i + 1, t + 1))
                        if t >= 2:
                            po.wait_ge(kss_done.handle, kss_done.at(i + 1, t - 1))
                        pool.tensor_tensor(ksq[t % 2][:], k32[t][:], k32[t][:], ALU.mult).then_inc(ksq_done.handle, 1)
                    if p == RECIPROCALS and (ahead or behind):
                        po.wait_ge(recips_done.handle, recips_done.at(i + 1, 1))
                    if behind and p == RECIPROCALS:
                        if now:
                            po.wait_ge(gate_done.handle, gate_done.at(i, 0))
                        pool.tensor_tensor(og[:].rearrange("p (n d) -> p n d", d=DV),
                                           o[:].rearrange("p t (h d) -> p (t h) d", d=DV), over(recips[:, 1, :], DV, 2), ALU.mult)\
                            .then_inc(on_done.handle, 1)
                        po.wait_ge(on_done.handle, on_done.at(i, 0))
                        pool.tensor_tensor(og[:], og[:], gate[even][:].rearrange("p t n -> p (t n)"), ALU.mult)\
                            .then_inc(og_done.handle, 1)
                    if ahead and RECIPROCALS + 1 <= p < RECIPROCALS + 1 + TB:
                        t = p - RECIPROCALS - 1
                        pool.tensor_tensor(khat[even][:, t, :].rearrange("p (h d) -> p h d", h=H),
                                           k32[t][:].rearrange("p (h d) -> p h d", h=H),
                                           over(recips[:, 0, t * H:(t + 1) * H], DK, 2), ALU.mult).then_inc(khat_done.handle, 1)
                    if ahead and p == VALUES + TB + 1:
                        po.wait_ge(g_sig.handle, g_sig.at(i + 1, TB))
                        pool.tensor_tensor(gate[even][:], gate[even][:], g[:], ALU.mult).then_inc(gate_half.handle, 1)
                        po.wait_ge(gate_half.handle, gate_half.at(i + 1, 1))
                        pool.tensor_tensor(gate[even][:].rearrange("p t (h d) -> p (t h) d", d=DV),
                                           gate[even][:].rearrange("p t (h d) -> p (t h) d", d=DV),
                                           over(norm_row[:], TB * H), ALU.mult).then_inc(gate_done.handle, 1)
                    if now and step == 0:
                        n = 2 * c + s
                        po.wait_ge(b_hi.handle, b_hi.at(i, n + 1))
                        pool.tensor_tensor(power[s][0][:, 1, :], b32[s][:], power[s][0][:, 0, :], ALU.subtract)\
                            .then_inc(b_lo.handle, 1)

            turn_by_turn(po, body)


def attention_phase(nc, xn_in, qk_w, qk_b, v_w, v_b, o_w, o_b, gamma1, gamma2, theta, position, half_sign,
                    eye, future, an_out, rest_out, turns):
    HEADS, HD, PAIRS = 16, 64, 8
    xn_v = xn_in.rearrange("(n t p) d -> n p t d", t=TB, p=P)
    TWO_PI = 6.283185307179586
    C1 = 6.28125
    C2 = float(np.float32(np.round((TWO_PI - C1) * 2 ** 21) / 2 ** 21))
    C3 = TWO_PI - C1 - C2
    ROUND = 1.5 * 2.0 ** 23
    UNITS = PAIRS * SEQS * 2
    NP = 2 * PAIRS
    RING = 4
    LAST = turns - 1
    CLOSE_O, CLOSE_SQUARE, CLOSE_SUM, ROOTS, RECIPROCALS, SCALES = 7, 9, 11, 12, 13, 14
    TURN_X, X_SPLIT = 19, 23
    V_SLOTS = {25: 0, 27: 1, 29: 2, 31: 3, 5: 4, 9: 5, 13: 6, 15: 7}

    with ExitStack() as ctx:
        m = Memory(nc, ctx, "attn")
        eye32, future_m = m.sbuf("eye32", [P, P]), m.sbuf("future32", [P, P])
        eyeb, futureb = m.sbuf("eyeb", [P, P], BF16), m.sbuf("futureb", [P, P], BF16)
        ones = m.sbuf("ones", [P, P])
        eps = m.sbuf("eps", [P, 1])
        gam1, gam2, ob = m.sbuf("gam1", [P, 1]), m.sbuf("gam2", [P, 1]), m.sbuf("ob", [P, 1])
        vb = m.sbuf("vb", [P, PAIRS])
        qkb = m.sbuf("qkb", [P, 4, PAIRS])
        th, sign = m.sbuf("th", [P, 1]), m.sbuf("sign", [P, 1])
        pos = m.sbuf("pos", [P, SEQ])
        ang = [m.sbuf(f"ang{k}", [P, SEQ]) for k in range(4)]
        table = m.sbuf("table", [P, 2, 2, SEQ])
        stage = m.sbuf("w_stage", [P, 6 * 1024])
        qkw = m.sbuf("qkw", [P, 2, 4 * 1024], F16)
        vw = m.sbuf("vw", [P, 2, 1024], F16)
        ow = m.sbuf("ow", [P, 2, 1024], F16)

        xn = m.sbuf("xn", [P, TB, P])
        sq = m.sbuf("sq", [P, TB * P])
        ss = m.sbuf("ss", [P, TB])
        std, rr = m.sbuf("std", [P, 2 * TB]), m.sbuf("rr", [P, 2 * TB])
        x2 = m.sbuf("x2", [P, TB, P])
        x2T, res = m.sbuf("x2T", [P, TILE]), m.sbuf("res", [P, TILE])
        xT = m.sbuf("xT", [P, 2, TILE], F16)
        V = m.sbuf("V", [P, TB, HEADS, HD + 1])
        rope1 = [m.sbuf(f"rope1{w}", [P, TILE]) for w in range(2)]
        rope2 = [m.sbuf(f"rope2{w}", [P, TILE]) for w in range(2)]
        rot = [m.sbuf(f"rot{w}", [P, TILE]) for w in range(2)]
        qk = [[m.sbuf(f"qk{w}_{k}", [P, 2, TILE], F16) for k in range(RING)] for w in range(2)]
        nmax = [m.sbuf(f"nmax{k}", [P, 3]) for k in range(RING)]
        prob = [m.sbuf(f"prob{k}", [P, 384]) for k in range(RING)]
        probT = [m.sbuf(f"probT{k}", [P, 384]) for k in range(RING)]
        rden = m.sbuf("rden", [P, SEQS, 4])
        ctxn = [m.sbuf(f"ctxn{k}", [P, SEQS, 2, P]) for k in range(2)]
        ctxT = m.sbuf("ctxT", [P, 2, PAIRS, TILE], F16)
        attn = m.sbuf("attn", [P, TILE])
        asq = m.sbuf("asq", [P, TILE])
        diag = m.sbuf("diag", [P, TILE])
        an = m.sbuf("an", [P, TILE])
        rest = m.sbuf("rest", [P, TILE])

        (pa, pb), sc, pt, cx = m.banks("proj", 2), m.banks("score", 2), m.banks("probT", 2), m.banks("ctx", 2)

        S = m.count
        const_in, stage_hi, w_ready = S("const_in"), S("stage_hi"), S("w_ready")
        stage_in = [S(f"stage_in{n}") for n in range(6)]
        ready, table_done = S("ready"), S("table_done")
        tab, act_tab = S("tab"), S("act_tab")
        x_loaded = S("x_loaded", 16)
        sq_done, ss_done, std_done, rr_done, x2_done = S("sq_done"), S("ss_done"), S("std_done"), S("rr_done"), S("x2_done")
        x2_ps, x2T_done, res_done, xT_hi, xT_lo = S("x2_ps"), S("x2T_done"), S("res_done"), S("xT_hi"), S("xT_lo")
        v_ps, v_out = S("v_ps", 2 * TB), S("v_out", 2 * TB)
        a_ps, a_rope = S("a_ps", 2 * PAIRS), S("a_rope", 2 * PAIRS)
        b_ps, b_rope = S("b_ps", 2 * PAIRS), S("b_rope", 2 * PAIRS)
        rot_done, qk_hi, qk_lo = S("rot_done", 2 * PAIRS), S("qk_hi", 2 * PAIRS), S("qk_lo", 2 * PAIRS)
        sc_ps, max_done, nmax_done, exp_done = S("sc_ps", UNITS), S("max_done", UNITS), S("nmax_done", UNITS), S("exp_done", UNITS)
        pt_ps = S("pt_ps", UNITS)
        pt_even, pt_odd = S("pt_even", UNITS // 2), S("pt_odd", UNITS // 2)
        pv_done, rden_done, norm_done = S("pv_done", UNITS), S("rden_done", UNITS // 2), S("norm_done", UNITS // 2)
        ct_ps, ct_hi, ct_lo = S("ct_ps", PAIRS), S("ct_hi", PAIRS), S("ct_lo", PAIRS)
        o_ps, attn_done, asq_done = S("o_ps"), S("attn_done"), S("asq_done")
        asum_ps, diag_done = S("asum_ps"), S("diag_done")
        bc_ps, an_done, rest_done, stored = S("bc_ps"), S("an_done"), S("rest_done"), S("stored", 32, 32)

        block = ctx.enter_context(nc.Block())
        consts = [(eye32, eye), (future_m, future), (gam1, gamma1.rearrange("(p a) -> p a", a=1)),
                  (gam2, gamma2.rearrange("(p a) -> p a", a=1)), (ob, o_b.rearrange("(p a) -> p a", a=1)),
                  (vb, v_b), (qkb, qk_b), (th, theta), (sign, half_sign),
                  (pos, position.to_broadcast([P, SEQ]))]
        qk_src, qk_dst = (a.rearrange(r, k=4, j=PAIRS) for a, r in ((qk_w, "p (k j n) -> p k j n"), (qkw[:], "p a (k j n) -> p a k j n")))
        parts = [(qk_src[:, :, j:j + 2], qk_dst[:, :, :, j:j + 2]) for j in range(0, PAIRS, 2)]
        parts.insert(1, (v_w.rearrange("p (k j n) -> p k j n", k=4, j=2), vw[:].rearrange("p a (k j n) -> p a k j n", k=4, j=2)))
        parts.append((o_w.rearrange("(k j p) n -> p k j n", p=P, k=4), ow[:].rearrange("p a (k j n) -> p a k j n", k=4, j=2)))
        split_at = {(-1, 29): 2, (0, 3): 3, (0, 11): 4, (0, 19): 5}
        needed_at = {(-1, 24): 2, (0, 0): 3, (0, 8): 4, (0, 16): 5}

        def staged(n):
            return stage[:, n * 1024:(n + 1) * 1024].rearrange("p (k j n) -> p k j n", k=4, j=2)

        @block.sync
        def _(sp):
            for dst, src in consts:
                sp.dma_start(dst[:], src).then_inc(const_in.handle, 16)
            sp.sem_inc(stored.handle, 32)

            def load(k):
                sp.dma_start(xn[:], xn_v[k]).then_inc(x_loaded.handle, 16)

            def store(k):
                sp.wait_ge(rest_done.handle, rest_done.at(k, 1))
                sp.dma_start(an_out[:, bass.ts(k, TILE)], an[:]).then_inc(stored.handle, 16)
                sp.dma_start(rest_out[:, bass.ts(k, TILE)], rest[:]).then_inc(stored.handle, 16)

            load(0)
            for n, (src, _) in enumerate(parts):
                for k in range(4):
                    sp.dma_start(staged(n)[:, k], src[:, k]).then_inc(stage_in[n].handle, 16)
            sp.wait_ge(x2_done.handle, x2_done.at(0, 1))
            load(1)
            with sp.Fori(1, LAST) as i:
                sp.wait_ge(x2_done.handle, x2_done.at(i, 1))
                load(i + 1)
                store(i - 1)
            store(LAST - 1)
            store(LAST)
            sp.wait_ge(stored.handle, 32 * (turns + 1))

        def turn_by_turn(eng, body):
            body(-1, now=False, ahead=True, behind=False)
            body(0, now=True, ahead=True, behind=False)
            with eng.Fori(1, LAST) as i:
                body(i, now=True, ahead=True, behind=True)
            body(LAST, now=True, ahead=False, behind=True)
            body(turns, now=False, ahead=False, behind=True)

        def made(n, now, ahead, behind, per):
            return behind if n < 0 else now if n < per else ahead

        def projection(u):
            return 2 * (u // 4 + 2) + u % 4 // 2

        def values_before(u):
            return V_SLOTS[u % UNITS] + (2 * TB if u > UNITS // 2 else 0)

        def head(w, j, s, hh, t0, t1):
            buf, a = qk[w][j % RING], s * SEQ
            return buf[hh * HD:(hh + 1) * HD, 0, a + t0:a + t1], buf[hh * HD:(hh + 1) * HD, 1, a + t0:a + t1]

        @block.tensor
        def _(te):
            pe = nc.tensor
            te.wait_ge(ready.handle, 5)
            xs = (xT[:, 0, :], xT[:, 1, :])

            def body(i, now, ahead, behind):

                def project(u):
                    n = projection(u)
                    if now or n > NP:
                        te.wait_ge(b_rope.handle, b_rope.at(i, n))
                    if u % 4 == 2 and made(u // 4 - 2, now, ahead, behind, PAIRS):
                        te.wait_ge(ct_lo.handle, ct_lo.at(i, u // 4 - 1))
                    if u == CLOSE_O + 1 and behind:
                        te.wait_ge(attn_done.handle, attn_done.at(i, 0))
                    if u == ROOTS and behind:
                        te.wait_ge(std_done.handle, std_done.at(i + 1, 1))
                    if u == TURN_X + 1 and ahead:
                        te.wait_ge(x2T_done.handle, x2T_done.at(i + 1, 1))
                    if u == TURN_X + 1 and behind:
                        te.wait_ge(an_done.handle, an_done.at(i, 0))
                    if (u - 1) % UNITS in V_SLOTS and (now or u > UNITS // 2):
                        te.wait_ge(v_out.handle, v_out.at(i, values_before(u - 1) + 1))
                    if n == NP:
                        te.wait_ge(xT_lo.handle, xT_lo.at(i + 1, 1))
                    w, j = n % 2, n // 2 % PAIRS
                    for kind, bank, done in ((2 * w, pa, a_ps), (2 * w + 1, pb, b_ps)):
                        at = kind * 1024 + j * P
                        split_product(pe, bank[:], (qkw[:, 0, at:at + P], qkw[:, 1, at:at + P]), xs).then_inc(done.handle, 1)

                def values(u):
                    half, t = V_SLOTS[u] // TB, V_SLOTS[u] % TB
                    te.wait_ge(b_rope.handle, b_rope.at(i, projection(u - 1) + 1))
                    split_product(pe, pb[:], (xT[:, 0, t * P:(t + 1) * P], xT[:, 1, t * P:(t + 1) * P]),
                                  (vw[:, 0, half * 512:(half + 1) * 512], vw[:, 1, half * 512:(half + 1) * 512]))\
                        .then_inc(v_ps.handle, 1)

                def scores(u):
                    j, s, hh = u // 4, u // 2 % 2, u % 2
                    bank = sc[u % 2]
                    if u % 4 == 0:
                        te.wait_ge(qk_lo.handle, qk_lo.at(i, 2 * j + 2))
                    if behind or u >= 2:
                        te.wait_ge(exp_done.handle, exp_done.at(i, u - 1))
                    split_product(pe, bank[:, 0:128], head(0, j, s, hh, 0, 128), head(1, j, s, hh, 0, 128), stop=False)
                    pe.matmul(bank[:, 0:128], eyeb[:], futureb[:], start=False, stop=True, skip_group_check=True)
                    split_product(pe, bank[:, 128:384], head(0, j, s, hh, 128, 256), head(1, j, s, hh, 0, 256), stop=False)
                    pe.matmul(bank[:, 256:384], eyeb[:], futureb[:], start=False, stop=True, skip_group_check=True)\
                        .then_inc(sc_ps.handle, 1)

                def turn_over(v):
                    te.wait_ge(exp_done.handle, exp_done.at(i, v + 1))
                    if behind or v >= 2:
                        read = (pt_even, pt_odd)[v % 2]
                        te.wait_ge(read.handle, read.at(i, v // 2))
                    for k in range(3):
                        last = pe.transpose(pt[v % 2][:, k * P:(k + 1) * P], prob[v % RING][:, k * P:(k + 1) * P], eye32[:])
                    last.then_inc(pt_ps.handle, 1)

                def mix(v):
                    v_abs = v % UNITS
                    j, s, hh = v_abs // 4, v_abs // 2 % 2, v_abs % 2
                    h = 2 * j + hh
                    read = (pt_even, pt_odd)[v % 2]
                    te.wait_ge(read.handle, read.at(i, v // 2 + 1))
                    if v in (0, UNITS // 2):
                        te.wait_ge(v_out.handle, v_out.at(i, TB if v == 0 else 2 * TB))
                    if hh == 0 and (behind or v >= 4):
                        te.wait_ge(norm_done.handle, norm_done.at(i, 2 * (v // 4) + s - 1))
                    W = HD + 1
                    o0, o1 = (cx[s][:, (2 * hh + b) * W:(2 * hh + b + 1) * W] for b in range(2))
                    pT = probT[v % RING]
                    pe.matmul(o0, pT[:, 0:128], V[:, 2 * s, h, :], start=True, stop=True, skip_group_check=True)
                    pe.matmul(o1, pT[:, 128:256], V[:, 2 * s, h, :], start=True, stop=False, skip_group_check=True)
                    pe.matmul(o1, pT[:, 256:384], V[:, 2 * s + 1, h, :], start=False, stop=True,
                              skip_group_check=True).then_inc(pv_done.handle, 1)

                def turn_ctx(u, j):
                    te.wait_ge(norm_done.handle, norm_done.at(i, 2 * j + 2))
                    if made(projection(u - 1), now, ahead, behind, NP):
                        te.wait_ge(a_rope.handle, a_rope.at(i, projection(u - 1) + 1))
                    else:
                        te.wait_ge(ct_lo.handle, ct_lo.at(i, j))
                    for s in range(SEQS):
                        for b in range(2):
                            at = (2 * s + b) * P
                            last = pe.transpose(pa[:, at:at + P], ctxn[j % 2][:, s, b, :], eye32[:])
                    last.then_inc(ct_ps.handle, 1)

                for u in range(UNITS):
                    if not behind and (i, u) in needed_at:
                        te.wait_ge(w_ready.handle, needed_at[i, u])
                    if now:
                        scores(u)
                    if made(u - 2, now, ahead, behind, UNITS):
                        turn_over(u - 2)
                    if made(u - 4, now, ahead, behind, UNITS):
                        mix(u - 4)
                    if u % 2 == 0 and made(projection(u), now, ahead, behind, NP) and (now or u >= TURN_X):
                        project(u)
                    if u % 4 == 1 and made(u // 4 - 2, now, ahead, behind, PAIRS):
                        turn_ctx(u, u // 4 - 2)
                    if u in V_SLOTS and (ahead if V_SLOTS[u] < TB else now):
                        values(u)
                    if u in (CLOSE_O, CLOSE_SUM, TURN_X) and now:
                        te.wait_ge(b_rope.handle, b_rope.at(i, projection(u - 1) + 1))
                    if u == CLOSE_O and behind:
                        te.wait_ge(w_ready.handle, len(parts))
                        te.wait_ge(ct_lo.handle, ct_lo.at(i, 0))
                        for j in range(PAIRS):
                            last = split_product(pe, pa[:], (ow[:, 0, j * P:(j + 1) * P], ow[:, 1, j * P:(j + 1) * P]),
                                                 (ctxT[:, 0, j, :], ctxT[:, 1, j, :]), start=(j == 0), stop=(j == PAIRS - 1))
                        last.then_inc(o_ps.handle, 1)
                    if u == CLOSE_SUM and behind:
                        te.wait_ge(asq_done.handle, asq_done.at(i, 0))
                        for t in range(TB):
                            last = pe.matmul(pa[:, t:t + 1], asq[:, t * P:(t + 1) * P], ones[:, 0:1], start=True, stop=True)
                        last.then_inc(asum_ps.handle, 1)
                    if u == TURN_X and ahead:
                        te.wait_ge(x2_done.handle, x2_done.at(i + 1, 1))
                        for t in range(TB):
                            last = pe.transpose(pa[:, t * P:(t + 1) * P], x2[:, t, :], eye32[:])
                        last.then_inc(x2_ps.handle, 1)
                    if u == TURN_X and behind:
                        te.wait_ge(diag_done.handle, diag_done.at(i, 0))
                        pe.matmul(pb[:], ones[:], diag[:], start=True, stop=True).then_inc(bc_ps.handle, 1)

            turn_by_turn(te, body)

        @block.scalar
        def _(ac):
            act = nc.scalar.activation
            ac.wait_ge(const_in.handle, 16 * len(consts))
            act(eyeb[:], eye32[:], ACT.Copy).then_inc(ready.handle, 1)
            act(futureb[:], future_m[:], ACT.Copy).then_inc(ready.handle, 1)

            def weights_high(n):
                ac.wait_ge(stage_in[n].handle, 4 * 16)
                act(parts[n][1][:, 0], staged(n), ACT.Copy).then_inc(stage_hi.handle, 1)

            weights_high(0)
            ac.wait_ge(tab.handle, 10)
            act(ang[2][:], ang[2][:], ACT.Sin).then_inc(act_tab.handle, 1)
            act(ang[3][:], ang[3][:], ACT.Sin).then_inc(act_tab.handle, 1)
            weights_high(1)
            ac.wait_ge(ready.handle, 5)

            def body(i, now, ahead, behind):

                def rope_high(n):
                    j = n // 2
                    ac.wait_ge(rot_done.handle, rot_done.at(i, n + 1))
                    if (now and j >= RING) or behind:
                        ac.wait_ge(sc_ps.handle, sc_ps.at(i, 4 * (j - RING + 1)))
                    act(qk[n % 2][j % RING][:, 0, :], rot[n % 2][:], ACT.Copy).then_inc(qk_hi.handle, 1)

                def values_out(u):
                    half, t = V_SLOTS[u % UNITS] // TB, V_SLOTS[u % UNITS] % TB
                    n = values_before(u)
                    ac.wait_ge(v_ps.handle, v_ps.at(i, n + 1))
                    if n == 2 * TB and now:
                        ac.wait_ge(pv_done.handle, pv_done.at(i, UNITS // 2))
                    if n == TB and behind:
                        ac.wait_ge(pv_done.handle, pv_done.at(i, 0))
                    act(V[:, t, half * 8:(half + 1) * 8, 0:HD], pb[:].rearrange("p (h d) -> p h d", d=HD), ACT.Copy)\
                        .then_inc(v_out.handle, 1)

                for u in range(UNITS):
                    j = u // 4
                    if not behind and (i, u) in split_at:
                        weights_high(split_at[i, u])
                    if u % 2 == 1 and made(u - 3, now, ahead, behind, UNITS):
                        ac.wait_ge(pt_ps.handle, pt_ps.at(i, u - 2))
                        if behind or u - 3 >= RING:
                            ac.wait_ge(pv_done.handle, pv_done.at(i, u - 2 - RING))
                        act(probT[(u - 3) % RING][:], pt[0][:, 0:384], ACT.Copy).then_inc(pt_even.handle, 1)
                    if u % 4 == 3 and made(2 * j + 4, now, ahead, behind, NP) and (now or u > TURN_X):
                        rope_high(2 * j + 4)
                    if u % 4 == 1 and made(2 * j + 3, now, ahead, behind, NP) and (now or u > 25):
                        rope_high(2 * j + 3)
                    if u == TURN_X + 1 and ahead:
                        ac.wait_ge(x2_ps.handle, x2_ps.at(i + 1, 1))
                        if now:
                            ac.wait_ge(res_done.handle, res_done.at(i, 1))
                        act(x2T[:], pa[:], ACT.Copy, scale=gam1[:]).then_inc(x2T_done.handle, 1)
                    if (u - 1) % UNITS in V_SLOTS and (now if u <= UNITS // 2 else ahead):
                        values_out(u - 1)
                    if u % 4 == 2 and made(j - 2, now, ahead, behind, PAIRS):
                        ac.wait_ge(ct_ps.handle, ct_ps.at(i, j - 1))
                        if j == 2 and behind:
                            ac.wait_ge(o_ps.handle, o_ps.at(i, 0))
                        act(ctxT[:, 0, (j - 2) % PAIRS, :], pa[:], ACT.Identity, bias=vb[:, (j - 2) % PAIRS:(j - 2) % PAIRS + 1])\
                            .then_inc(ct_hi.handle, 1)
                    if u == X_SPLIT and ahead:
                        ac.wait_ge(x2T_done.handle, x2T_done.at(i + 1, 1))
                        if now:
                            ac.wait_ge(b_ps.handle, b_ps.at(i, NP))
                        act(xT[:, 0, :], x2T[:], ACT.Copy).then_inc(xT_hi.handle, 1)
                    if now:
                        v = u % RING
                        ac.wait_ge(nmax_done.handle, nmax_done.at(i, u + 1))
                        if behind or u >= RING:
                            ac.wait_ge(pt_ps.handle, pt_ps.at(i, u - RING + 1))
                        act(prob[v][:, 0:128], sc[u % 2][:, 0:128], ACT.Exp, bias=nmax[v][:, 0:1])
                        act(prob[v][:, 128:384], sc[u % 2][:, 128:384], ACT.Exp, bias=nmax[v][:, 1:2])\
                            .then_inc(exp_done.handle, 1)
                    if u == CLOSE_SQUARE and behind:
                        ac.wait_ge(attn_done.handle, attn_done.at(i, 0))
                        act(asq[:], attn[:], ACT.Square).then_inc(asq_done.handle, 1)
                    if u == CLOSE_SQUARE and ahead:
                        ac.wait_ge(x_loaded.handle, x_loaded.at(i + 1, 16))
                        act(sq[:], xn[:].rearrange("p t d -> p (t d)"), ACT.Square).then_inc(sq_done.handle, 1)
                    if u == ROOTS:
                        if ahead:
                            ac.wait_ge(ss_done.handle, ss_done.at(i + 1, 1))
                            last = act(std[:, 0:TB], ss[:], ACT.Sqrt, bias=eps[:], scale=1.0 / P)
                        if behind:
                            ac.wait_ge(asum_ps.handle, asum_ps.at(i, 0))
                            last = act(std[:, TB:], pa[:, 0:TB], ACT.Sqrt, bias=eps[:], scale=1.0 / P)
                        last.then_inc(std_done.handle, 1)

            turn_by_turn(ac, body)

        @block.vector
        def _(ve):
            vec = nc.vector
            vec.memset(eps[:], EPS).then_inc(ready.handle, 1)
            vec.memset(ones[:], 1.0).then_inc(ready.handle, 1)
            vec.memset(V[:, :, :, HD:HD + 1], 1.0).then_inc(ready.handle, 1)

            def weights_low(n):
                ve.wait_ge(stage_hi.handle, n + 1)
                vec.tensor_tensor(parts[n][1][:, 1], staged(n), parts[n][1][:, 0], ALU.subtract).then_inc(w_ready.handle, 1)

            ve.wait_ge(const_in.handle, 16 * len(consts))

            def step(ins):
                step.n += 1
                ins.then_inc(tab.handle, 1)
                ve.wait_ge(tab.handle, step.n)

            step.n = 0
            turns_of, red, sine, cosine = ang
            step(vec.tensor_scalar(red[:], pos[:], th[:], None, ALU.mult))
            step(vec.tensor_scalar(turns_of[:], red[:], 1.0 / TWO_PI, None, ALU.mult))
            step(vec.tensor_scalar(turns_of[:], turns_of[:], ROUND, None, ALU.add))
            step(vec.tensor_scalar(turns_of[:], turns_of[:], -ROUND, None, ALU.add))
            for part in (C1, C2, C3):
                step(vec.scalar_tensor_tensor(out=red[:], in0=turns_of[:], scalar=-part, in1=red[:], op0=ALU.mult, op1=ALU.add))
            step(vec.tensor_scalar(sine[:], red[:], 3.1415925, -3.1415925, ALU.min, ALU.max))
            step(vec.scalar_tensor_tensor(out=cosine[:], in0=sine[:], scalar=-1.0, in1=sine[:], op0=ALU.mult, op1=ALU.max))
            step(vec.tensor_scalar(cosine[:], cosine[:], -1.0, TWO_PI / 4, ALU.mult, ALU.add))
            weights_low(0)
            ve.wait_ge(act_tab.handle, 2)
            scale = 1.0 / HD ** 0.5
            vec.tensor_scalar(table[:, 1, 0, :], cosine[:], 1.0, None, ALU.mult).then_inc(table_done.handle, 1)
            vec.tensor_scalar(table[:, 0, 0, :], cosine[:], scale, None, ALU.mult).then_inc(table_done.handle, 1)
            vec.tensor_scalar(table[:, 1, 1, :], sine[:], sign[:], None, ALU.mult).then_inc(table_done.handle, 1)
            vec.tensor_scalar(table[:, 0, 1, :], sine[:], sign[:], scale, ALU.mult, ALU.mult).then_inc(table_done.handle, 1)
            ve.wait_ge(table_done.handle, 4)
            weights_low(1)

            def body(i, now, ahead, behind):

                def rope(n):
                    w, j = n % 2, n // 2 % PAIRS
                    for kind, bank, out, got, done in ((0, pa, rope1, a_ps, a_rope), (1, pb, rope2, b_ps, b_rope)):
                        ve.wait_ge(got.handle, got.at(i, n + 1))
                        if kind == 0 and (now or n >= NP + 2):
                            ve.wait_ge(rot_done.handle, rot_done.at(i, n - 1))
                        vec.scalar_tensor_tensor(out=out[w][:].rearrange("p (s n) -> p s n", s=SEQS),
                                                 in0=bank[:].rearrange("p (s n) -> p s n", s=SEQS),
                                                 scalar=qkb[:, 2 * w + kind, j:j + 1], in1=over(table[:, w, kind, :], SEQS),
                                                 op0=ALU.add, op1=ALU.mult).then_inc(done.handle, 1)

                def normalise(k):
                    j, s = k // 2, k % 2
                    ve.wait_ge(pv_done.handle, pv_done.at(i, 2 * k + 2))
                    got = cx[s][:, 0:4 * (HD + 1)].rearrange("p (h b d) -> p h b d", h=2, b=2)
                    vec.reciprocal(rden[:, s, :].rearrange("p (h b a) -> p h b a", h=2, a=1), got[:, :, :, HD:HD + 1])\
                       .then_inc(rden_done.handle, 1)
                    ve.wait_ge(rden_done.handle, rden_done.at(i, k + 1))
                    if s == 0 and (behind or j >= 2):
                        ve.wait_ge(ct_ps.handle, ct_ps.at(i, j - 1))
                    vec.tensor_tensor(ctxn[j % 2][:, s, :, :].rearrange("p b (h d) -> p h b d", h=2), got[:, :, :, 0:HD],
                                      over(rden[:, s, :].rearrange("p (h b) -> p h b", h=2), HD, 3), ALU.mult)\
                       .then_inc(norm_done.handle, 1)

                for u in range(UNITS):
                    j = u // 4
                    if not behind and (i, u) in split_at:
                        weights_low(split_at[i, u])
                    if u == CLOSE_O + 1 and behind:
                        ve.wait_ge(o_ps.handle, o_ps.at(i, 0))
                        vec.tensor_tensor(attn[:], pa[:], res[:], ALU.add).then_inc(attn_done.handle, 1)
                    if u == TURN_X + 1 and behind:
                        ve.wait_ge(bc_ps.handle, bc_ps.at(i, 0))
                        ve.wait_ge(stored.handle, stored.at(i - 1, 0))
                        vec.scalar_tensor_tensor(out=an[:], in0=attn[:], scalar=gam2[:], in1=pb[:], op0=ALU.mult, op1=ALU.mult)\
                           .then_inc(an_done.handle, 1)
                    if u % 2 == 1 and made(projection(u - 1), now, ahead, behind, NP) and (now or u > TURN_X):
                        rope(projection(u - 1))
                    if u % 2 == 0 and made(u - 3, now, ahead, behind, UNITS):
                        ve.wait_ge(pt_ps.handle, pt_ps.at(i, u - 2))
                        if behind or u - 3 >= RING:
                            ve.wait_ge(pv_done.handle, pv_done.at(i, u - 2 - RING))
                        vec.tensor_copy(probT[(u - 3) % RING][:], pt[1][:, 0:384]).then_inc(pt_odd.handle, 1)
                    if now:
                        v = u % RING
                        ve.wait_ge(sc_ps.handle, sc_ps.at(i, u + 1))
                        if behind or u >= RING:
                            ve.wait_ge(exp_done.handle, exp_done.at(i, u - RING + 1))
                        vec.tensor_reduce(nmax[v][:], sc[u % 2][:, 0:384].rearrange("p (k n) -> p k n", k=3), AX, ALU.max,
                                          negate=True).then_inc(max_done.handle, 1)
                        ve.wait_ge(max_done.handle, max_done.at(i, u + 1))
                        vec.tensor_tensor(nmax[v][:, 1:2], nmax[v][:, 1:2], nmax[v][:, 2:3], ALU.min)\
                           .then_inc(nmax_done.handle, 1)
                    if u % 4 == 2 and made(j - 2, now, ahead, behind, PAIRS):
                        p = (j - 2) % PAIRS
                        ve.wait_ge(ct_hi.handle, ct_hi.at(i, j - 1))
                        vec.scalar_tensor_tensor(out=ctxT[:, 1, p, :], in0=pa[:], scalar=vb[:, p:p + 1], in1=ctxT[:, 0, p, :],
                                                 op0=ALU.add, op1=ALU.subtract).then_inc(ct_lo.handle, 1)
                    if u % 2 == 0 and made(u - 6, now, ahead, behind, UNITS):
                        normalise((u - 6) // 2)
                    if u == CLOSE_SQUARE and now:
                        ve.wait_ge(x2T_done.handle, x2T_done.at(i, 1))
                        if behind:
                            ve.wait_ge(attn_done.handle, attn_done.at(i, 0))
                        vec.tensor_scalar(res[:], x2T[:], ob[:], None, ALU.add).then_inc(res_done.handle, 1)
                    if u == CLOSE_SQUARE + 1 and ahead:
                        ve.wait_ge(sq_done.handle, sq_done.at(i + 1, 1))
                        vec.tensor_reduce(ss[:], sq[:].rearrange("p (t d) -> p t d", t=TB), AX, ALU.add)\
                           .then_inc(ss_done.handle, 1)
                    if u == RECIPROCALS:
                        ve.wait_ge(std_done.handle, std_done.at(i + 1, 1))
                        cut = slice(0 if ahead else TB, 2 * TB if behind else TB)
                        vec.reciprocal(rr[:, cut], std[:, cut]).then_inc(rr_done.handle, 1)

            turn_by_turn(ve, body)

        @block.gpsimd
        def _(po):
            pool = nc.gpsimd

            def body(i, now, ahead, behind):

                def low(n):
                    w, j = n % 2, n // 2
                    po.wait_ge(qk_hi.handle, qk_hi.at(i, n + 1))
                    pool.tensor_tensor(qk[w][j % RING][:, 1, :], rot[w][:], qk[w][j % RING][:, 0, :], ALU.subtract)\
                        .then_inc(qk_lo.handle, 1)

                for u in range(UNITS):
                    j = u // 4
                    if u % 4 == 3 and made(2 * j + 4, now, ahead, behind, NP) and (now or u > TURN_X):
                        low(2 * j + 4)
                    if u % 4 == 1 and made(2 * j + 3, now, ahead, behind, NP) and (now or u > 25):
                        low(2 * j + 3)
                    if u % 2 == 1 and made(projection(u - 1), now, ahead, behind, NP) and (now or u > TURN_X):
                        n = projection(u - 1)
                        po.wait_ge(b_rope.handle, b_rope.at(i, n + 1))
                        if now or n >= NP + 2:
                            po.wait_ge(qk_lo.handle, qk_lo.at(i, n - 1))
                        pool.tensor_tensor(rot[n % 2][:], rope1[n % 2][:], rope2[n % 2][:], ALU.add).then_inc(rot_done.handle, 1)
                    if u == SCALES:
                        po.wait_ge(rr_done.handle, rr_done.at(i + 1, 1))
                    if u == SCALES and ahead:
                        if now:
                            po.wait_ge(x2_ps.handle, x2_ps.at(i, 1))
                        pool.tensor_tensor(x2[:], xn[:], over(rr[:, 0:TB], P, 2), ALU.mult).then_inc(x2_done.handle, 1)
                    if u == SCALES and behind:
                        pool.tensor_tensor(diag[:].rearrange("p (t n) -> p t n", t=TB), over(eye32[:], TB), over(rr[:, TB:], P, 2),
                                           ALU.mult).then_inc(diag_done.handle, 1)
                    if u == TURN_X + 2 and behind:
                        po.wait_ge(an_done.handle, an_done.at(i, 0))
                        pool.tensor_tensor(rest[:], an[:], attn[:], ALU.add).then_inc(rest_done.handle, 1)
                    if u == X_SPLIT and ahead:
                        po.wait_ge(xT_hi.handle, xT_hi.at(i + 1, 1))
                        pool.tensor_tensor(xT[:, 1, :], x2T[:], xT[:, 0, :], ALU.subtract).then_inc(xT_lo.handle, 1)

            turn_by_turn(po, body)


def experts_phase(nc, an_in, rest_in, s_in, x_in, router_w, router_b, w1, b1, w2, b2, number, eye,
                  x1_out, turns):
    E, ER, TOP = 32, 31, 3
    LAG = 4
    HB, TBUF = 3, 5
    HEAD = 11
    SLOTS = E + LAG
    PART = 8
    s_v = s_in.rearrange("(n t p) d -> n p t d", t=TB, p=P)
    x_v = x_in.rearrange("(n t p) d -> n p t d", t=TB, p=P)
    x1_v = x1_out.rearrange("(n t p) d -> n p t d", t=TB, p=P)

    with ExitStack() as ctx:
        m = Memory(nc, ctx, "moe")
        eye32, eye16 = m.sbuf("eye32", [P, P]), m.sbuf("eye16", [P, P], F16)
        stage = m.sbuf("w_stage", [P, 2, E * P])
        w1_s, w2_s = m.sbuf("w1", [P, 2, E * P], F16), m.sbuf("w2", [P, 2, E * P], F16)
        small = m.sbuf("small", [P, P + ER])
        small16 = m.sbuf("small16", [P, 2, P + ER], F16)
        b1_s = m.sbuf("b1", [P, E])
        rb = m.sbuf("rb", [P, ER])
        num = m.sbuf("num", [P, ER])

        an_f = m.sbuf("an_f", [P, TILE])
        an_next, an = m.sbuf("an_next", [P, 2, TILE], F16), m.sbuf("an", [P, 2, TILE], F16)
        lg, ex, pr = m.sbuf("lg", [P, TB, ER]), m.sbuf("ex", [P, TB, ER]), m.sbuf("pr", [P, TB, ER])
        mx, sm = m.sbuf("mx", [P, TB]), m.sbuf("sm", [P, TB])
        top, top_i, top_f = m.sbuf("top", [P, TB, 8]), m.sbuf("top_i", [P, TB, 8], mybir.dt.uint32), m.sbuf("top_f", [P, TB, 8])
        gates_cur = m.sbuf("gates_cur", [P, TB, ER])
        hit, chosen = m.sbuf("hit", [P, TB, TOP, ER]), m.sbuf("chosen", [P, TB, ER])
        gates = m.sbuf("gates", [P, TB, ER])
        gate16 = m.sbuf("gate16", [P, TB, 64], F16)
        gates_next, gatesT = m.sbuf("gates_next", [64, TILE], F16), m.sbuf("gatesT", [64, TILE], F16)
        h32 = [m.sbuf(f"h32_{k}", [P, TILE]) for k in range(4)]
        h16 = [m.sbuf(f"h16_{k}", [P, 2, TILE], F16) for k in range(TBUF)]
        total = m.sbuf("total", [P, TB, P])
        rest, s_s, x_s = m.sbuf("rest", [P, TILE]), m.sbuf("s_s", [P, TB, P]), m.sbuf("x_s", [P, TB, P])
        y, sl, ys = (m.sbuf(n, [P, TB, P]) for n in ("y", "sl", "ys"))
        x1 = m.sbuf("x1", [P, TB, P])

        H, O, (Y,), (m0,) = m.banks("h", HB), m.banks("o", 3), m.banks("y", 1), m.banks("misc", 1)

        S = m.count
        const_in, stage_hi, w_ready, ready = S("const_in"), S("stage_hi"), S("w_ready"), S("ready")
        stage_in = [S(f"stage_in{n}") for n in range(2 * E // PART)]
        an_loaded, an_hi, an_lo = S("an_loaded", 16), S("an_hi"), S("an_lo", 1, 1)
        lg_ps, lg_done, ex_done = S("lg_ps"), S("lg_done"), S("ex_done")
        CHAIN = 13
        chain = S("chain", CHAIN)
        gate_split, gT_ps, gT_copied = S("gate_split"), S("gT_ps"), S("gT_copied")
        an_moved, gates_moved = S("an_moved"), S("gates_moved")
        h_ps, gelu_done, h_hi, h_lo = (S(n, E) for n in ("h_ps", "gelu_done", "h_hi", "h_lo"))
        o_ps, added = S("o_ps", E), S("added", E - 1)
        rest_loaded, s_loaded, x_loaded = S("rest_loaded", 16), S("s_loaded", 16), S("x_loaded", 16)
        y_done, sl_done, ys_done = S("y_done", 1, 1), S("sl_done"), S("ys_done", 1, 1)
        x1_done, x1_stored = S("x1_done", 1, 1), S("x1_stored", 16, 16)
        order = S("order")

        block = ctx.enter_context(nc.Block())
        consts = [(eye32, eye), (small[0:64, 0:P], b2), (small[:, P:], router_w), (b1_s, b1),
                  (rb, router_b.rearrange("(a e) -> a e", a=1).to_broadcast([P, ER])), (num, number.to_broadcast([P, ER]))]
        parts = [(n % 2, n // 2 * PART) for n in range(2 * E // PART)]
        w_s = (w1_s, w2_s)
        LAST = turns - 1

        @block.sync
        def _(sp):
            for dst, src in consts:
                sp.dma_start(dst[:], src).then_inc(const_in.handle, 16)
            sp.sem_inc(an_lo.handle, 1)
            sp.sem_inc(y_done.handle, 1)
            sp.sem_inc(ys_done.handle, 1)
            sp.sem_inc(x1_done.handle, 1)
            sp.sem_inc(x1_stored.handle, 16)

            def load_an(k):
                sp.wait_ge(an_lo.handle, an_lo.before(k))
                sp.dma_start(an_f[:], an_in[:, bass.ts(k, TILE)]).then_inc(an_loaded.handle, 16)

            def load_rest(k):
                sp.wait_ge(y_done.handle, y_done.before(k))
                sp.dma_start(rest[:], rest_in[:, bass.ts(k, TILE)]).then_inc(rest_loaded.handle, 16)

            def load_end(k):
                sp.wait_ge(ys_done.handle, ys_done.before(k))
                sp.dma_start(s_s[:], s_v[k]).then_inc(s_loaded.handle, 16)
                sp.wait_ge(x1_done.handle, x1_done.before(k))
                sp.dma_start(x_s[:], x_v[k]).then_inc(x_loaded.handle, 16)

            def store(k):
                sp.wait_ge(x1_done.handle, x1_done.at(k, 1))
                sp.dma_start(x1_v[k], x1[:]).then_inc(x1_stored.handle, 16)

            load_an(0)
            for n, (which, e) in enumerate(parts):
                sp.dma_start(stage[:, which, e * P:(e + PART) * P].rearrange("p (e h) -> p e h", e=PART),
                             (w1, w2)[which][e:e + PART].rearrange("e p h -> p e h")).then_inc(stage_in[n].handle, 16)
            load_rest(0)
            load_end(0)
            load_an(1)
            load_rest(1)
            with sp.Fori(1, LAST) as i:
                load_an(i + 1)
                load_rest(i + 1)
                store(i - 1)
                load_end(i)
            store(LAST - 1)
            load_end(LAST)
            store(LAST)
            sp.wait_ge(x1_stored.handle, 16 * (turns + 1))

        @block.tensor
        def _(te):
            pe = nc.tensor
            te.wait_ge(ready.handle, 5)

            def logits(k):
                te.wait_ge(an_lo.handle, an_lo.at(k, 1))
                te.wait_ge(an_hi.handle, an_hi.at(k, 1))
                for t in range(TB):
                    last = split_product(pe, m0[:, t * 32:t * 32 + ER],
                                         (an_next[:, 0, t * P:(t + 1) * P], an_next[:, 1, t * P:(t + 1) * P]),
                                         (small16[:, 0, P:], small16[:, 1, P:]))
                last.then_inc(lg_ps.handle, 1)

            def turn_gates(k):
                te.wait_ge(gate_split.handle, gate_split.at(k, 1))
                te.sem_inc(order.handle, 1)
                for t in range(TB):
                    last = pe.transpose(m0[0:64, :].bitcast(F16)[:, t * P:(t + 1) * P], gate16[:, t, :], eye16[:])
                last.then_inc(gT_ps.handle, 1)

            def base(i, t):
                at = slice(t * P, (t + 1) * P)
                pe.matmul(Y[:, at], gatesT[:, at], small16[0:64, 1, 0:P], start=True, stop=False, skip_group_check=True)
                pe.matmul(Y[:, at], gatesT[:, at], small16[0:64, 0, 0:P], start=False, stop=False, skip_group_check=True)
                pe.matmul(Y[:, at], rest[:, at], eye32[:], start=False, stop=False, skip_group_check=True)

            def body(i, ahead, behind):
                te.wait_ge(an_moved.handle, an_moved.at(i, 1))
                for e in range(SLOTS):
                    if not behind and e < E and e % PART == 0:
                        te.wait_ge(w_ready.handle, 2 * (e // PART) + 2)
                    if e < E:
                        if e >= HB:
                            te.wait_ge(gelu_done.handle, gelu_done.at(i, e - HB + 1))
                        split_product(pe, H[e % HB][:], (w1_s[:, 0, e * P:(e + 1) * P], w1_s[:, 1, e * P:(e + 1) * P]),
                                      (an[:, 0, :], an[:, 1, :])).then_inc(h_ps.handle, 1)
                    if e >= LAG:
                        k = e - LAG
                        shared = k == E - 1
                        te.wait_ge(h_hi.handle, h_hi.at(i, k + 1))
                        te.wait_ge(h_lo.handle, h_lo.at(i, k + 1))
                        if not shared and (behind or k >= 3):
                            te.wait_ge(added.handle, added.at(i, k - 2 if k >= 3 else 0))
                        if shared:
                            te.wait_ge(y_done.handle, y_done.before(i))
                            te.wait_ge(rest_loaded.handle, rest_loaded.at(i, 16))
                            te.wait_ge(gates_moved.handle, gates_moved.at(i, 1))
                        for t in range(TB):
                            at = slice(t * P, (t + 1) * P)
                            if shared:
                                base(i, t)
                            last = split_product(pe, (Y if shared else O[k % 3])[:, at],
                                                 (h16[k % TBUF][:, 0, at], h16[k % TBUF][:, 1, at]),
                                                 (w2_s[:, 0, k * P:(k + 1) * P], w2_s[:, 1, k * P:(k + 1) * P]), start=not shared)
                        last.then_inc(o_ps.handle, 1)
                    if ahead and e == HEAD:
                        logits(i + 1)
                    if ahead and e == HEAD + 15:
                        turn_gates(i + 1)

            logits(0)
            turn_gates(0)
            body(0, True, False)
            with te.Fori(1, LAST) as i:
                body(i, True, True)
            body(LAST, False, True)

        @block.scalar
        def _(ac):
            act = nc.scalar.activation
            ac.wait_ge(const_in.handle, 16 * len(consts))
            act(eye16[:], eye32[:], ACT.Copy).then_inc(ready.handle, 1)
            act(small16[:, 0, P:], small[:, P:], ACT.Copy)
            act(small16[0:64, 0, 0:P], small[0:64, 0:P], ACT.Copy).then_inc(ready.handle, 1)

            def weights_high(n):
                which, e = parts[n]
                cut = slice(e * P, (e + PART) * P)
                ac.wait_ge(stage_in[n].handle, 16)
                act(w_s[which][:, 0, cut], stage[:, which, cut], ACT.Copy).then_inc(stage_hi.handle, 1)

            def high(k):
                ac.wait_ge(an_loaded.handle, an_loaded.at(k, 16))
                act(an_next[:, 0, :], an_f[:], ACT.Copy).then_inc(an_hi.handle, 1)

            def exps(k):
                ac.wait_ge(lg_done.handle, lg_done.at(k, 1))
                act(ex[:], lg[:], ACT.Exp).then_inc(ex_done.handle, 1)

            def copy_gates(k):
                ac.wait_ge(gT_ps.handle, gT_ps.at(k, 1))
                act(gates_next[:], m0[0:64, :].bitcast(F16)[:, 0:TILE], ACT.Copy).then_inc(gT_copied.handle, 1)

            def gate_y(k):
                ac.wait_ge(y_done.handle, y_done.at(k, 1))
                act(sl[:], y[:], ACT.Silu).then_inc(sl_done.handle, 1)

            def body(i, ahead, behind):

                def high_half(k):
                    ac.wait_ge(gelu_done.handle, gelu_done.at(i, k + 1))
                    if k >= TBUF:
                        ac.wait_ge(o_ps.handle, o_ps.at(i, k - TBUF + 1))
                    act(h16[k % TBUF][:, 0, :], h32[k % 4][:], ACT.Copy).then_inc(h_hi.handle, 1)

                for e in range(E):
                    if not behind and e % 4 == 1 and e // 4 + 2 < len(parts):
                        weights_high(e // 4 + 2)
                    if behind and e == 0:
                        gate_y(i - 1)
                    if e:
                        high_half(e - 1)
                    ac.wait_ge(h_ps.handle, h_ps.at(i, e + 1))
                    if e >= 4:
                        ac.wait_ge(h_lo.handle, h_lo.at(i, e - 3))
                    act(h32[e % 4][:], H[e % HB][:], ACT.Gelu, bias=b1_s[:, e:e + 1]).then_inc(gelu_done.handle, 1)
                    if ahead and e == HEAD - 4:
                        ac.wait_ge(an_moved.handle, an_moved.at(i, 1))
                        high(i + 1)
                    if ahead and e == HEAD + 3:
                        exps(i + 1)
                    if ahead and e == HEAD + 15:
                        copy_gates(i + 1)
                high_half(E - 1)

            high(0)
            exps(0)
            weights_high(0)
            weights_high(1)
            copy_gates(0)
            body(0, True, False)
            with ac.Fori(1, LAST) as i:
                body(i, True, True)
            body(LAST, False, True)
            gate_y(LAST)

        @block.vector
        def _(ve):
            vec = nc.vector
            ve.wait_ge(const_in.handle, 16 * len(consts))
            vec.memset(gate16[:, :, ER:ER + 1], 1.0).then_inc(ready.handle, 1)
            vec.memset(gate16[:, :, 63:64], 0.0).then_inc(ready.handle, 1)
            ve.wait_ge(ready.handle, 4)
            vec.tensor_tensor(small16[:, 1, P:], small[:, P:], small16[:, 0, P:], ALU.subtract)
            vec.tensor_tensor(small16[0:64, 1, 0:P], small[0:64, 0:P], small16[0:64, 0, 0:P], ALU.subtract)\
               .then_inc(ready.handle, 1)

            def weights_low(n):
                which, e = parts[n]
                cut = slice(e * P, (e + PART) * P)
                ve.wait_ge(stage_hi.handle, n + 1)
                vec.tensor_tensor(w_s[which][:, 1, cut], stage[:, which, cut], w_s[which][:, 0, cut], ALU.subtract)\
                   .then_inc(w_ready.handle, 1)

            def router(k):
                steps = [0]

                def step(ins):
                    steps[0] += 1
                    ins.then_inc(chain.handle, 1)
                    ve.wait_ge(chain.handle, chain.at(k, steps[0]))

                ve.wait_ge(lg_ps.handle, lg_ps.at(k, 1))
                step(vec.tensor_tensor(lg[:], m0[:, 0:TB * 32].rearrange("p (t e) -> p t e", t=TB)[:, :, 0:ER],
                                       over(rb[:], TB), ALU.add))
                step(vec.tensor_reduce(mx[:], lg[:], AX, ALU.max))
                vec.tensor_tensor(lg[:], lg[:], over(mx[:], ER, 2), ALU.subtract).then_inc(lg_done.handle, 1)
                yield
                ve.wait_ge(ex_done.handle, ex_done.at(k, 1))
                step(vec.tensor_reduce(sm[:], ex[:], AX, ALU.add))
                step(vec.reciprocal(sm[:], sm[:]))
                step(vec.tensor_tensor(pr[:], ex[:], over(sm[:], ER, 2), ALU.mult))
                yield
                ve.sem_inc(order.handle, 1)
                for t in range(TB):
                    last = vec.max(top[:, t, :], pr[:, t, :])
                step(last)
                ve.sem_inc(order.handle, 1)
                yield
                for t in range(TB):
                    last = vec.max_index(top_i[:, t, :], top[:, t, :], pr[:, t, :])
                step(last)
                yield
                step(vec.tensor_copy(top_f[:], top_i[:]))
                step(vec.tensor_tensor(hit[:], over(over(num[:], TOP), TB), over(top_f[:, :, 0:TOP], ER, 3), ALU.is_equal))
                yield
                step(vec.tensor_reduce(chosen[:], hit[:].rearrange("p t k e -> p t e k"), AX, ALU.add))
                step(vec.tensor_tensor(gates[:], pr[:], chosen[:], ALU.mult))
                yield
                step(vec.tensor_copy(gate16[:, :, 0:ER], gates[:]))
                step(vec.tensor_tensor(chosen[:], gates[:], gate16[:, :, 0:ER], ALU.subtract))
                vec.tensor_copy(gate16[:, :, 32:32 + ER], chosen[:]).then_inc(gate_split.handle, 1)
                assert steps[0] == CHAIN
                yield

            def move_an(k):
                ve.wait_ge(an_lo.handle, an_lo.at(k, 1))
                ve.wait_ge(an_hi.handle, an_hi.at(k, 1))
                vec.tensor_copy(an[:], an_next[:]).then_inc(an_moved.handle, 1)

            def move_gates(k):
                ve.wait_ge(gT_copied.handle, gT_copied.at(k, 1))
                vec.tensor_copy(gates_cur[:], gates[:])
                vec.tensor_copy(gatesT[:], gates_next[:]).then_inc(gates_moved.handle, 1)

            def add_x(k):
                ve.wait_ge(ys_done.handle, ys_done.at(k, 1))
                ve.wait_ge(x_loaded.handle, x_loaded.at(k, 16))
                ve.wait_ge(x1_stored.handle, x1_stored.before(k))
                vec.tensor_tensor(x1[:], ys[:], x_s[:], ALU.add).then_inc(x1_done.handle, 1)

            def body(i, ahead, behind):
                part = router(i + 1) if ahead else iter(())
                for e in range(E + 1):
                    if not behind and e % 4 == 1 and e // 4 + 2 < len(parts):
                        weights_low(e // 4 + 2)
                    if e >= LAG and e < E:
                        add(i, e - LAG, behind)
                    if behind and e == 5:
                        add_x(i - 1)
                    if e >= HEAD + 2:
                        next(part, None)
                if ahead:
                    ve.wait_ge(h_ps.handle, h_ps.at(i, E))
                    move_an(i + 1)
                for k in range(E - LAG, E - 1):
                    add(i, k, behind)
                for _ in part:
                    pass
                ve.wait_ge(o_ps.handle, o_ps.at(i, E))
                ve.wait_ge(added.handle, added.at(i, E - 1))
                vec.tensor_tensor(y[:].rearrange("p t d -> p (t d)"), Y[:], total[:].rearrange("p t d -> p (t d)"), ALU.add)\
                   .then_inc(y_done.handle, 1)
                if ahead:
                    move_gates(i + 1)

            def add(i, k, behind):
                ve.wait_ge(o_ps.handle, o_ps.at(i, k + 1))
                if k == 0:
                    ve.wait_ge(gates_moved.handle, gates_moved.at(i, 1))
                if k or behind:
                    ve.wait_ge(added.handle, added.at(i, k))
                for t in range(TB):
                    out, gate = O[k % 3][:, t * P:(t + 1) * P], gates_cur[:, t, k:k + 1]
                    if k:
                        last = vec.scalar_tensor_tensor(out=total[:, t, :], in0=out, scalar=gate, in1=total[:, t, :],
                                                        op0=ALU.mult, op1=ALU.add)
                    else:
                        last = vec.tensor_scalar(total[:, t, :], out, gate, None, ALU.mult)
                last.then_inc(added.handle, 1)

            for _ in router(0):
                pass
            weights_low(0)
            weights_low(1)
            move_an(0)
            move_gates(0)
            body(0, True, False)
            with ve.Fori(1, LAST) as i:
                body(i, True, True)
            body(LAST, False, True)
            add_x(LAST)

        @block.gpsimd
        def _(po):
            pool = nc.gpsimd

            def low(k):
                po.wait_ge(an_hi.handle, an_hi.at(k, 1))
                pool.tensor_tensor(an_next[:, 1, :], an_f[:], an_next[:, 0, :], ALU.subtract).then_inc(an_lo.handle, 1)

            def scale_s(k):
                po.wait_ge(sl_done.handle, sl_done.at(k, 1))
                po.wait_ge(s_loaded.handle, s_loaded.at(k, 16))
                pool.tensor_tensor(ys[:], sl[:], s_s[:], ALU.mult).then_inc(ys_done.handle, 1)

            def body(i, ahead, behind):
                for e in range(E):
                    if behind and e == 4:
                        scale_s(i - 1)
                    po.wait_ge(h_hi.handle, h_hi.at(i, e + 1))
                    pool.tensor_tensor(h16[e % TBUF][:, 1, :], h32[e % 4][:], h16[e % TBUF][:, 0, :], ALU.subtract)\
                        .then_inc(h_lo.handle, 1)
                    if ahead and e == HEAD - 4:
                        low(i + 1)

            low(0)
            body(0, True, False)
            with po.Fori(1, LAST) as i:
                body(i, True, True)
            body(LAST, False, True)
            scale_s(LAST)


def second_layer_phase(nc, x_in, wqkvo, bo, gate_w, wg, wu, wd, spread, number, block_mask, head_mask, eye,
                       s_tmp, out, turns):
    HEADS, HD, ER, TOP = 16, 8, 8, 2
    HT = wg.shape[1] // P
    LAG, TBUF = 3, 4
    SLOTS = HT + LAG
    PART = 8
    x_v = x_in.rearrange("(n t p) d -> n p t d", t=TB, p=P)
    out_v = out.rearrange("(n t p) d -> n p t d", t=TB, p=P)
    KX = P + HEADS

    with ExitStack() as ctx:
        m = Memory(nc, ctx, "second")
        eye32, eye16 = m.sbuf("eye32", [P, P]), m.sbuf("eye16", [P, P], F16)
        eps = m.sbuf("eps", [P, 1])
        stage = m.sbuf("w_stage", [P, 3, HT * P])
        wg_s, wu_s, wd_s = (m.sbuf(n, [P, 2, HT * P], F16) for n in ("wg", "wu", "wd"))
        small, small16 = m.sbuf("small", [P, 4 * P + ER]), m.sbuf("small16", [P, 2, 4 * P + ER], F16)
        bo_s = m.sbuf("bo", [P, 1])
        num = m.sbuf("num", [P, ER])
        spread_s = m.sbuf("spread", [64, HT * P], F16)
        bmask, hmask = m.sbuf("bmask", [P, P]), m.sbuf("hmask", [P, HEADS])

        def w(a, b):
            return small16[:, 0, a:b], small16[:, 1, a:b]

        x_s = m.sbuf("x_s", [P, TB, P])
        stats, mean_var = m.sbuf("stats", [P, TB, 6]), m.sbuf("mean_var", [P, TB, 2])
        std, rstd = m.sbuf("std", [P, TB]), m.sbuf("rstd", [P, TB])
        xn = m.sbuf("xn", [P, TB, P])
        x_next, x_cur = m.sbuf("x_next", [P, 2, TILE], F16), m.sbuf("x_cur", [P, 2, TILE], F16)
        arg, ex = m.sbuf("arg", [P, 2 * TILE + TB * TOP]), m.sbuf("ex", [P, 2 * TILE + TB * TOP])
        pos_part = m.sbuf("pos_part", [P, 2 * TILE])
        feat = m.sbuf("feat", [P, 2 * TILE])
        v1 = m.sbuf("v1", [P, TB, P + 1])
        kvx = m.sbuf("kvx", [P, SEQS, KX])
        den = m.sbuf("den", [P, TB, HEADS])
        rden = m.sbuf("rden", [P, TB, HEADS])
        mixed = m.sbuf("mixed", [P, TB, P])
        mT = m.sbuf("mT", [P, 2, TILE], F16)
        s_next, s_cur = m.sbuf("s_next", [P, TILE]), m.sbuf("s_cur", [P, TILE])
        lg = m.sbuf("lg", [P, TB, ER])
        top, top_i, top_f = m.sbuf("top", [P, TB, 8]), m.sbuf("top_i", [P, TB, 8], mybir.dt.uint32), m.sbuf("top_f", [P, TB, 8])
        wsum = m.sbuf("wsum", [P, TB])
        share = m.sbuf("share", [P, TB, TOP])
        hit = m.sbuf("hit", [P, TB, TOP, ER])
        gates = m.sbuf("gates", [P, TB, ER])
        gate16 = m.sbuf("gate16", [P, TB, 64], F16)
        gates_next, gatesT = m.sbuf("gates_next", [64, TILE], F16), m.sbuf("gatesT", [64, TILE], F16)
        s32 = [m.sbuf(f"s32_{k}", [P, TILE]) for k in range(2)]
        a32 = [m.sbuf(f"a32_{k}", [P, TILE]) for k in range(2)]
        t32 = [m.sbuf(f"t32_{k}", [P, TILE]) for k in range(3)]
        t16 = [m.sbuf(f"t16_{k}", [P, 2, TILE], F16) for k in range(TBUF)]
        x_r, y = m.sbuf("x_r", [P, TB, P]), m.sbuf("y", [P, TB, P])
        sl, ys = m.sbuf("sl", [P, TILE]), m.sbuf("ys", [P, TILE])

        G, U, (C,), (Y,), (m0, m1) = m.banks("g", 2), m.banks("u", 2), m.banks("c", 1), m.banks("y", 1), m.banks("misc", 2)

        S = m.count
        const_in, stage_hi, w_ready, ready = S("const_in"), S("stage_hi"), S("w_ready"), S("ready")
        stage_in = [S(f"stage_in{n}") for n in range(3 * HT // PART)]
        x_loaded, stats_done, aggr_done, std_done, rstd_done = S("x_loaded", 16), S("stats_done"), S("aggr_done"), S("std_done"), S("rstd_done")
        xn_done, xT_ps, xT_hi, xT_lo = S("xn_done", 1, 1), S("xT_ps"), S("xT_hi"), S("xT_lo")
        lg_ps, q_ps, q_min, q_max = S("lg_ps"), S("q_ps"), S("q_min"), S("q_max")
        kv_ps, k_min, kv_out = S("kv_ps", 2), S("k_min", 2), S("kv_out", 2)
        arg_done, ex_done, feat_done = S("arg_done"), S("ex_done"), S("feat_done")
        sum_ps, kvx_done, mix_ps = S("sum_ps", SEQS), S("kvx_done", SEQS), S("mix_ps", 2)
        den_done, rden_done, mix_done = S("den_done", 2), S("rden_done"), S("mix_done", 2)
        mT_ps, mT_hi, mT_lo, s_ps, s_done = S("mT_ps"), S("mT_hi"), S("mT_lo"), S("s_ps"), S("s_done")
        s_stored = S("s_stored", 16, 16)
        CHAIN = 11
        chain = S("chain", CHAIN)
        gate_split, gT_ps, gT_copied, moved = S("gate_split"), S("gT_ps"), S("gT_copied"), S("moved")
        g_ps, u_ps, c_ps = S("g_ps", HT), S("u_ps", HT), S("c_ps", HT)
        silu_done, a_done, t_done, t_hi, t_lo, y_step = (S(n, HT) for n in ("silu_done", "a_done", "t_done", "t_hi", "t_lo", "y_step"))
        s_loaded, xr_loaded = S("s_loaded", 16), S("xr_loaded", 16)
        sl_done, ys_done, yT_ps, y_done, y_stored = S("sl_done", 1, 1), S("ys_done", 1, 1), S("yT_ps"), S("y_done", 1, 1), S("y_stored", 16, 16)
        order = S("order")

        block = ctx.enter_context(nc.Block())
        consts = [(eye32, eye), (small[:, 0:4 * P], wqkvo), (small[:, 4 * P:], gate_w),
                  (bo_s, bo.rearrange("(p a) -> p a", a=1)), (num, number[:, 0:ER].to_broadcast([P, ER])),
                  (spread_s, spread), (bmask, block_mask), (hmask, head_mask)]
        parts = [(n % 3, n // 3 * PART) for n in range(3 * HT // PART)]
        w_s = (wg_s, wu_s, wd_s)
        more_weights = {n // 3 * PART - 7 + 2 * (n % 3): n for n in range(3, len(parts))}
        LAST = turns - 1

        @block.sync
        def _(sp):
            for dst, src in consts:
                sp.dma_start(dst[:], src).then_inc(const_in.handle, 16)
            sp.sem_inc(xn_done.handle, 1)
            sp.sem_inc(sl_done.handle, 1)
            sp.sem_inc(ys_done.handle, 1)
            sp.sem_inc(y_done.handle, 1)
            sp.sem_inc(s_stored.handle, 16)
            sp.sem_inc(y_stored.handle, 16)

            def load_x(k):
                sp.wait_ge(xn_done.handle, xn_done.before(k))
                sp.dma_start(x_s[:], x_v[k]).then_inc(x_loaded.handle, 16)

            def load_end(k):
                sp.wait_ge(s_stored.handle, s_stored.at(k, 16))
                sp.wait_ge(ys_done.handle, ys_done.before(k))
                sp.dma_start(s_cur[:], s_tmp[:, bass.ts(k, TILE)]).then_inc(s_loaded.handle, 16)
                sp.wait_ge(y_done.handle, y_done.before(k))
                sp.dma_start(x_r[:], x_v[k]).then_inc(xr_loaded.handle, 16)

            def store_s(k):
                sp.wait_ge(s_done.handle, s_done.at(k, 1))
                sp.dma_start(s_tmp[:, bass.ts(k, TILE)], s_next[:]).then_inc(s_stored.handle, 16)

            def store(k):
                sp.wait_ge(y_done.handle, y_done.at(k, 1))
                sp.dma_start(out_v[k], y[:]).then_inc(y_stored.handle, 16)

            load_x(0)
            for n, (which, j) in enumerate(parts):
                cut, into = slice(j * P, (j + PART) * P), stage[:, which, j * P:(j + PART) * P]
                if which < 2:
                    sp.dma_start(into, (wg, wu)[which][:, cut]).then_inc(stage_in[n].handle, 16)
                else:
                    sp.dma_start(into.rearrange("p (j n) -> p j n", n=P), wd.rearrange("(j p) n -> p j n", p=P)[:, j:j + PART])\
                        .then_inc(stage_in[n].handle, 16)
            store_s(0)
            load_x(1)
            load_end(0)
            store_s(1)
            with sp.Fori(1, LAST) as i:
                load_x(i + 1)
                store(i - 1)
                load_end(i)
                store_s(i + 1)
            store(LAST - 1)
            load_end(LAST)
            store(LAST)
            sp.wait_ge(y_stored.handle, 16 * (turns + 1))
            sp.wait_ge(s_stored.handle, 16 * (turns + 1))

        @block.tensor
        def _(te):
            pe = nc.tensor
            te.wait_ge(ready.handle, 6)

            def tok(pair, t):
                return pair[:, 0, t * P:(t + 1) * P], pair[:, 1, t * P:(t + 1) * P]

            def turn_x(k):
                te.wait_ge(xn_done.handle, xn_done.at(k, 1))
                for t in range(TB):
                    last = pe.transpose(m0[:, t * P:(t + 1) * P], xn[:, t, :], eye32[:])
                last.then_inc(xT_ps.handle, 1)

            def queries(k):
                te.wait_ge(xT_lo.handle, xT_lo.at(k, 1))
                for t in range(TB):
                    last = split_product(pe, m1[:, t * ER:(t + 1) * ER], tok(x_next, t), w(4 * P, 4 * P + ER))
                last.then_inc(lg_ps.handle, 1)
                split_product(pe, m0[:], w(0, P), (x_next[:, 0, :], x_next[:, 1, :])).then_inc(q_ps.handle, 1)

            def keys_values(k):
                te.wait_ge(q_min.handle, q_min.at(k, 1))
                te.wait_ge(q_max.handle, q_max.at(k, 1))
                te.wait_ge(chain.handle, chain.at(k, 1))
                for s, bank in enumerate((m0, m1)):
                    for b in range(2):
                        last = split_product(pe, bank[:, b * 2 * P:(b + 1) * 2 * P], tok(x_next, 2 * s + b), w(P, 3 * P))
                    last.then_inc(kv_ps.handle, 1)

            def sums(k):
                te.wait_ge(feat_done.handle, feat_done.at(k, 1))
                te.wait_ge(kv_out.handle, kv_out.at(k, 2))
                te.wait_ge(k_min.handle, k_min.at(k, 2))
                for s, bank in enumerate((m0, m1)):
                    for b in range(2):
                        t = 2 * s + b
                        last = pe.matmul(bank[:, 0:P + 1], feat[:, TILE + t * P:TILE + (t + 1) * P], v1[:, t, :],
                                         start=(b == 0), stop=(b == 1), skip_group_check=True)
                    last.then_inc(sum_ps.handle, 1)

            def mix(k):
                for s, bank in enumerate((m0, m1)):
                    te.wait_ge(kvx_done.handle, kvx_done.at(k, s + 1))
                    for b in range(2):
                        t = 2 * s + b
                        last = pe.matmul(bank[:, b * KX:(b + 1) * KX], feat[:, t * P:(t + 1) * P], kvx[:, s, :],
                                         start=True, stop=True, skip_group_check=True)
                    last.then_inc(mix_ps.handle, 1)

            def turn_mixed(k):
                te.wait_ge(mix_done.handle, mix_done.at(k, 2))
                for t in range(TB):
                    last = pe.transpose(m0[:, t * P:(t + 1) * P], mixed[:, t, :], eye32[:])
                last.then_inc(mT_ps.handle, 1)

            def project(k):
                te.wait_ge(mT_lo.handle, mT_lo.at(k, 1))
                split_product(pe, m1[:], w(3 * P, 4 * P), (mT[:, 0, :], mT[:, 1, :])).then_inc(s_ps.handle, 1)

            def turn_gates(k):
                te.wait_ge(gate_split.handle, gate_split.at(k, 1))
                te.sem_inc(order.handle, 1)
                for t in range(TB):
                    last = pe.transpose(m0[0:64, :].bitcast(F16)[:, t * P:(t + 1) * P], gate16[:, t, :], eye16[:])
                last.then_inc(gT_ps.handle, 1)

            def turn_y(k, newest):
                te.wait_ge(ys_done.handle, ys_done.at(k, 1))
                te.wait_ge(s_done.handle, s_done.at(newest, 1))
                for t in range(TB):
                    last = pe.transpose(m1[:, t * P:(t + 1) * P], ys[:, t * P:(t + 1) * P], eye32[:])
                last.then_inc(yT_ps.handle, 1)

            ahead_of = {3: turn_x, 6: queries, 8: keys_values, 14: sums, 15: mix, 18: turn_mixed, 20: project, 21: turn_gates}

            def body(i, ahead, behind):
                te.wait_ge(moved.handle, moved.at(i, 1))
                for j in range(SLOTS):
                    if not behind and j < HT and j % PART == 0:
                        te.wait_ge(w_ready.handle, 3 * (j // PART) + 3)
                    if j < HT:
                        at = slice(j * P, (j + 1) * P)
                        xs = (x_cur[:, 0, :], x_cur[:, 1, :])
                        if j >= 2:
                            te.wait_ge(silu_done.handle, silu_done.at(i, j - 1))
                        split_product(pe, G[j % 2][:], (wg_s[:, 0, at], wg_s[:, 1, at]), xs).then_inc(g_ps.handle, 1)
                        if j >= 2:
                            te.wait_ge(a_done.handle, a_done.at(i, j - 1))
                        split_product(pe, U[j % 2][:], (wu_s[:, 0, at], wu_s[:, 1, at]), xs).then_inc(u_ps.handle, 1)
                    if j >= LAG:
                        k = j - LAG
                        at = slice(k * P, (k + 1) * P)
                        if k == 0:
                            te.wait_ge(sl_done.handle, sl_done.before(i))
                        te.wait_ge(t_hi.handle, t_hi.at(i, k + 1))
                        te.wait_ge(t_lo.handle, t_lo.at(i, k + 1))
                        split_product(pe, Y[:], (wd_s[:, 0, at], wd_s[:, 1, at]),
                                      (t16[k % TBUF][:, 0, :], t16[k % TBUF][:, 1, :]), start=(k == 0), stop=(k == HT - 1))\
                            .then_inc(y_step.handle, 1)
                    if j < HT:
                        if j:
                            te.wait_ge(t_done.handle, t_done.at(i, j))
                        pe.matmul(C[:], spread_s[:, j * P:(j + 1) * P], gatesT[:], start=True, stop=True)\
                            .then_inc(c_ps.handle, 1)
                    if behind and j == 2:
                        turn_y(i - 1, i)
                    if ahead and j in ahead_of:
                        ahead_of[j](i + 1)

            for part in ahead_of.values():
                part(0)
            body(0, True, False)
            with te.Fori(1, LAST) as i:
                body(i, True, True)
            body(LAST, False, True)
            turn_y(LAST, LAST)

        @block.scalar
        def _(ac):
            act = nc.scalar.activation
            ac.wait_ge(const_in.handle, 16 * len(consts))
            act(eye16[:], eye32[:], ACT.Copy).then_inc(ready.handle, 1)
            act(small16[:, 0, :], small[:], ACT.Copy).then_inc(ready.handle, 1)

            def weights_high(n):
                which, j = parts[n]
                cut = slice(j * P, (j + PART) * P)
                ac.wait_ge(stage_in[n].handle, 16)
                act(w_s[which][:, 0, cut], stage[:, which, cut], ACT.Copy).then_inc(stage_hi.handle, 1)

            ac.wait_ge(ready.handle, 6)

            def root(k):
                ac.wait_ge(aggr_done.handle, aggr_done.at(k, 1))
                act(std[:], mean_var[:, :, 1], ACT.Sqrt, bias=eps[:]).then_inc(std_done.handle, 1)

            def x_high(k):
                ac.wait_ge(xT_ps.handle, xT_ps.at(k, 1))
                act(x_next[:, 0, :], m0[:], ACT.Copy).then_inc(xT_hi.handle, 1)

            def q_part(k):
                ac.wait_ge(q_ps.handle, q_ps.at(k, 1))
                act(pos_part[:, 0:TILE], m0[:], ACT.Relu).then_inc(q_max.handle, 1)

            def kv_part(k):
                for s, bank in enumerate((m0, m1)):
                    kv = bank[:].rearrange("p (b c n) -> p b c n", b=2, c=2)
                    ac.wait_ge(kv_ps.handle, kv_ps.at(k, s + 1))
                    act(pos_part[:, TILE + s * 256:TILE + (s + 1) * 256].rearrange("p (b n) -> p b n", b=2), kv[:, :, 0, :],
                        ACT.Relu)
                    act(v1[:, 2 * s:2 * s + 2, 0:P], kv[:, :, 1, :], ACT.Copy).then_inc(kv_out.handle, 1)

            def exps(k):
                ac.wait_ge(arg_done.handle, arg_done.at(k, 1))
                ac.wait_ge(k_min.handle, k_min.at(k, 2))
                ac.wait_ge(q_min.handle, q_min.at(k, 1))
                act(ex[:], arg[:], ACT.Exp).then_inc(ex_done.handle, 1)

            def m_high(k):
                ac.wait_ge(mT_ps.handle, mT_ps.at(k, 1))
                act(mT[:, 0, :], m0[:], ACT.Copy).then_inc(mT_hi.handle, 1)

            def s_copy(k):
                ac.wait_ge(s_ps.handle, s_ps.at(k, 1))
                ac.wait_ge(s_stored.handle, s_stored.before(k))
                act(s_next[:], m1[:], ACT.Identity, bias=bo_s[:]).then_inc(s_done.handle, 1)

            def copy_gates(k):
                ac.wait_ge(gT_ps.handle, gT_ps.at(k, 1))
                act(gates_next[:], m0[0:64, :].bitcast(F16)[:, 0:TILE], ACT.Copy).then_inc(gT_copied.handle, 1)

            def gate_y(k):
                ac.wait_ge(y_step.handle, y_step.at(k, HT))
                ac.wait_ge(ys_done.handle, ys_done.before(k))
                act(sl[:], Y[:], ACT.Silu).then_inc(sl_done.handle, 1)

            ahead_of = {1: root, 4: x_high, 7: q_part, 8: kv_part, 12: exps, 19: m_high, 21: s_copy, 22: copy_gates}

            def body(i, ahead, behind):
                for j in range(HT + 1):
                    if not behind and j in more_weights:
                        weights_high(more_weights[j])
                    if behind and j == 0:
                        gate_y(i - 1)
                    if j < HT:
                        ac.wait_ge(g_ps.handle, g_ps.at(i, j + 1))
                        if j >= 2:
                            ac.wait_ge(a_done.handle, a_done.at(i, j - 1))
                        act(s32[j % 2][:], G[j % 2][:], ACT.Silu).then_inc(silu_done.handle, 1)
                    if j:
                        ac.wait_ge(t_done.handle, t_done.at(i, j))
                        if j > TBUF:
                            ac.wait_ge(y_step.handle, y_step.at(i, j - TBUF))
                        act(t16[(j - 1) % TBUF][:, 0, :], t32[(j - 1) % 3][:], ACT.Copy).then_inc(t_hi.handle, 1)
                    if ahead and j in ahead_of:
                        ahead_of[j](i + 1)

            for n, part in enumerate(ahead_of.values()):
                part(0)
                if 2 <= n < 5:
                    weights_high(n - 2)
            body(0, True, False)
            with ac.Fori(1, LAST) as i:
                body(i, True, True)
            body(LAST, False, True)
            gate_y(LAST)

        @block.vector
        def _(ve):
            vec = nc.vector
            ve.wait_ge(const_in.handle, 16 * len(consts))
            vec.memset(gate16[:], 0.0).then_inc(ready.handle, 1)
            ve.wait_ge(ready.handle, 3)
            vec.memset(gate16[:, :, ER:ER + 1], 1.0)
            vec.memset(eps[:], EPS)
            vec.memset(v1[:, :, P:P + 1], 1.0).then_inc(ready.handle, 2)
            vec.tensor_tensor(small16[:, 1, :], small[:], small16[:, 0, :], ALU.subtract).then_inc(ready.handle, 1)

            def weights_low(n):
                which, j = parts[n]
                cut = slice(j * P, (j + PART) * P)
                ve.wait_ge(stage_hi.handle, n + 1)
                vec.tensor_tensor(w_s[which][:, 1, cut], stage[:, which, cut], w_s[which][:, 0, cut], ALU.subtract)\
                   .then_inc(w_ready.handle, 1)

            def norm_stats(k):
                ve.wait_ge(x_loaded.handle, x_loaded.at(k, 16))
                for t in range(TB):
                    last = vec.bn_stats(stats[:, t, :], x_s[:, t, :])
                last.then_inc(stats_done.handle, 1)
                ve.wait_ge(stats_done.handle, stats_done.at(k, 1))
                ve.sem_inc(order.handle, 1)
                for t in range(TB):
                    last = vec.bn_aggr(mean_var[:, t, :], stats[:, t, :])
                last.then_inc(aggr_done.handle, 1)

            def norm(k):
                ve.wait_ge(std_done.handle, std_done.at(k, 1))
                vec.reciprocal(rstd[:], std[:]).then_inc(rstd_done.handle, 1)
                ve.wait_ge(rstd_done.handle, rstd_done.at(k, 1))
                for t in range(TB):
                    last = vec.tensor_scalar(xn[:, t, :], x_s[:, t, :], mean_var[:, t, 0:1], rstd[:, t:t + 1],
                                             ALU.subtract, ALU.mult)
                last.then_inc(xn_done.handle, 1)

            def x_low(k):
                ve.wait_ge(xT_hi.handle, xT_hi.at(k, 1))
                vec.tensor_tensor(x_next[:, 1, :], m0[:], x_next[:, 0, :], ALU.subtract).then_inc(xT_lo.handle, 1)

            steps = [0]

            def step(k, ins):
                steps[0] += 1
                ins.then_inc(chain.handle, 1)
                ve.wait_ge(chain.handle, chain.at(k, steps[0]))

            def q_neg(k):
                steps[0] = 0
                ve.wait_ge(lg_ps.handle, lg_ps.at(k, 1))
                step(k, vec.tensor_copy(lg[:], m1[:, 0:TB * ER].rearrange("p (t e) -> p t e", t=TB)))
                ve.wait_ge(q_max.handle, q_max.at(k, 1))
                vec.tensor_scalar(arg[:, 0:TILE], m0[:], 0.0, None, ALU.min).then_inc(q_min.handle, 1)
                ve.sem_inc(order.handle, 1)
                for t in range(TB):
                    last = vec.max(top[:, t, :], lg[:, t, :])
                step(k, last)
                ve.sem_inc(order.handle, 1)

            def k_neg(k):
                for t in range(TB):
                    last = vec.max_index(top_i[:, t, :], top[:, t, :], lg[:, t, :])
                step(k, last)
                vec.tensor_tensor(arg[:, 2 * TILE:].rearrange("p (t k) -> p t k", t=TB), top[:, :, 0:TOP],
                                  top[:, :, 0:1].to_broadcast([P, TB, TOP]), ALU.subtract).then_inc(arg_done.handle, 1)
                for s, bank in enumerate((m0, m1)):
                    ve.wait_ge(kv_out.handle, kv_out.at(k, s + 1))
                    vec.tensor_scalar(arg[:, TILE + s * 256:TILE + (s + 1) * 256].rearrange("p (b n) -> p b n", b=2),
                                      bank[:].rearrange("p (b c n) -> p b c n", b=2, c=2)[:, :, 0, :], 0.0, None, ALU.min)\
                       .then_inc(k_min.handle, 1)

            def choose(k):
                e3 = ex[:, 2 * TILE:].rearrange("p (t k) -> p t k", t=TB)
                ve.wait_ge(ex_done.handle, ex_done.at(k, 1))
                step(k, vec.tensor_reduce(wsum[:], e3, AX, ALU.add))
                step(k, vec.reciprocal(wsum[:], wsum[:]))
                step(k, vec.tensor_tensor(share[:], e3, over(wsum[:], TOP, 2), ALU.mult))
                step(k, vec.tensor_copy(top_f[:], top_i[:]))
                step(k, vec.tensor_tensor(hit[:], over(over(num[:], TOP), TB), over(top_f[:, :, 0:TOP], ER, 3), ALU.is_equal))

            def choose_more(k):
                step(k, vec.tensor_tensor(hit[:], hit[:], over(share[:], ER, 3), ALU.mult))
                step(k, vec.tensor_reduce(gates[:], hit[:].rearrange("p t k e -> p t e k"), AX, ALU.add))
                step(k, vec.tensor_copy(gate16[:, :, 0:ER], gates[:]))
                assert steps[0] == CHAIN
                vec.tensor_tensor(gate16[:, :, 32:32 + ER], gates[:], gate16[:, :, 0:ER], ALU.subtract)\
                   .then_inc(gate_split.handle, 1)

            def mask_sums(k):
                for s, bank in enumerate((m0, m1)):
                    ve.wait_ge(sum_ps.handle, sum_ps.at(k, s + 1))
                    vec.tensor_tensor(kvx[:, s, 0:P], bank[:, 0:P], bmask[:], ALU.mult)
                    vec.tensor_scalar(kvx[:, s, P:], hmask[:], bank[:, P:P + 1], None, ALU.mult).then_inc(kvx_done.handle, 1)

            def divide(k):
                for s, bank in enumerate((m0, m1)):
                    ve.wait_ge(mix_ps.handle, mix_ps.at(k, s + 1))
                    got = bank[:, 0:2 * KX].rearrange("p (b n) -> p b n", b=2)
                    vec.tensor_scalar(den[:, 2 * s:2 * s + 2, :], got[:, :, P:], 1e-6, None, ALU.add).then_inc(den_done.handle, 1)
                ve.wait_ge(den_done.handle, den_done.at(k, 2))
                vec.reciprocal(rden[:], den[:]).then_inc(rden_done.handle, 1)
                ve.wait_ge(rden_done.handle, rden_done.at(k, 1))
                for s, bank in enumerate((m0, m1)):
                    for b in range(2):
                        t = 2 * s + b
                        last = vec.tensor_tensor(mixed[:, t, :].rearrange("p (h d) -> p h d", d=HD),
                                                 bank[:, b * KX:b * KX + P].rearrange("p (h d) -> p h d", d=HD),
                                                 over(rden[:, t, :], HD, 2), ALU.mult)
                    last.then_inc(mix_done.handle, 1)

            def m_low(k):
                ve.wait_ge(mT_hi.handle, mT_hi.at(k, 1))
                vec.tensor_tensor(mT[:, 1, :], m0[:], mT[:, 0, :], ALU.subtract).then_inc(mT_lo.handle, 1)

            def move(k):
                ve.wait_ge(gT_copied.handle, gT_copied.at(k, 1))
                vec.tensor_copy(x_cur[:], x_next[:])
                vec.tensor_copy(gatesT[:], gates_next[:]).then_inc(moved.handle, 1)

            def add_x(k):
                ve.wait_ge(yT_ps.handle, yT_ps.at(k, 1))
                ve.wait_ge(xr_loaded.handle, xr_loaded.at(k, 16))
                ve.wait_ge(y_stored.handle, y_stored.before(k))
                vec.tensor_tensor(y[:].rearrange("p t d -> p (t d)"), m1[:], x_r[:].rearrange("p t d -> p (t d)"), ALU.add)\
                   .then_inc(y_done.handle, 1)

            ahead_of = {0: norm_stats, 1: norm, 5: x_low, 7: q_neg, 8: k_neg, 12: choose, 14: mask_sums, 16: divide,
                        17: choose_more, 20: m_low}

            def body(i, ahead, behind):
                nxt = i + 1
                for j in range(HT + 1):
                    if not behind and j in more_weights:
                        weights_low(more_weights[j])
                    if j:
                        ve.wait_ge(c_ps.handle, c_ps.at(i, j))
                        ve.wait_ge(a_done.handle, a_done.at(i, j))
                        if j > 3:
                            ve.wait_ge(t_lo.handle, t_lo.at(i, j - 3))
                        vec.tensor_tensor(t32[(j - 1) % 3][:], C[:], a32[(j - 1) % 2][:], ALU.mult).then_inc(t_done.handle, 1)
                    if j < HT:
                        ve.wait_ge(u_ps.handle, u_ps.at(i, j + 1))
                        ve.wait_ge(silu_done.handle, silu_done.at(i, j + 1))
                        vec.tensor_tensor(a32[j % 2][:], U[j % 2][:], s32[j % 2][:], ALU.mult).then_inc(a_done.handle, 1)
                    if behind and j == 4:
                        add_x(i - 1)
                    if ahead and j in ahead_of:
                        ahead_of[j](nxt)
                if ahead:
                    move(nxt)

            for n, part in enumerate(ahead_of.values()):
                part(0)
                if 3 <= n < 6:
                    weights_low(n - 3)
            move(0)
            body(0, True, False)
            with ve.Fori(1, LAST) as i:
                body(i, True, True)
            body(LAST, False, True)
            add_x(LAST)

        @block.gpsimd
        def _(po):
            pool = nc.gpsimd

            def features(k):
                po.wait_ge(ex_done.handle, ex_done.at(k, 1))
                pool.tensor_tensor(feat[:], ex[:, 0:2 * TILE], pos_part[:], ALU.add).then_inc(feat_done.handle, 1)

            def scale_s(k):
                po.wait_ge(sl_done.handle, sl_done.at(k, 1))
                po.wait_ge(s_loaded.handle, s_loaded.at(k, 16))
                pool.tensor_tensor(ys[:], sl[:], s_cur[:], ALU.mult).then_inc(ys_done.handle, 1)

            def body(i, ahead, behind):
                for j in range(HT):
                    if behind and j == 1:
                        scale_s(i - 1)
                    po.wait_ge(t_hi.handle, t_hi.at(i, j + 1))
                    pool.tensor_tensor(t16[j % TBUF][:, 1, :], t32[j % 3][:], t16[j % TBUF][:, 0, :], ALU.subtract)\
                        .then_inc(t_lo.handle, 1)
                    if ahead and j == 11:
                        features(i + 1)

            features(0)
            body(0, True, False)
            with po.Fori(1, LAST) as i:
                body(i, True, True)
            body(LAST, False, True)
            scale_s(LAST)


def recurrent_depth_two_kernel(nc, x, wq, wk, wvgb, wo, norm_w, qk_w, qk_b, v_w, v_b, o_w, o_b, gamma1, gamma2, theta,
                               position, half_sign, router_w, router_b, w1, b1, w2, b2, wqkvo, bo, gate_w, wg, wu, wd,
                               eye, below, upto, future, spread, number, block_mask, head_mask, out):
    tokens = x.shape[0]
    turns = tokens // TILE

    def activation(name, shape):
        return nc.dram_tensor(name, shape, F32, kind="Internal").ap()

    xn, mixer, x1 = (activation(n, (tokens, P)) for n in ("xn", "mixer", "x1"))
    an, rest, mixer2 = (activation(n, (P, tokens)) for n in ("an", "rest", "mixer2"))
    delta_phase(nc, x, wq, wk, wvgb, wo, norm_w, eye, below, upto, xn, mixer)
    attention_phase(nc, xn, qk_w, qk_b, v_w, v_b, o_w, o_b, gamma1, gamma2, theta, position, half_sign, eye, future,
                    an, rest, turns)
    experts_phase(nc, an, rest, mixer, x, router_w, router_b, w1, b1, w2, b2, number, eye, x1, turns)
    second_layer_phase(nc, x1, wqkvo, bo, gate_w, wg, wu, wd, spread, number, block_mask, head_mask, eye, mixer2, out,
                       turns)


def kernel(**inputs):
    import concourse.bacc as bacc
    from concourse.bass_utils import run_bass_kernel_spmd

    L0 = {k[3:]: np.asarray(v) for k, v in inputs.items() if k.startswith("L0_")}
    L1 = {k[3:]: np.asarray(v) for k, v in inputs.items() if k.startswith("L1_")}
    x = L0["attn_x"]
    heads, hd = 16, 64

    even_odd = np.concatenate([np.arange(0, hd, 2), np.arange(1, hd, 2)])
    odd_even = np.concatenate([even_odd[hd // 2:], even_odd[:hd // 2]])

    def columns(w, order):
        return w.reshape(w.shape[:-1] + (heads, hd))[..., order].reshape(w.shape)

    def four(q, k):
        return [columns(q, even_odd), columns(q, odd_even), columns(k, even_odd), columns(k, odd_even)]

    ne = L0["ffn_re_w1"].shape[0]
    b2 = np.zeros((64, P), np.float32)
    b2[:ne], b2[ne], b2[32:32 + ne] = L0["ffn_re_b2"], L0["ffn_sh_b2"], L0["ffn_re_b2"]

    experts, _, inter = L1["ffn_Wg"].shape
    units = experts * inter + L1["ffn_Sg"].shape[1]
    padded = -(-units // P) * P

    def stack(w, shared):
        return np.concatenate([w.transpose(1, 0, 2).reshape(P, -1), shared, np.zeros((P, padded - units), np.float32)], 1)

    owner = np.minimum(np.arange(padded) // inter, experts)
    spread = np.zeros((64, padded), np.float16)
    spread[owner, np.arange(padded)] = 1
    spread[32 + owner[owner < experts], np.arange(padded)[owner < experts]] = 1

    args = {
        "x": x.reshape(-1, P), "wq": L0["attn_Wq"], "wk": L0["attn_Wk"],
        "wvgb": np.concatenate([L0["attn_Wv"], L0["attn_Wg"], L0["attn_Wb"]], 1),
        "wo": L0["attn_Wo"], "norm_w": L0["attn_norm_w"],
        "qk_w": np.concatenate(four(L0["ffn_q_w"], L0["ffn_k_w"]), 1),
        "qk_b": np.stack(four(L0["ffn_q_b"], L0["ffn_k_b"])).reshape(4, 8, P).transpose(2, 0, 1),
        "v_w": L0["ffn_v_w"], "v_b": L0["ffn_v_b"].reshape(8, P).T, "o_w": L0["ffn_o_w"], "o_b": L0["ffn_o_b"],
        "gamma1": L0["ffn_gamma1"], "gamma2": L0["ffn_gamma2"], "theta": np.tile(L0["ffn_theta"], 4)[:, None],
        "position": np.arange(SEQ, dtype=np.float32)[None],
        "half_sign": np.where((np.arange(P) // 32) % 2, 1, -1).astype(np.float32)[:, None],
        "router_w": L0["ffn_router_w"], "router_b": L0["ffn_router_b"],
        "w1": np.concatenate([L0["ffn_re_w1"], L0["ffn_sh_w1"][None]]),
        "b1": np.concatenate([L0["ffn_re_b1"], L0["ffn_sh_b1"][None]]).T,
        "w2": np.concatenate([L0["ffn_re_w2"], L0["ffn_sh_w2"][None]]), "b2": b2,
        "wqkvo": np.concatenate([L1["attn_wq"].T, L1["attn_wk"].T, L1["attn_wv"].T, L1["attn_wo"].T], 1),
        "bo": L1["attn_bo"], "gate_w": L1["ffn_gate_w"],
        "wg": stack(L1["ffn_Wg"], L1["ffn_Sg"]), "wu": stack(L1["ffn_Wu"], L1["ffn_Su"]),
        "wd": np.concatenate([L1["ffn_Wd"].reshape(-1, P), L1["ffn_Sd"], np.zeros((padded - units, P), np.float32)]),
        "eye": np.eye(P, dtype=np.float32), "below": np.tril(np.ones((P, P), np.float32), -1),
        "upto": np.triu(np.ones((P, P), np.float32)), "future": np.triu(np.full((P, P), -1e30, np.float32), 1),
        "spread": spread,
        "number": np.arange(ne, dtype=np.float32)[None],
        "block_mask": np.kron(np.eye(16), np.ones((8, 8))).astype(np.float32),
        "head_mask": np.kron(np.eye(16), np.ones((8, 1))).astype(np.float32),
    }
    nc = bacc.Bacc("TRN2", target_bir_lowering=False, num_devices=1)
    arrays, aps = {}, {}
    for name, a in args.items():
        arrays[f"in_{name}"] = np.ascontiguousarray(a)
        aps[name] = nc.dram_tensor(f"in_{name}", a.shape, mybir.dt.from_np(a.dtype), kind="ExternalInput").ap()
    out = nc.dram_tensor("out", (x.shape[0] * x.shape[1], P), F32, kind="ExternalOutput").ap()
    recurrent_depth_two_kernel(nc, out=out, **aps)
    result = run_bass_kernel_spmd(nc, [arrays], core_ids=[0])
    return result.results[0]["out"].reshape(x.shape)
```
